# Optimizing a Trainium2 kernel written in Bass

```python
import numpy as np
import jax
import jax.numpy as jnp

def _softmax(x, axis=-1):
    return jax.nn.softmax(x, axis=axis)

def _gelu(x):
    return jax.nn.gelu(x, approximate=True)

def _silu(x):
    return jax.nn.silu(x)

def _sigmoid(x):
    return jax.nn.sigmoid(x)

def _layernorm(x, axis=-1, eps=1e-05):
    m = jnp.mean(x, axis=axis, keepdims=True)
    v = jnp.var(x, axis=axis, keepdims=True)
    return (x - m) / jnp.sqrt(v + eps)

def _scatter_add(tgt, idx, src, axis=0):
    return tgt.at[idx].add(src)

def _segment_sum(src, seg, n):
    return jax.ops.segment_sum(src, seg, n)
kernel_name = 'mk_gps_d1_gnn_r8_01281e'

def setup_inputs(seed: int=0):
    np.random.seed(seed)
    _w = jnp.asarray

    def _rec_inputs():
        import jax
        import jax.numpy as jnp
        _gk = jax.random.key(seed)
        x = -8.776e-05 + 1 * jax.random.normal(jax.random.fold_in(_gk, 1), (6250, 256), jnp.float32)
        src = jax.random.randint(jax.random.fold_in(_gk, 2), (200000,), 0, 6250, jnp.int32)
        dst = jax.random.randint(jax.random.fold_in(_gk, 3), (200000,), 0, 6250, jnp.int32)
        _o = jnp.argsort(dst, stable=True)
        src = src[_o]
        dst = dst[_o]
        return (x, src, dst)
    x, src, dst = _rec_inputs()

    def _L0_gnn_setup():
        import math
        import jax, jax.numpy as jnp
        import numpy as np
        N = 2500
        E = 40000
        D_IN = 256
        D_OUT = 256
        H = 8
        DK = D_OUT // H
        key = jax.random.key(seed)
        ks = jax.random.split(key, 16)
        h = jax.random.normal(ks[0], (N, D_IN), dtype=jnp.float32)
        src = jax.random.randint(ks[1], (E,), 0, N, dtype=jnp.int32)
        dst = jax.random.randint(ks[2], (E,), 0, N, dtype=jnp.int32)
        s = 1.0 / math.sqrt(D_IN)
        Wk = jax.random.uniform(ks[3], (D_OUT, D_IN), jnp.float32, -s, s)
        bk = jnp.zeros((D_OUT,), jnp.float32)
        Wq = jax.random.uniform(ks[4], (D_OUT, D_IN), jnp.float32, -s, s)
        bq = jnp.zeros((D_OUT,), jnp.float32)
        Wv = jax.random.uniform(ks[5], (D_OUT, D_IN), jnp.float32, -s, s)
        bv = jnp.zeros((D_OUT,), jnp.float32)
        so = 1.0 / math.sqrt(D_OUT)
        Wa = jax.random.uniform(ks[6], (D_OUT, D_OUT), jnp.float32, -so, so)
        ba = jnp.zeros((D_OUT,), jnp.float32)
        bound = math.sqrt(6.0 / (DK + DK))
        rel_att = jax.random.uniform(ks[7], (H, DK, DK), jnp.float32, -bound, bound)
        rel_msg = jax.random.uniform(ks[8], (H, DK, DK), jnp.float32, -bound, bound)
        rel_pri = jnp.ones((H,), jnp.float32)
        skip = jnp.ones((), jnp.float32)
        return {'h': h, 'src': src, 'dst': dst, 'Wk': Wk, 'bk': bk, 'Wq': Wq, 'bq': bq, 'Wv': Wv, 'bv': bv, 'Wa': Wa, 'ba': ba, 'rel_att': rel_att, 'rel_msg': rel_msg, 'rel_pri': rel_pri, 'skip': skip}
    _L0_gnn_all = _L0_gnn_setup()
    _L0_gnn_in = {k: v for k, v in _L0_gnn_all.items() if k in ('Wk', 'bk', 'Wq', 'bq', 'Wv', 'bv', 'Wa', 'ba', 'rel_att', 'rel_msg', 'rel_pri', 'skip')}
    del _L0_gnn_all

    def _L0_mix_setup():
        import jax, jax.numpy as jnp
        import numpy as np
        EPS = 1e-05

        def _layernorm(x, weight, bias):
            mean = jnp.mean(x, axis=-1, keepdims=True)
            std = jnp.std(x, axis=-1, keepdims=True, ddof=1)
            out = (x - mean) / (std + EPS)
            return weight * out + bias
        key = jax.random.key(seed)
        B, N, C = (4, 4096, 256)
        H, hc = (8, C // 8)
        kx, = jax.random.split(key, 1)
        x = jax.random.normal(kx, (B, N, C), dtype=jnp.float32)
        return {'x': x, 'kln_weight': jnp.ones((H, 1, hc), dtype=jnp.float32), 'kln_bias': jnp.zeros((H, 1, hc), dtype=jnp.float32), 'vln_weight': jnp.ones((H, 1, hc), dtype=jnp.float32), 'vln_bias': jnp.zeros((H, 1, hc), dtype=jnp.float32)}
    _L0_mix_all = _L0_mix_setup()
    _L0_mix_in = {k: v for k, v in _L0_mix_all.items() if k in ('kln_weight', 'kln_bias', 'vln_weight', 'vln_bias')}
    del _L0_mix_all

    def _L0_ffn_setup():
        import jax, jax.numpy as jnp
        import numpy as np
        TOP_K = 2
        key = jax.random.key(seed)
        ks = jax.random.split(key, 4)
        B, L, D, H, E = (8, 512, 256, 1024, 8)
        s = 0.02
        return {'x': jax.random.normal(ks[0], (B, L, D), jnp.float32), 'Wg': jax.random.normal(ks[1], (D, E), jnp.float32) * s, 'bg': jnp.zeros((E,), jnp.float32), 'W1': jax.random.normal(ks[2], (E, D, H), jnp.float32) * s, 'b1': jnp.zeros((E, H), jnp.float32), 'W2': jax.random.normal(ks[3], (E, H, D), jnp.float32) * s, 'b2': jnp.zeros((E, D), jnp.float32)}
    _L0_ffn_all = _L0_ffn_setup()
    _L0_ffn_in = {k: v for k, v in _L0_ffn_all.items() if k in ('Wg', 'bg', 'W1', 'b1', 'W2', 'b2')}
    del _L0_ffn_all
    return {'x': x, 'src': src, 'dst': dst, 'L0_gnn_Wk': _L0_gnn_in['Wk'], 'L0_gnn_bk': _L0_gnn_in['bk'], 'L0_gnn_Wq': _L0_gnn_in['Wq'], 'L0_gnn_bq': _L0_gnn_in['bq'], 'L0_gnn_Wv': _L0_gnn_in['Wv'], 'L0_gnn_bv': _L0_gnn_in['bv'], 'L0_gnn_Wa': _L0_gnn_in['Wa'], 'L0_gnn_ba': _L0_gnn_in['ba'], 'L0_gnn_rel_att': _L0_gnn_in['rel_att'], 'L0_gnn_rel_msg': _L0_gnn_in['rel_msg'], 'L0_gnn_rel_pri': _L0_gnn_in['rel_pri'], 'L0_gnn_skip': _L0_gnn_in['skip'], 'L0_mix_kln_weight': _L0_mix_in['kln_weight'], 'L0_mix_kln_bias': _L0_mix_in['kln_bias'], 'L0_mix_vln_weight': _L0_mix_in['vln_weight'], 'L0_mix_vln_bias': _L0_mix_in['vln_bias'], 'L0_ffn_Wg': _L0_ffn_in['Wg'], 'L0_ffn_bg': _L0_ffn_in['bg'], 'L0_ffn_W1': _L0_ffn_in['W1'], 'L0_ffn_b1': _L0_ffn_in['b1'], 'L0_ffn_W2': _L0_ffn_in['W2'], 'L0_ffn_b2': _L0_ffn_in['b2']}

def reference(x, src, dst, L0_gnn_Wk, L0_gnn_bk, L0_gnn_Wq, L0_gnn_bq, L0_gnn_Wv, L0_gnn_bv, L0_gnn_Wa, L0_gnn_ba, L0_gnn_rel_att, L0_gnn_rel_msg, L0_gnn_rel_pri, L0_gnn_skip, L0_mix_kln_weight, L0_mix_kln_bias, L0_mix_vln_weight, L0_mix_vln_bias, L0_ffn_Wg, L0_ffn_bg, L0_ffn_W1, L0_ffn_b1, L0_ffn_W2, L0_ffn_b2):
    import jax
    import jax.numpy as jnp

    def _L0_gnn_ref(h, src, dst, Wk, bk, Wq, bq, Wv, bv, Wa, ba, rel_att, rel_msg, rel_pri, skip):
        import math
        import jax, jax.numpy as jnp
        import numpy as np
        N = 2500
        E = 40000
        D_IN = 256
        D_OUT = 256
        H = 8
        DK = D_OUT // H
        n = h.shape[0]
        sqrt_dk = math.sqrt(DK)
        k = (h @ Wk.T + bk).reshape(n, H, DK)
        q = (h @ Wq.T + bq).reshape(n, H, DK)
        v = (h @ Wv.T + bv).reshape(n, H, DK)
        k = jnp.einsum('nhd,hde->nhe', k, rel_att)
        v = jnp.einsum('nhd,hde->nhe', v, rel_msg)
        score = jnp.einsum('ehd,ehd->eh', q[dst], k[src]) * rel_pri / sqrt_dk
        m = jax.ops.segment_max(score, dst, num_segments=n)
        ex = jnp.exp(score - m[dst])
        z = jax.ops.segment_sum(ex, dst, num_segments=n)
        attn = ex / z[dst]
        agg = jax.ops.segment_sum(v[src] * attn[:, :, None], dst, num_segments=n)
        t = agg.reshape(n, D_OUT)
        trans = t @ Wa.T + ba
        alpha = jax.nn.sigmoid(skip)
        return trans * alpha + h * (1.0 - alpha)

    def _L0_mix_ref(x, kln_weight, kln_bias, vln_weight, vln_bias):
        import jax, jax.numpy as jnp
        import numpy as np
        EPS = 1e-05

        def _layernorm(x, weight, bias):
            mean = jnp.mean(x, axis=-1, keepdims=True)
            std = jnp.std(x, axis=-1, keepdims=True, ddof=1)
            out = (x - mean) / (std + EPS)
            return weight * out + bias
        B, N, C = x.shape
        H = kln_weight.shape[0]
        hc = C // H
        qkv = x.reshape(B, N, H, hc).transpose(0, 2, 1, 3)
        q = qkv
        k = _layernorm(qkv, kln_weight, kln_bias)
        v = _layernorm(qkv, vln_weight, vln_bias)
        kv = jnp.einsum('bhnd,bhne->bhde', k, v) / N
        out = jnp.einsum('bhnd,bhde->bhne', q, kv)
        out = out.transpose(0, 2, 1, 3).reshape(B, N, C)
        return out + x

    def _L0_ffn_ref(x, Wg, bg, W1, b1, W2, b2):
        import jax, jax.numpy as jnp
        import numpy as np
        TOP_K = 2
        B, L, D = x.shape
        E = W1.shape[0]
        xf = x.reshape(-1, D)
        gate_logits = xf @ Wg + bg
        top_w, top_i = jax.lax.top_k(gate_logits, TOP_K)
        top_w = jax.nn.softmax(top_w, axis=-1)
        w_dense = jnp.sum(jax.nn.one_hot(top_i, E, dtype=xf.dtype) * top_w[..., None], axis=1)
        out = jnp.zeros_like(xf)
        for e in range(E):
            h = jax.nn.gelu(xf @ W1[e] + b1[e], approximate=False)
            out = out + w_dense[:, e:e + 1] * (h @ W2[e] + b2[e])
        return out.reshape(B, L, D)
    xn = _layernorm(x, axis=-1)
    x = x + _L0_gnn_ref(xn, src, dst, L0_gnn_Wk, L0_gnn_bk, L0_gnn_Wq, L0_gnn_bq, L0_gnn_Wv, L0_gnn_bv, L0_gnn_Wa, L0_gnn_ba, L0_gnn_rel_att, L0_gnn_rel_msg, L0_gnn_rel_pri, L0_gnn_skip) + _L0_mix_ref(xn[None], L0_mix_kln_weight, L0_mix_kln_bias, L0_mix_vln_weight, L0_mix_vln_bias)[0]
    x = x + _L0_ffn_ref(_layernorm(x, axis=-1)[None], L0_ffn_Wg, L0_ffn_bg, L0_ffn_W1, L0_ffn_b1, L0_ffn_W2, L0_ffn_b2)[0]
    return x

_drawn_inputs = setup_inputs


def setup_inputs(seed=0):
    import zlib

    import numpy as np

    out = dict(_drawn_inputs(seed))
    spreads = {'L0_gnn_bk': (0.0, 2.0),
     'L0_gnn_bq': (0.0, 0.8),
     'L0_gnn_bv': (0.0, 0.558),
     'L0_gnn_ba': (0.0, 0.329),
     'L0_gnn_rel_pri': (1.0, 0.6),
     'L0_mix_kln_weight': (1.0, 0.6),
     'L0_mix_kln_bias': (0.0, 0.503),
     'L0_mix_vln_weight': (1.0, 0.6),
     'L0_mix_vln_bias': (0.0, 0.502),
     'L0_ffn_bg': (0.0, 0.516),
     'L0_ffn_b1': (0.0, 2.0),
     'L0_ffn_b2': (0.0, 0.365)}
    factors = {'L0_gnn_Wk': 8.0,
     'L0_gnn_Wq': 8.0,
     'L0_gnn_Wv': 3.818,
     'L0_gnn_Wa': 2.79,
     'L0_gnn_rel_att': 8.0,
     'L0_gnn_rel_msg': 2.944,
     'L0_ffn_W1': 5.04}
    for name, (base, spread) in spreads.items():
        noise = np.random.default_rng([zlib.crc32(name.encode()), seed]).standard_normal(out[name].shape)
        drawn = base * np.exp(spread * noise) if base else spread * noise
        out[name] = jnp.asarray(drawn.astype(out[name].dtype))
    for name, factor in factors.items():
        out[name] = (out[name] * factor).astype(out[name].dtype)
    return out
```

```python
from contextlib import ExitStack

import concourse.bass as bass
from concourse import mybir

F32 = mybir.dt.float32
I32 = mybir.dt.int32
U32 = mybir.dt.uint32
ALU = mybir.AluOpType
ACT = mybir.ActivationFunctionType
X = mybir.AxisListType.X

P = 128
N = 6250
E = 200000
D = 256
H = 8
DK = D // H
HALVES = D // P
NT = 50
RT = -(-N // P)
NP = NT * P
SLOTS = 8
GROUPS = 8
FAST = SLOTS * GROUPS
UNROLL = 3
BLOCKS = 13
EROWS = BLOCKS * P
SCHED = 512
SKIP = 65536.0
PASSES = -(-RT * GROUPS // UNROLL)
NEG = -1.0e30
LN_EPS = 1e-5
NE = 8
HID = 1024
HC = HID // P
TOK = 2 * P
PJ = 9
ATT = 30
SPL = 12
FFN = 12


def bcast(ap, dims):
    return ap.to_broadcast(dims)


def build(nc, a, out):
    kvd = nc.dram_tensor("kv_table", (NP, 2 * D), F32, kind="Internal").ap()
    xntd = nc.dram_tensor("xn_transposed", (NT, P, D), F32, kind="Internal").ap()
    aggd = nc.dram_tensor("aggregated", (NT, P, D), F32, kind="Internal").ap()
    rpd = nc.dram_tensor("row_pointers", ((NT + 1) * P, 1), I32, kind="Internal").ap()
    schedd = nc.dram_tensor("schedule", (SCHED, 2), I32, kind="Internal").ap()

    with ExitStack() as root:
        root.enter_context(nc.allow_non_contiguous_dma(reason="columns of a few thousand entries, once"))
        def sb(ctx, name, shape, dt=F32):
            return ctx.enter_context(nc.sbuf_tensor(name, shape, dt))

        def pb(ctx, name, shape, dt=F32):
            return ctx.enter_context(nc.psum_tensor(name, shape, dt))

        def sem(name):
            return root.enter_context(nc.semaphore(name))

        ident = sb(root, "ident", [P, P])
        ones = sb(root, "ones", [P, P])
        a_fold = sb(root, "a_fold", [P, HALVES, D])
        mix_w = sb(root, "mix_w", [P, HALVES, P])
        aba = sb(root, "aba", [P, D])
        small = sb(root, "small", [P, 16])
        alpha = small[:, 0:1]
        two_minus_alpha = small[:, 1:2]
        eps_ln = small[:, 2:3]
        zero_col = small[:, 3:4]
        valid = sb(root, "valid", [P, NT])

        att = ExitStack()
        qtab = sb(att, "qtab", [P, NT, D])
        start_f = sb(att, "start_f", [P, NT])
        deg_f = sb(att, "deg_f", [P, NT])
        counts = sb(att, "counts", [1, 4], I32)
        over_n = sb(att, "over_n", [1, 2 * NT], I32)
        sched = sb(att, "sched", [1, 2 * SCHED], I32)
        idx_tab = sb(att, "idx_tab", [P, NT * FAST], I32)
        neg_tab = sb(att, "neg_tab", [P, NT * FAST])

        pro = ExitStack()
        wq = sb(pro, "wq", [P, HALVES, D])
        wkv = sb(pro, "wkv", [P, HALVES, 2 * D])
        bias = sb(pro, "bias", [P, 3 * D])
        kln_wc = sb(pro, "kln_wc", [P, HALVES])
        kln_bc = sb(pro, "kln_bc", [P, HALVES])
        vln_wb = sb(pro, "vln_wb", [P, D])
        vln_bb = sb(pro, "vln_bb", [P, D])
        head_mask = sb(pro, "head_mask", [P, P])

        pre = ExitStack()
        w_raw = sb(pre, "w_raw", [P, 4, HALVES, D])
        b_col = sb(pre, "b_col", [P, 4, HALVES])
        rel = sb(pre, "rel", [P, 2, HALVES, P])
        pri = sb(pre, "pri", [P, HALVES])
        qdiag = sb(pre, "qdiag", [P, HALVES, P])
        adiag = sb(pre, "adiag", [P, P])
        first = sb(pre, "first", [P, BLOCKS], I32)
        first_f = sb(pre, "first_f", [P, BLOCKS])
        spread = sb(pre, "spread", [P, EROWS])
        firsts = sb(pre, "firsts", [P, EROWS])
        junk = sb(pre, "junk", [P, EROWS])
        node_i = sb(pre, "node_i", [P, NT], I32)
        node_f = sb(pre, "node_f", [P, NT])
        coarse = sb(pre, "coarse", [P, NT])
        block_f = sb(pre, "block_f", [P, NT])
        block_i = sb(pre, "block_i", [P, NT], I32)
        rows = sb(pre, "rows", [P, NT, P], I32)
        fine = sb(pre, "fine", [P, NT])
        start_i = sb(pre, "start_i", [P, NT + 1], I32)
        end_i = sb(pre, "end_i", [P, NT], I32)
        end_f = sb(pre, "end_f", [P, NT])
        slot_i = sb(pre, "slot_i", [P, FAST], I32)
        slot_f = sb(pre, "slot_f", [P, FAST])
        fpos_i = sb(pre, "fpos_i", [P, SCHED // P], I32)
        fpos = sb(pre, "fpos", [P, SCHED // P])
        window = sb(pre, "window", [P, NT, FAST], I32)
        upto = sb(pre, "upto", [NT, NT])
        tmax = sb(pre, "tmax", [NT, 1])
        tint = sb(pre, "tint", [NT, 2], I32)
        tng = sb(pre, "tng", [NT, 4])
        gend = sb(pre, "gend", [P, NT])
        grow = sb(pre, "grow", [P, NT])
        orow = sb(pre, "orow", [P, 2 * NT])
        sch_f = sb(pre, "sch_f", [P, SCHED // P, 4])
        sch_i = sb(pre, "sch_i", [P, SCHED // P, 2], I32)
        k3_i = sb(pre, "k3_i", [1, SCHED], I32)
        k3_f = sb(pre, "k3_f", [1, SCHED])
        cnt_f = sb(pre, "cnt_f", [1, 4])
        pre_ps = ExitStack()
        ps_first = pb(pre_ps, "ps_first", [P, 4, 512])
        ps_w = pb(pre_ps, "ps_w", [P, 3, 512])
        ps_small = pb(pre_ps, "ps_small", [P, 512])
        pre_ps.close()
        pre.close()

        prj = ExitStack()
        xt = sb(prj, "xt", [P, 2, D])
        st6 = sb(prj, "st6", [P, 2, 6])
        mv = sb(prj, "mv", [P, 2, 2])
        rstd = sb(prj, "rstd", [P, 2, 1])
        xn = sb(prj, "xn", [P, 2, D])
        hsum = sb(prj, "hsum", [P, 2, H])
        hss = sb(prj, "hss", [P, 2, H])
        hr = sb(prj, "hr", [P, 2, H])
        xc = sb(prj, "xc", [P, 2, D])
        sq = sb(prj, "sq", [P, 2, D])
        nh = sb(prj, "nh", [P, 2, D])
        xnt = sb(prj, "xnt", [P, 2, HALVES, P])
        kvst = sb(prj, "kvst", [P, 2, 2 * D])
        zeros = sb(prj, "zeros", [P, 512])
        s_col = sb(prj, "s_col", [P, HALVES])
        t_col = sb(prj, "t_col", [P, HALVES])
        mtmp = sb(prj, "mtmp", [P, 4, P])
        prj_ps = ExitStack()
        ps_t = pb(prj_ps, "ps_t", [P, 2, 512])
        ps_q = pb(prj_ps, "ps_q", [P, 2, 512])
        ps_kv = pb(prj_ps, "ps_kv", [P, 2, 512])
        ps_g = pb(prj_ps, "ps_g", [P, 512])
        prj_ps.close()
        prj.close()
        pro.close()

        acc = sb(att, "acc", [P, NT, D])
        m_tab = sb(att, "m_tab", [P, NT, H])
        z_tab = sb(att, "z_tab", [P, NT, H])
        kv = [sb(att, f"kv{k}", [P, SLOTS, 2 * D]) for k in range(UNROLL)]
        idx = [sb(att, f"idx{k}", [P, SLOTS], I32) for k in range(UNROLL)]
        prod = sb(att, "prod", [P, SLOTS * D])
        ex = [sb(att, f"ex{k}", [P, (SLOTS + 1) * H]) for k in range(UNROLL)]
        hmax = [sb(att, f"hmax{k}", [P, H]) for k in range(UNROLL)]
        mnew = [sb(att, f"mnew{k}", [P, H]) for k in range(UNROLL)]
        zsum = [sb(att, f"zsum{k}", [P, H]) for k in range(UNROLL)]
        o_pos = sb(att, "o_pos", [P, 2])
        o_posi = sb(att, "o_posi", [P, 1], I32)
        o_win = sb(att, "o_win", [P, SLOTS], I32)
        o_msk = sb(att, "o_msk", [P, 2, SLOTS])
        iota8 = sb(att, "iota8", [P, SLOTS])
        att_ps = ExitStack()
        ps_sum = [pb(att_ps, f"ps_sum{k}", [P, 512]) for k in range(UNROLL)]
        att_ps.close()
        att.close()

        w1 = sb(root, "w1", [P, NE, HALVES, HID])
        w2 = sb(root, "w2", [P, NE, HC, D])
        wg = sb(root, "wg", [P, HALVES, NE])
        b1 = sb(root, "b1", [P, NE * HC])
        b1r = sb(root, "b1r", [NE * HC, P])
        b2 = sb(root, "b2", [NE, D])
        bgb = sb(root, "bgb", [P, NE])
        iotae = sb(root, "iotae", [P, NE])
        fx = sb(root, "fx", [P, 2, D])
        fxnt = sb(root, "fxnt", [P, 2, HALVES, P])
        fagg = sb(root, "fagg", [P, 2, D])
        faggt = sb(root, "faggt", [P, 2, HALVES, P])
        x2 = sb(root, "x2", [P, 2, D])
        x3 = sb(root, "x3", [P, 2, D])
        x3t = sb(root, "x3t", [P, HALVES, TOK])
        fst = sb(root, "fst", [P, 2, 6])
        fmv = sb(root, "fmv", [P, 2, 2])
        frs = sb(root, "frs", [P, 2, 1])
        lg = sb(root, "lg", [P, 2, NE])
        top = sb(root, "top", [P, 2, 8])
        topi = sb(root, "topi", [P, 2, 8], U32)
        topf = sb(root, "topf", [P, 2, 8])
        gw = sb(root, "gw", [P, 2, 4])
        wd = sb(root, "wd", [P, 2, NE])
        wd2 = sb(root, "wd2", [P, 2, NE])
        wdt = sb(root, "wdt", [NE, 2, P])
        hid = sb(root, "hid", [P, 2, HC, TOK])
        ffn_ps = ExitStack()
        ps_h = pb(ffn_ps, "ps_h", [P, 4, 2, TOK])
        ps_y = pb(ffn_ps, "ps_y", [P, 2, 2, D])
        ps_a = pb(ffn_ps, "ps_a", [P, 2, D])
        ps_b = pb(ffn_ps, "ps_b", [P, 512])

        names = """pool_const w_in small_in first_in dve_pre dve_prj dve_att dve_pjl dve_attl dve_spt dve_spl dve_ffl ffn_step dve_step act_pre pe_pre
            block_ready rows_in start_ready start_out end_in window_in sched_ready sched_out sched_in prep_done
            tables_ready pool_step pool_ready
            xnt_ready kvst_ready st_free xnt_out kv_out x2_free x_in0 x_in1 x_free var_ready std_ready xn_ready xt_ps hss_ready hstd_ready
            nh_ready proj_ps gram_ps x_loaded prj_stored gram_done mix_ready
            o_idx o_winin o_kvidx o_gath o_sready o_pready o_vready o_sum att_done agg_out agg_ready left
            w_ffn w_ffns fx_in fagg_in fxn_in agt_ps agt_sb res_ps var2 std2 x3_ready x3_ps x3_sb gate_ps gate_d gate_e gate_n wd_ready wdt_ps wdt_sb
            b2_ps h_ps h_sb y_ps y_used out_ready outd in_free b1_ps ffn_const""".split()
        S = {n: sem(n) for n in names}
        idx_ready = [sem(f"idx_ready{k}") for k in range(UNROLL)]
        kv_free = [sem(f"kv_free{k}") for k in range(UNROLL)]
        gathered = [sem(f"gathered{k}") for k in range(UNROLL)]
        s_ready = [sem(f"s_ready{k}") for k in range(UNROLL)]
        p_ready = [sem(f"p_ready{k}") for k in range(UNROLL)]
        v_ready = [sem(f"v_ready{k}") for k in range(UNROLL)]
        summed = [sem(f"summed{k}") for k in range(UNROLL)]

        def chain(eng, s, i=0, per=0, first=0):
            n = [0]

            def link(ins, carry=False):
                n[0] += 1
                ins.then_inc(s, 1)
                eng.wait_ge(s, i * per + first + n[0])
                if carry:
                    eng.sem_inc(S["dve_step"], 1)

            link.n = n
            return link

        src_rows = a["src"]
        dst_rows = a["dst"]
        block = root.enter_context(nc.Block())

        def gather(pool, dst_ap, table, idx_ap, bound, s):
            pool.indirect_dma_start(out=dst_ap, out_offset=None, in_=table,
                                    in_offset=bass.IndirectOffsetOnAxis(ap=idx_ap, axis=0),
                                    bounds_check=bound, oob_is_err=False).then_inc(s, 16)

        def pool_wait(pool, s, value):
            pool.wait_ge(s, value)
            pool.sem_inc(S["pool_step"], 1)

        @block.sync
        def _(sp):
            sp.dma_start(first[:, :], dst_rows.rearrange("(j q) c -> q j c", q=P)[:, :, 0]).then_inc(S["first_in"], 16)
            for n, w in enumerate(("Wq", "Wk", "Wv", "Wa")):
                sp.dma_start(w_raw[:, n], a["L0_gnn_" + w].rearrange("(c p) n -> p c n", p=P)).then_inc(S["w_in"], 16)
            for n, b in enumerate(("bq", "bk", "bv")):
                sp.dma_start(b_col[:, n], a["L0_gnn_" + b].rearrange("(c p) -> p c", p=P)).then_inc(S["small_in"], 16)
            sp.dma_start(aba[:, :], a["L0_gnn_ba"].partition_broadcast(P)).then_inc(S["small_in"], 16)
            sp.wait_ge(S["pool_const"], 5)
            for n, r in enumerate(("rel_att", "rel_msg")):
                for h in range(H):
                    o = DK * (h % 4)
                    sp.dma_start(rel[o:o + DK, n, h // 4, o:o + DK], a["L0_gnn_" + r][h]).then_inc(S["small_in"], 16)
            for h in range(H):
                o = DK * (h % 4)
                sp.dma_start(pri[o:o + DK, h // 4:h // 4 + 1],
                             a["L0_gnn_rel_pri"][h:h + 1].partition_broadcast(DK)).then_inc(S["small_in"], 16)
            sp.dma_start(alpha, a["L0_gnn_skip"].partition_broadcast(P)).then_inc(S["small_in"], 16)
            for t, nme in ((kln_wc, "kln_weight"), (kln_bc, "kln_bias")):
                sp.dma_start(t[:, :], a["L0_mix_" + nme].rearrange("(c p) -> p c", p=P)).then_inc(S["small_in"], 16)
            for t, nme in ((vln_wb, "vln_weight"), (vln_bb, "vln_bias")):
                sp.dma_start(t[:, :], a["L0_mix_" + nme].partition_broadcast(P)).then_inc(S["small_in"], 16)
            sp.wait_ge(S["start_ready"], 1)
            sp.dma_start(rpd.rearrange("(t p) o -> p (t o)", p=P), start_i[:, :]).then_inc(S["start_out"], 16)
            sp.wait_ge(S["start_out"], 16)
            sp.dma_start(end_i[:, :], rpd[1:NP + 1, :].rearrange("(t p) o -> p (t o)", p=P)).then_inc(S["end_in"], 16)
            sp.wait_ge(S["sched_ready"], 1)
            sp.dma_start(schedd.rearrange("(c p) w -> p c w", p=P), sch_i[:, :, :]).then_inc(S["sched_out"], 16)
            sp.wait_ge(S["sched_out"], 16)
            sp.dma_start(sched[:, :], schedd.rearrange("(a f) w -> a (f w)", a=1)).then_inc(S["sched_in"], 16)
            sp.wait_ge(S["prep_done"], 1)
            with sp.Fori(0, NT // 2) as i:
                sp.wait_ge(S["x_free"], i + 1)
                for b in range(2):
                    sp.dma_start(xt[:, b, :], a["x"][bass.ds((2 * i + b) * P, P), :]).then_inc(S[f"x_in{b}"], 16)
            sp.wait_ge(S["att_done"], 1)
            sp.dma_start(aggd.rearrange("t p f -> p t f"), acc[:, :, :]).then_inc(S["agg_out"], 16)
            sp.wait_ge(S["agg_out"], 16)
            sp.wait_ge(S["left"], 3)
            sp.sem_inc(S["agg_ready"], 1)
            sp.dma_start(wg[:, :, :], a["L0_ffn_Wg"].rearrange("(c p) n -> p c n", p=P)).then_inc(S["w_ffns"], 16)
            sp.dma_start(b1r[:, :], a["L0_ffn_b1"].rearrange("e (c p) -> (e c) p", p=P)).then_inc(S["w_ffns"], 16)
            sp.dma_start(b2[:, :], a["L0_ffn_b2"]).then_inc(S["w_ffns"], 16)
            sp.dma_start(bgb[:, :], a["L0_ffn_bg"].partition_broadcast(P)).then_inc(S["w_ffns"], 16)
            for e in range(NE):
                sp.dma_start(w1[:, e], a["L0_ffn_W1"][e].rearrange("(c p) n -> p c n", p=P)).then_inc(S["w_ffn"], 16)
                sp.dma_start(w2[:, e], a["L0_ffn_W2"][e].rearrange("(c p) n -> p c n", p=P)).then_inc(S["w_ffn"], 16)
            sp.sem_inc(S["x2_free"], 1)

            def load(i):
                sp.dma_start(fagg[:, :, :], aggd[bass.ds(2 * i, 2)].rearrange("t p f -> p t f")).then_inc(S["fx_in"], 16)
                sp.dma_start(fxnt[:, :, :, :], xntd[bass.ds(2 * i, 2)].rearrange("t p (c f) -> p t c f", c=HALVES))\
                    .then_inc(S["fx_in"], 16)
                sp.dma_start(fx[:, :, :], a["x"][bass.ds(2 * i * P, TOK), :].rearrange("(t p) f -> p t f", p=P))\
                    .then_inc(S["fx_in"], 16)

            def store(i):
                sp.wait_ge(S["out_ready"], i + 1)
                sp.dma_start(out[bass.ds(2 * i * P, TOK), :].rearrange("(t p) f -> p t f", p=P), x2[:, :, :])\
                    .then_inc(S["outd"], 16)
                sp.wait_ge(S["outd"], 16 * i + 16)
                sp.sem_inc(S["x2_free"], 1)

            load(0)
            with sp.Fori(0, NT // 2 - 1) as i:
                sp.wait_ge(S["in_free"], i + 1)
                load(i + 1)
                store(i)
            store(NT // 2 - 1)
            sp.wait_ge(S["outd"], 16 * (NT // 2))

        @block.gpsimd
        def _(pool):
            g = nc.gpsimd
            g.memset(ident[:, :], 0.0).then_inc(S["pool_const"], 1)
            g.memset(ones[:, :], 1.0).then_inc(S["pool_const"], 1)
            g.memset(rel[:, :, :, :], 0.0).then_inc(S["pool_const"], 1)
            g.iota(node_i[:, :], [[P, NT]], base=0, channel_multiplier=1).then_inc(S["pool_const"], 1)
            g.iota(slot_i[:, :], [[1, FAST]], base=0, channel_multiplier=0).then_inc(S["pool_const"], 1)
            g.iota(fpos_i[:, :], [[P, SCHED // P]], base=0, channel_multiplier=1).then_inc(S["pool_const"], 1)
            g.iota(k3_i[:, :], [[UNROLL, SCHED]], base=0, channel_multiplier=0).then_inc(S["pool_const"], 1)
            g.memset(upto[:, :], 1.0).then_inc(S["pool_const"], 1)
            g.memset(head_mask[:, :], 1.0).then_inc(S["pool_const"], 1)
            g.memset(start_i[:, NT:NT + 1], E).then_inc(S["pool_const"], 1)
            pool.wait_ge(S["pool_const"], 10)
            g.affine_select(out=ident[:, :], in_=ident[:, :], compare_op=ALU.not_equal, fill=1.0, base=0,
                            pattern=[[-1, P]], channel_multiplier=1).then_inc(S["pool_const"], 1)
            g.affine_select(out=upto[:, :], in_=upto[:, :], compare_op=ALU.is_ge, fill=0.0, base=0,
                            pattern=[[1, NT]], channel_multiplier=-1).then_inc(S["pool_const"], 1)
            hm = head_mask[:, :].rearrange("p (h d) -> p h d", h=4)
            g.affine_select(out=hm, in_=hm, compare_op=ALU.is_ge, fill=0.0, base=0,
                            pattern=[[-DK, 4], [0, DK]], channel_multiplier=1).then_inc(S["pool_const"], 1)
            pool.wait_ge(S["pool_const"], 13)
            g.affine_select(out=hm, in_=hm, compare_op=ALU.is_ge, fill=0.0, base=DK - 1,
                            pattern=[[DK, 4], [0, DK]], channel_multiplier=-1).then_inc(S["pool_const"], 1)
            pool.wait_ge(S["block_ready"], 1)
            for t in range(NT):
                gather(pool, rows[:, t, :], dst_rows, block_i[:, t:t + 1], EROWS - 1, S["rows_in"])
            pool.wait_ge(S["start_ready"], 1)
            for t in range(NT):
                gather(pool, window[:, t, :], src_rows, start_i[:, t:t + 1], E, S["window_in"])
            pool.sem_inc(S["st_free"], 1)
            with pool.Fori(0, NT // 2) as i:
                for b in range(2):
                    pool_wait(pool, S["xnt_ready"], 2 * i + b + 1)
                    pool.dma_start(xntd[bass.ds(2 * i + b, 1)].rearrange("t p f -> p (t f)"),
                                   xnt[:, b].rearrange("p c f -> p (c f)")).then_inc(S["xnt_out"], 16)
                    pool_wait(pool, S["kvst_ready"], 2 * i + b + 1)
                    pool.dma_start(kvd[bass.ds((2 * i + b) * P, P), :], kvst[:, b, :]).then_inc(S["kv_out"], 16)
                pool_wait(pool, S["xnt_out"], 32 * i + 32)
                pool_wait(pool, S["kv_out"], 32 * i + 32)
                pool.sem_inc(S["st_free"], 1)
            pool.wait_ge(S["mix_ready"], 1)
            for k in range(UNROLL):
                g.memset(kv[k][:, :, :], 0.0).then_inc(kv_free[k], 1)
            for s in range(SLOTS):
                g.memset(iota8[:, s:s + 1], float(s)).then_inc(S["pool_ready"], 1)
            pool.wait_ge(S["tables_ready"], 1)
            passes = pool.value_load(counts[0:1, 0:1], min_val=1, max_val=PASSES)
            with pool.Fori(0, passes) as i:
                for k in range(UNROLL):
                    pool_wait(pool, idx_ready[k], i + 1)
                    pool_wait(pool, kv_free[k], i + 1)
                    for s in range(SLOTS):
                        gather(pool, kv[k][:, s, :], kvd, idx[k][:, s:s + 1], N - 1, gathered[k])
            flag = pool.value_load(counts[0:1, 1:2], min_val=0, max_val=1)
            with pool.If(flag > 0):
                with pool.Fori(0, NT) as t:
                    n = pool.value_load(over_n[0:1, bass.ds(t, 1)], min_val=1, max_val=E // SLOTS + 1)
                    n0 = pool.value_load(over_n[0:1, bass.ds(t + NT, 1)], min_val=0, max_val=E // SLOTS + NT)
                    with pool.Fori(0, n) as i:
                        pool_wait(pool, S["o_idx"], n0 + i + 1)
                        gather(pool, o_win[:, :], src_rows, o_posi[:, 0:1], E, S["o_winin"])
                        pool_wait(pool, S["o_kvidx"], n0 + i + 1)
                        for s in range(SLOTS):
                            gather(pool, kv[0][:, s, :], kvd, idx[0][:, s:s + 1], N - 1, S["o_gath"])
            pool.sem_inc(S["left"], 1)
            pool.wait_ge(S["agg_ready"], 1)
            g.iota(topi[:, 0, :], [[1, NE]], base=0, channel_multiplier=0).then_inc(S["ffn_const"], 1)

        @block.tensor
        def _(pe):
            mm = nc.tensor.matmul
            pe.wait_ge(S["dve_pre"], 1)
            for c in range(4):
                w = min(512, EROWS - 512 * c)
                ins = mm(ps_first[:, c, 0:w], ones[:, :], spread[:, 512 * c:512 * c + w], start=True, stop=True)
            ins.then_inc(S["pe_pre"], 1)
            pe.wait_ge(S["w_in"], 64)
            pe.wait_ge(S["small_in"], 16 * 33)
            pe.wait_ge(S["dve_pre"], 2)
            for half in range(HALVES):
                cin = slice(half * P, (half + 1) * P)
                for hc in range(HALVES):
                    for n in range(3):
                        r = qdiag[:, hc] if n == 0 else rel[:, n - 1, hc]
                        ins = mm(ps_w[:, n, half * D + hc * P:half * D + (hc + 1) * P], w_raw[:, n, hc, cin], r,
                                 start=True, stop=True)
            ins.then_inc(S["pe_pre"], 1)
            for half in range(HALVES):
                cin = slice(half * P, (half + 1) * P)
                for hc in range(HALVES):
                    ins = mm(ps_small[:, half * D + hc * P:half * D + (hc + 1) * P], w_raw[:, 3, hc, cin], adiag[:, :],
                             start=True, stop=True)
            ins.then_inc(S["pe_pre"], 1)
            pe.wait_ge(S["dve_pre"], 3)
            for n in range(3):
                for hc in range(HALVES):
                    r = qdiag[:, hc] if n == 0 else rel[:, n - 1, hc]
                    ins = mm(ps_w[:, n, hc * P:(hc + 1) * P], bcast(b_col[:, n, hc:hc + 1], [P, P]), r,
                             start=True, stop=True)
            ins.then_inc(S["pe_pre"], 1)
            pe.wait_ge(S["dve_pre"], 4)
            nc.tensor.transpose(ps_small[0:NT, 0:P], deg_f[:, :], ident[:, :]).then_inc(S["pe_pre"], 1)
            pe.wait_ge(S["dve_pre"], 5)
            mm(ps_small[:, 128:128 + NT], bcast(tng[:, 0:1], [NT, P]), upto[:, :], start=True, stop=True)
            mm(ps_small[:, 192:192 + NT], bcast(tng[:, 0:1], [NT, P]), ident[0:NT, 0:NT], start=True, stop=True)
            mm(ps_small[:, 256:256 + NT], bcast(tng[:, 1:2], [NT, P]), upto[:, :], start=True, stop=True)
            mm(ps_small[:, 320:320 + NT], bcast(tng[:, 1:2], [NT, P]), ident[0:NT, 0:NT], start=True, stop=True)
            mm(ps_small[:, 384:385], bcast(tng[:, 3:4], [NT, P]), ones[0:NT, 0:1], start=True, stop=True)\
                .then_inc(S["pe_pre"], 1)

            pe.wait_ge(S["prep_done"], 1)
            mm(ps_g[:, :], zeros[:, 0:P], zeros[:, :], start=True, stop=False, skip_group_check=True).then_inc(S["gram_ps"], 1)
            with pe.Fori(0, NT // 2) as i:
                for b in range(2):
                    pe.wait_ge(S["xn_ready"], 2 * i + b + 1)
                    for c in range(HALVES):
                        ins = nc.tensor.transpose(ps_t[:, b, c * P:(c + 1) * P], xn[:, b, c * P:(c + 1) * P], ident[:, :])
                    ins.then_inc(S["xt_ps"], 1)
                for b in range(2):
                    pe.wait_ge(S["xnt_ready"], 2 * i + b + 1)
                    for c in range(HALVES):
                        mm(ps_q[:, b, 0:D], xnt[:, b, c, :], wq[:, c, :], start=(c == 0), stop=(c == HALVES - 1))
                    for c in range(HALVES):
                        ins = mm(ps_kv[:, b, :], xnt[:, b, c, :], wkv[:, c, :], start=(c == 0), stop=(c == HALVES - 1))
                    ins.then_inc(S["proj_ps"], 1)
                for b in range(2):
                    pe.wait_ge(S["nh_ready"], 2 * i + b + 1)
                    for c in range(HALVES):
                        cs = slice(c * P, (c + 1) * P)
                        mm(ps_g[:, cs], nh[:, b, cs], nh[:, b, cs], start=False, stop=False, skip_group_check=True)
                    mm(ps_g[:, D:2 * D], ones[:, :], nh[:, b, :], start=False, stop=False,
                       skip_group_check=True).then_inc(S["gram_ps"], 1)

            pe.wait_ge(S["tables_ready"], 1)
            passes = pe.value_load(counts[0:1, 0:1], min_val=1, max_val=PASSES)
            with pe.Fori(0, passes) as i:
                for k in range(UNROLL):
                    pe.wait_ge(v_ready[k], i + 1)
                    for s in range(SLOTS):
                        ins = mm(ps_sum[k][:, 0:D], ident[:, :], kv[k][:, s, D:2 * D], start=(s == 0), stop=(s == SLOTS - 1))
                    ins.then_inc(summed[k], 1)
                    pe.wait_ge(summed[k], i + 1)
                    pe.sem_inc(kv_free[k], 1)
            flag = pe.value_load(counts[0:1, 1:2], min_val=0, max_val=1)
            with pe.If(flag > 0):
                with pe.Fori(0, NT) as t:
                    n = pe.value_load(over_n[0:1, bass.ds(t, 1)], min_val=1, max_val=E // SLOTS + 1)
                    n0 = pe.value_load(over_n[0:1, bass.ds(t + NT, 1)], min_val=0, max_val=E // SLOTS + NT)
                    with pe.Fori(0, n) as i:
                        pe.wait_ge(S["o_vready"], n0 + i + 1)
                        for s in range(SLOTS):
                            ins = mm(ps_sum[0][:, 0:D], ident[:, :], kv[0][:, s, D:2 * D], start=(s == 0), stop=(s == SLOTS - 1))
                        ins.then_inc(S["o_sum"], 1)

            pe.sem_inc(S["left"], 1)
            pe.wait_ge(S["agg_ready"], 1)
            pe.wait_ge(S["w_ffns"], 64)
            nc.tensor.transpose(ps_b[:, 0:NE * HC], b1r[:, :], ident[0:NE * HC, 0:NE * HC]).then_inc(S["b1_ps"], 1)
            pe.wait_ge(S["w_ffn"], 16 * 2 * NE)
            pe.wait_ge(S["ffn_const"], 2)
            with pe.Fori(0, NT // 2) as i:
                pe.wait_ge(S["fx_in"], 48 * i + 48)
                pe.wait_ge(S["ffn_step"], i + 1)
                for b in range(2):
                    for c in range(HALVES):
                        ins = nc.tensor.transpose(ps_a[:, b, c * P:(c + 1) * P], fagg[:, b, c * P:(c + 1) * P], ident[:, :])
                ins.then_inc(S["agt_ps"], 1)
                pe.wait_ge(S["agt_sb"], i + 1)
                for b in range(2):
                    for c in range(HALVES):
                        mm(ps_a[:, b, :], faggt[:, b, c, :], a_fold[:, c, :], start=(c == 0), stop=False, skip_group_check=True)
                    for c in range(HALVES):
                        ins = mm(ps_a[:, b, c * P:(c + 1) * P], fxnt[:, b, c, :], mix_w[:, c, :], start=False,
                                 stop=(c == 1), skip_group_check=True)
                ins.then_inc(S["res_ps"], 1)
                pe.wait_ge(S["x3_ready"], i + 1)
                for b in range(2):
                    for c in range(HALVES):
                        ins = nc.tensor.transpose(ps_a[:, c, b * P:(b + 1) * P], x3[:, b, c * P:(c + 1) * P], ident[:, :])
                ins.then_inc(S["x3_ps"], 1)
                pe.wait_ge(S["x3_sb"], i + 1)
                for b in range(2):
                    for c in range(HALVES):
                        ins = mm(ps_b[:, 64 + b * NE:64 + (b + 1) * NE], x3t[:, c, b * P:(b + 1) * P], wg[:, c, :],
                                 start=(c == 0), stop=(c == HALVES - 1), skip_group_check=True)
                ins.then_inc(S["gate_ps"], 1)

                def up(e):
                    for q in range(HC // 2):
                        pe.wait_ge(S["h_sb"], 32 * i + 4 * e + q + 1)
                        for j in range(2):
                            c0 = (2 * q + j) * P
                            for c in range(HALVES):
                                ins = mm(ps_h[:, q, j, :], w1[:, e, c, c0:c0 + P], x3t[:, c, :],
                                         start=(c == 0), stop=(c == HALVES - 1), skip_group_check=True)
                        ins.then_inc(S["h_ps"], 1)

                def down(e):
                    pe.wait_ge(S["h_sb"], 32 * i + 4 * (e + 1) + 4)
                    pe.wait_ge(S["y_used"], 8 * i + e + 1)
                    for b in range(2):
                        for c in range(HC):
                            ins = mm(ps_y[:, e % 2, b, :], hid[:, e % 2, c, b * P:(b + 1) * P], w2[:, e, c, :],
                                     start=(c == 0), stop=(c == HC - 1))
                    ins.then_inc(S["y_ps"], 1)

                up(0)
                for e in range(1, NE):
                    up(e)
                    down(e - 1)
                down(NE - 1)
                pe.wait_ge(S["wd_ready"], i + 1)
                for b in range(2):
                    ins = nc.tensor.transpose(ps_b[0:NE, 128 + b * P:128 + (b + 1) * P], wd[:, b, :], ident[:, :])
                ins.then_inc(S["wdt_ps"], 1)
                pe.wait_ge(S["wdt_sb"], i + 1)
                for b in range(2):
                    ins = mm(ps_a[:, b, :], wdt[:, b, :], b2[:, :], start=True, stop=True)
                ins.then_inc(S["b2_ps"], 1)

        @block.scalar
        def _(act):
            ac = nc.scalar.activation
            act.wait_ge(S["small_in"], 16 * 33)
            ac(alpha, alpha, ACT.Exp, scale=-1.0).then_inc(S["act_pre"], 1)
            act.wait_ge(S["prep_done"], 1)
            with act.Fori(0, NT // 2) as i:
                for b in range(2):
                    act.wait_ge(S["var_ready"], 2 * i + b + 1)
                    ac(rstd[:, b, :], mv[:, b, 1:2], ACT.Sqrt, bias=eps_ln).then_inc(S["std_ready"], 1)
                for b in range(2):
                    act.wait_ge(S["xt_ps"], 2 * i + b + 1)
                    act.wait_ge(S["st_free"], i + 1)
                    ac(xnt[:, b], ps_t[:, b, 0:D].rearrange("p (c f) -> p c f", c=HALVES), ACT.Copy).then_inc(S["xnt_ready"], 1)
                for b in range(2):
                    act.wait_ge(S["hss_ready"], 2 * i + b + 1)
                    ac(hss[:, b, :], hss[:, b, :], ACT.Sqrt, bias=zero_col, scale=1.0 / (DK - 1)).then_inc(S["hstd_ready"], 1)
            act.wait_ge(S["tables_ready"], 1)
            passes = act.value_load(counts[0:1, 0:1], min_val=1, max_val=PASSES)
            with act.Fori(0, passes) as i:
                for k in range(UNROLL):
                    act.wait_ge(s_ready[k], i + 1)
                    ac(ex[k][:, :], ex[k][:, :], ACT.Exp).then_inc(p_ready[k], 1)
            flag = act.value_load(counts[0:1, 1:2], min_val=0, max_val=1)
            with act.If(flag > 0):
                with act.Fori(0, NT) as t:
                    n = act.value_load(over_n[0:1, bass.ds(t, 1)], min_val=1, max_val=E // SLOTS + 1)
                    n0 = act.value_load(over_n[0:1, bass.ds(t + NT, 1)], min_val=0, max_val=E // SLOTS + NT)
                    with act.Fori(0, n) as i:
                        act.wait_ge(S["o_sready"], n0 + i + 1)
                        ac(ex[0][:, :], ex[0][:, :], ACT.Exp).then_inc(S["o_pready"], 1)
            act.sem_inc(S["left"], 1)
            act.wait_ge(S["agg_ready"], 1)
            act.wait_ge(S["b1_ps"], 1)
            ac(b1[:, :], ps_b[:, 0:NE * HC], ACT.Copy).then_inc(S["ffn_const"], 1)
            act.wait_ge(S["ffn_const"], 2)
            act.sem_inc(S["h_sb"], 4)
            with act.Fori(0, NT // 2) as i:
                act.wait_ge(S["agt_ps"], i + 1)
                ac(faggt[:, :, :, :], ps_a[:, :, :].rearrange("p b (c f) -> p b c f", c=HALVES), ACT.Copy).then_inc(S["agt_sb"], 1)
                act.wait_ge(S["var2"], i + 1)
                ac(frs[:, :, :], fmv[:, :, 1:2], ACT.Sqrt, bias=eps_ln).then_inc(S["std2"], 1)
                act.wait_ge(S["x3_ps"], i + 1)
                ac(x3t[:, :, :], ps_a[:, :, :], ACT.Copy).then_inc(S["x3_sb"], 1)
                act.wait_ge(S["gate_d"], i + 1)
                ac(gw[:, :, 1:2], gw[:, :, 0:1], ACT.Exp).then_inc(S["gate_e"], 1)
                for e in range(NE):
                    for q in range(HC // 2):
                        act.wait_ge(S["h_ps"], 32 * i + 4 * e + q + 1)
                        if e > 1:
                            act.wait_ge(S["y_ps"], 8 * i + e - 1)
                        for j in range(2):
                            c = 2 * q + j
                            ins = ac(hid[:, e % 2, c, :], ps_h[:, q, j, :], ACT.Gelu, bias=b1[:, e * HC + c:e * HC + c + 1])
                        ins.then_inc(S["h_sb"], 1)
                act.wait_ge(S["wdt_ps"], i + 1)
                ac(wdt[:, :, :], ps_b[0:NE, 128:128 + 2 * P].rearrange("p (b f) -> p b f", b=2), ACT.Copy).then_inc(S["wdt_sb"], 1)

        @block.vector
        def _(dve):
            v = nc.vector
            tt, ts, stt, red = v.tensor_tensor, v.tensor_scalar, v.scalar_tensor_tensor, v.tensor_reduce
            link = chain(dve, S["dve_prj"])
            dve.wait_ge(S["first_in"], 16)
            dve.wait_ge(S["pool_const"], 14)
            link(v.memset(small[:, 2:4], 0.0))
            link(v.memset(eps_ln, LN_EPS))
            link(v.tensor_copy(first_f[:, :], first[:, :]))
            for j in range(BLOCKS):
                ins = ts(spread[:, j * P:(j + 1) * P], ident[:, :], first_f[:, j:j + 1], None, ALU.mult)
            ins.then_inc(S["dve_pre"], 1)
            dve.wait_ge(S["small_in"], 16 * 33)
            dve.wait_ge(S["act_pre"], 1)
            link(ts(alpha, alpha, 1.0, None, ALU.add))
            link(v.reciprocal(alpha, alpha))
            link(ts(two_minus_alpha, alpha, -1.0, 2.0, ALU.mult, ALU.add))
            link(ts(aba[:, :], aba[:, :], alpha, None, ALU.mult))
            link(ts(pri[:, :], pri[:, :], float(DK) ** -0.5, None, ALU.mult))
            for hc in range(HALVES):
                ts(qdiag[:, hc, :], ident[:, :], pri[:, hc:hc + 1], None, ALU.mult)
            ts(adiag[:, :], ident[:, :], alpha, None, ALU.mult).then_inc(S["dve_pre"], 1)
            dve.wait_ge(S["pe_pre"], 3)
            v.tensor_copy(wq[:, :, :], ps_w[:, 0, :].rearrange("p (c n) -> p c n", c=HALVES))
            v.tensor_copy(wkv[:, :, 0:D], ps_w[:, 1, :].rearrange("p (c n) -> p c n", c=HALVES))
            v.tensor_copy(wkv[:, :, D:2 * D], ps_w[:, 2, :].rearrange("p (c n) -> p c n", c=HALVES))
            v.tensor_copy(a_fold[:, :, :], ps_small[:, :].rearrange("p (c n) -> p c n", c=HALVES)).then_inc(S["dve_pre"], 1)
            dve.wait_ge(S["pe_pre"], 4)
            link(v.tensor_copy(bias[:, :].rearrange("p (a n) -> p a n", a=3), ps_w[:, :, 0:D]))
            for c in range(4):
                w = min(512, EROWS - 512 * c)
                ins = v.tensor_copy(firsts[:, 512 * c:512 * c + w], ps_first[:, c, 0:w])
            link(ins)
            link(v.tensor_copy(node_f[:, :], node_i[:, :]))
            with dve.Fori(0, NT) as t:
                ts(junk[:, :], firsts[:, :], node_f[:, bass.ds(t, 1)], 0.0, ALU.is_lt, ALU.add,
                   accum_out=coarse[:, bass.ds(t, 1)]).then_inc(S["dve_att"], 1)
                dve.wait_ge(S["dve_att"], t + 1)
            link(ts(block_f[:, :], coarse[:, :], -1.0, 0.0, ALU.add, ALU.max))
            v.tensor_copy(block_i[:, :], block_f[:, :]).then_inc(S["block_ready"], 1)
            dve.wait_ge(S["rows_in"], 16 * NT)
            with dve.Fori(0, NT) as t:
                ts(junk[:, 0:P], rows[:, bass.ds(t, 1), :].rearrange("p a c -> p (a c)"), node_f[:, bass.ds(t, 1)], 0.0,
                   ALU.is_lt, ALU.add, accum_out=fine[:, bass.ds(t, 1)]).then_inc(S["dve_att"], 1)
                dve.wait_ge(S["dve_att"], NT + t + 1)
            link(stt(start_f[:, :], block_f[:, :], float(P), fine[:, :], ALU.mult, ALU.add))
            v.tensor_copy(start_i[:, 0:NT], start_f[:, :]).then_inc(S["start_ready"], 1)
            dve.wait_ge(S["end_in"], 16)
            link(v.tensor_copy(end_f[:, :], end_i[:, :]))
            link(tt(deg_f[:, :], end_f[:, :], start_f[:, :], ALU.subtract))
            ts(valid[:, :], deg_f[:, :], 0.5, None, ALU.is_gt).then_inc(S["dve_pre"], 1)
            dve.wait_ge(S["pe_pre"], 5)
            link(red(tmax[:, :], ps_small[0:NT, 0:P], X, ALU.max))
            link(ts(tint[:, 0:1], tmax[:, :], float(SLOTS - 1), None, ALU.add))
            link(ts(tint[:, 1:2], tint[:, 0:1], 3, None, ALU.logical_shift_right))
            link(v.tensor_copy(tng[:, 2:3], tint[:, 1:2]))
            link(ts(tng[:, 0:1], tng[:, 2:3], 1.0, float(GROUPS), ALU.max, ALU.min))
            link(ts(tng[:, 3:4], tng[:, 2:3], -float(GROUPS), 0.0, ALU.add, ALU.max))
            ts(tng[:, 1:2], tng[:, 3:4], 1.0, None, ALU.max).then_inc(S["dve_pre"], 1)
            dve.wait_ge(S["pe_pre"], 6)
            v.tensor_copy(gend[:, :], ps_small[:, 128:128 + NT])
            v.tensor_copy(grow[:, :], ps_small[:, 192:192 + NT])
            v.tensor_copy(orow[:, 0:NT], ps_small[:, 256:256 + NT])
            link(v.tensor_copy(orow[:, NT:2 * NT], ps_small[:, 320:320 + NT]))
            v.tensor_copy(over_n[:, 0:NT], orow[0:1, NT:2 * NT])
            link(tt(over_n[:, NT:2 * NT], orow[0:1, 0:NT], orow[0:1, NT:2 * NT], ALU.subtract))
            link(v.tensor_copy(fpos[:, :], fpos_i[:, :]))
            for c in range(SCHED // P):
                link(ts(junk[:, 0:RT], gend[:, 0:RT], fpos[:, c:c + 1], 0.0, ALU.is_le, ALU.add,
                        accum_out=sch_f[:, c, 0:1]))
                link(stt(junk[:, 0:RT], gend[:, 0:RT], fpos[:, c:c + 1], grow[:, 0:RT], ALU.is_le, ALU.mult,
                         accum_out=sch_f[:, c, 1:2]))
                link(tt(sch_f[:, c, 2:3], fpos[:, c:c + 1], sch_f[:, c, 1:2], ALU.subtract))
            link(ts(sch_f[:, :, 2], sch_f[:, :, 2], float(GROUPS - 1), None, ALU.min))
            link(stt(sch_f[:, :, 3], sch_f[:, :, 0], float(GROUPS), sch_f[:, :, 2], ALU.mult, ALU.add))
            v.tensor_copy(sch_i[:, :, 0], sch_f[:, :, 0])
            v.tensor_copy(sch_i[:, :, 1], sch_f[:, :, 3]).then_inc(S["sched_ready"], 1)
            link(v.tensor_copy(k3_f[:, :], k3_i[:, :]))
            link(ts(junk[0:1, 0:SCHED], k3_f[:, :], gend[0:1, RT - 1:RT], 0.0, ALU.is_lt, ALU.add, accum_out=cnt_f[:, 0:1]))
            link(ts(cnt_f[:, 1:2], ps_small[0:1, 384:385], 0.5, None, ALU.is_gt))
            link(v.tensor_copy(counts[:, 0:2], cnt_f[:, 0:2]))
            link(v.tensor_copy(slot_f[:, :], slot_i[:, :]))
            neg3 = neg_tab[:, :].rearrange("p (t s) -> p t s", t=NT)
            link(tt(neg3, bcast(slot_f[:, :].unsqueeze(1), [P, NT, FAST]), bcast(deg_f[:, :].unsqueeze(2), [P, NT, FAST]),
                    ALU.is_ge))
            dve.wait_ge(S["window_in"], 16 * NT)
            link(stt(idx_tab[:, :], neg_tab[:, :], SKIP, window[:, :, :].rearrange("p t s -> p (t s)"), ALU.mult, ALU.add))
            link(ts(neg_tab[:, :], neg_tab[:, :], NEG, None, ALU.mult))
            dve.wait_ge(S["sched_in"], 16)
            link(v.memset(zeros[:, :], 0.0))
            dve.sem_inc(S["x_free"], 1)
            dve.sem_inc(S["prep_done"], 1)

            pairs = range(2)
            with dve.Fori(0, NT // 2) as i:
                pl = chain(dve, S["dve_pjl"], i, PJ)
                for b in pairs:
                    dve.wait_ge(S[f"x_in{b}"], 16 * i + 16)
                    ins = v.bn_stats(st6[:, b, :], xt[:, b, :])
                pl(ins, carry=True)
                for b in pairs:
                    v.bn_aggr(mv[:, b, :], st6[:, b, :]).then_inc(S["var_ready"], 1)
                for b in pairs:
                    dve.wait_ge(S["std_ready"], 2 * i + b + 1)
                    pl(v.reciprocal(rstd[:, b, :], rstd[:, b, :]))
                    dve.wait_ge(S["var_ready"], 2 * i + b + 1)
                    ts(xn[:, b, :], xt[:, b, :], mv[:, b, 0:1], rstd[:, b, :], ALU.subtract, ALU.mult)\
                        .then_inc(S["xn_ready"], 1)
                dve.wait_ge(S["xn_ready"], 2 * i + 2)
                dve.sem_inc(S["x_free"], 1)
                xn4 = xn[:, :, :].rearrange("p b (h d) -> p b h d", h=H)
                for b in pairs:
                    ins = red(hsum[:, b, :], xn4[:, b], X, ALU.add)
                pl(ins)
                pl(ts(hsum[:, :, :], hsum[:, :, :], 1.0 / DK, None, ALU.mult))
                for b in pairs:
                    ins = tt(xc[:, b, :].rearrange("p (h d) -> p h d", h=H), xn4[:, b],
                             bcast(hsum[:, b, :].unsqueeze(2), [P, H, DK]), ALU.subtract)
                pl(ins)
                pl(tt(sq[:, :, :], xc[:, :, :], xc[:, :, :], ALU.mult))
                for b in pairs:
                    red(hss[:, b, :], sq[:, b, :].rearrange("p (h d) -> p h d", h=H), X, ALU.add)\
                        .then_inc(S["hss_ready"], 1)
                dve.wait_ge(S["hstd_ready"], 2 * i + 2)
                pl(ts(hss[:, :, :], hss[:, :, :], LN_EPS, None, ALU.add))
                pl(v.reciprocal(hr[:, :, :], hss[:, :, :]))
                dve.wait_ge(S["gram_ps"], 2 * i + 1)
                for b in pairs:
                    tt(nh[:, b, :].rearrange("p (h d) -> p h d", h=H), xc[:, b, :].rearrange("p (h d) -> p h d", h=H),
                       bcast(hr[:, b, :].unsqueeze(2), [P, H, DK]), ALU.mult).then_inc(S["nh_ready"], 1)
                for b in pairs:
                    dve.wait_ge(S["proj_ps"], 2 * i + b + 1)
                    tt(qtab[:, bass.ds(2 * i + b, 1), :].rearrange("p a f -> p (a f)"), ps_q[:, b, 0:D], bias[:, 0:D], ALU.add)
                    dve.wait_ge(S["st_free"], i + 1)
                    tt(kvst[:, b, :], ps_kv[:, b, :], bias[:, D:3 * D], ALU.add).then_inc(S["kvst_ready"], 1)
                assert pl.n[0] == PJ, pl.n[0]
            dve.wait_ge(S["gram_ps"], NT + 1)
            for c in range(HALVES):
                cs = slice(c * P, (c + 1) * P)
                sums = ps_g[:, D + c * P:D + (c + 1) * P]
                link(stt(mtmp[:, 0, :], sums, 1.0, ident[:, :], ALU.mult, ALU.mult, accum_out=s_col[:, c:c + 1]))
                link(tt(t_col[:, c:c + 1], kln_wc[:, c:c + 1], s_col[:, c:c + 1], ALU.mult))
                link(tt(mtmp[:, 0, :], ps_g[:, cs], vln_wb[:, cs], ALU.mult))
                link(ts(mtmp[:, 0, :], mtmp[:, 0, :], kln_wc[:, c:c + 1], None, ALU.mult))
                link(stt(mtmp[:, 1, :], vln_bb[:, cs], t_col[:, c:c + 1], mtmp[:, 0, :], ALU.mult, ALU.add))
                link(tt(mtmp[:, 2, :], sums, vln_wb[:, cs], ALU.mult))
                link(stt(mtmp[:, 3, :], vln_bb[:, cs], float(N), mtmp[:, 2, :], ALU.mult, ALU.add))
                link(stt(mtmp[:, 0, :], mtmp[:, 3, :], kln_bc[:, c:c + 1], mtmp[:, 1, :], ALU.mult, ALU.add))
                link(stt(mtmp[:, 1, :], mtmp[:, 0, :], 1.0 / N, head_mask[:, :], ALU.mult, ALU.mult))
                link(stt(mix_w[:, c, :], ident[:, :], two_minus_alpha, mtmp[:, 1, :], ALU.mult, ALU.add))
            dve.wait_ge(S["st_free"], NT // 2 + 1)
            dve.sem_inc(S["mix_ready"], 1)
            v.memset(m_tab[:, :, :], NEG)
            v.memset(z_tab[:, :, :], 0.0)
            v.memset(o_win[:, :], 0)
            link(v.memset(acc[:, :, :], 0.0))
            dve.sem_inc(S["tables_ready"], 1)

            def column(tab, t, w):
                return tab[:, bass.ds(t, 1), :].rearrange("p a f -> p (a f)")

            def stage(k, w, first):
                v.tensor_copy(idx[k][:, :], idx_tab[:, bass.ds(w * SLOTS, SLOTS)]).then_inc(idx_ready[k], 1)

            def scores(ln, k, t, neg, done):
                e3 = ex[k][:, 0:SLOTS * H].rearrange("p (s h) -> p s h", s=SLOTS)
                m = column(m_tab, t, H)
                ln(tt(prod[:, :].rearrange("p (s f) -> p s f", s=SLOTS), kv[k][:, :, 0:D],
                      bcast(qtab[:, bass.ds(t, 1), :], [P, SLOTS, D]), ALU.mult))
                ln(red(ex[k][:, 0:SLOTS * H], prod[:, :].rearrange("p (a d) -> p a d", d=DK), X, ALU.add))
                ln(tt(e3, e3, bcast(neg.unsqueeze(2), [P, SLOTS, H]), ALU.add))
                ln(red(hmax[k][:, :], e3.rearrange("p s h -> p h s"), X, ALU.max))
                ln(tt(mnew[k][:, :], hmax[k][:, :], m, ALU.max))
                tt(ex[k][:, SLOTS * H:], m, mnew[k][:, :], ALU.subtract)
                ln(tt(e3, e3, bcast(mnew[k][:, :].unsqueeze(1), [P, SLOTS, H]), ALU.subtract))
                ts(m, mnew[k][:, :], 1.0, None, ALU.mult).then_inc(done, 1)

            def weigh(ln, k, t, ready, value, done):
                e3 = ex[k][:, 0:SLOTS * H].rearrange("p (s h) -> p s h", s=SLOTS)
                z = column(z_tab, t, H)
                v4 = kv[k][:, :, D:2 * D].rearrange("p s (h d) -> p s h d", h=H)
                dve.wait_ge(ready, value)
                tt(v4, v4, bcast(e3.unsqueeze(3), [P, SLOTS, H, DK]), ALU.mult).then_inc(done, 1)
                red(zsum[k][:, :], e3.rearrange("p s h -> p h s"), X, ALU.add)
                ln(tt(z, z, ex[k][:, SLOTS * H:], ALU.mult))
                ln(tt(z, z, zsum[k][:, :], ALU.add))

            def add_up(ln, k, t, ready, value):
                o = column(acc, t, D)
                o3 = o.rearrange("p (h d) -> p h d", h=H)
                ln(tt(o3, o3, bcast(ex[k][:, SLOTS * H:].unsqueeze(2), [P, H, DK]), ALU.mult))
                dve.wait_ge(ready, value)
                ln(tt(o, o, ps_sum[k][:, 0:D], ALU.add))

            def entry(f):
                t = dve.value_load(sched[0:1, bass.ds(2 * f, 1)], min_val=0, max_val=NT - 1)
                w = dve.value_load(sched[0:1, bass.ds(2 * f + 1, 1)], min_val=0, max_val=NT * GROUPS - 1)
                return t, w

            passes = dve.value_load(counts[0:1, 0:1], min_val=1, max_val=PASSES)
            for k in range(UNROLL):
                w = dve.value_load(sched[0:1, 2 * k + 1:2 * k + 2], min_val=0, max_val=NT * GROUPS - 1)
                stage(k, w, True)
            with dve.Fori(0, passes) as i:
                ln = chain(dve, S["dve_attl"], i, ATT)
                ent = [entry(i * UNROLL + k) for k in range(UNROLL)]
                nxt = [entry(i * UNROLL + UNROLL + k)[1] for k in range(UNROLL)]

                def front(k):
                    t, w = ent[k]
                    dve.wait_ge(gathered[k], 16 * SLOTS * i + 16 * SLOTS)
                    scores(ln, k, t, neg_tab[:, bass.ds(w * SLOTS, SLOTS)], s_ready[k])
                    stage(k, nxt[k], False)
                    dve.wait_ge(s_ready[k], i + 1)

                def back(k):
                    weigh(ln, k, ent[k][0], p_ready[k], i + 1, v_ready[k])

                def total(k):
                    add_up(ln, k, ent[k][0], summed[k], i + 1)

                front(0)
                front(1)
                back(0)
                front(2)
                back(1)
                total(0)
                back(2)
                total(1)
                total(2)
                assert ln.n[0] == ATT, ln.n[0]
            flag = dve.value_load(counts[0:1, 1:2], min_val=0, max_val=1)
            with dve.If(flag > 0):
                with dve.Fori(0, NT) as t:
                    n = dve.value_load(over_n[0:1, bass.ds(t, 1)], min_val=1, max_val=E // SLOTS + 1)
                    n0 = dve.value_load(over_n[0:1, bass.ds(t + NT, 1)], min_val=0, max_val=E // SLOTS + NT)
                    lt = chain(dve, S["dve_spt"], t, 2)
                    lt(ts(o_pos[:, 0:1], start_f[:, bass.ds(t, 1)], float(FAST), None, ALU.add))
                    lt(ts(o_pos[:, 1:2], deg_f[:, bass.ds(t, 1)], -float(FAST), None, ALU.add), carry=True)
                    with dve.Fori(0, n) as i:
                        ln = chain(dve, S["dve_spl"], n0 + i, SPL)
                        v.tensor_copy(o_posi[:, :], o_pos[:, 0:1]).then_inc(S["o_idx"], 1)
                        ln(ts(o_msk[:, 0, :], iota8[:, :], o_pos[:, 1:2], None, ALU.is_ge))
                        ts(o_msk[:, 1, :], o_msk[:, 0, :], NEG, None, ALU.mult)
                        dve.wait_ge(S["o_winin"], 16 * (n0 + i) + 16)
                        stt(idx[0][:, :], o_msk[:, 0, :], SKIP, o_win[:, :], ALU.mult, ALU.add).then_inc(S["o_kvidx"], 1)
                        ts(o_pos[:, 0:1], o_pos[:, 0:1], float(SLOTS), None, ALU.add)
                        ln(ts(o_pos[:, 1:2], o_pos[:, 1:2], -float(SLOTS), None, ALU.add))
                        dve.wait_ge(S["o_gath"], 16 * SLOTS * (n0 + i) + 16 * SLOTS)
                        scores(ln, 0, t, o_msk[:, 1, :], S["o_sready"])
                        weigh(ln, 0, t, S["o_pready"], n0 + i + 1, S["o_vready"])
                        add_up(ln, 0, t, S["o_sum"], n0 + i + 1)
                        assert ln.n[0] == SPL, ln.n[0]
            link(ts(z_tab[:, :, :], z_tab[:, :, :], 0.5, None, ALU.max))
            link(v.reciprocal(z_tab[:, :, :], z_tab[:, :, :]))
            link(tt(z_tab[:, :, :], z_tab[:, :, :], bcast(valid[:, :].unsqueeze(2), [P, NT, H]), ALU.mult))
            acc4 = acc[:, :, :].rearrange("p t (h d) -> p (t h) d", h=H)
            link(tt(acc4, acc4, bcast(z_tab[:, :, :].rearrange("p t h -> p (t h)").unsqueeze(2), [P, NT * H, DK]), ALU.mult))
            dve.sem_inc(S["att_done"], 1)

            dve.wait_ge(S["agg_ready"], 1)
            dve.wait_ge(S["ffn_const"], 2)
            dve.wait_ge(S["w_ffns"], 64)
            link(v.tensor_copy(iotae[:, :], topi[:, 0, :]))
            dve.sem_inc(S["y_used"], 2)
            dve.sem_inc(S["ffn_step"], 1)
            with dve.Fori(0, NT // 2) as i:
                ln = chain(dve, S["dve_ffl"], i, FFN)
                dve.wait_ge(S["res_ps"], i + 1)
                dve.wait_ge(S["fx_in"], 48 * i + 48)
                dve.wait_ge(S["x2_free"], i + 1)
                ln(tt(x2[:, :, :], ps_a[:, :, :], fx[:, :, :], ALU.add))
                dve.sem_inc(S["in_free"], 1)
                ln(tt(x2[:, :, :], x2[:, :, :], bcast(aba[:, :].unsqueeze(1), [P, 2, D]), ALU.add))
                for b in pairs:
                    ins = v.bn_stats(fst[:, b, :], x2[:, b, :])
                ln(ins, carry=True)
                v.bn_aggr(fmv[:, 0, :], fst[:, 0, :])
                v.bn_aggr(fmv[:, 1, :], fst[:, 1, :]).then_inc(S["var2"], 1)
                dve.wait_ge(S["std2"], i + 1)
                ln(v.reciprocal(frs[:, :, :], frs[:, :, :]))
                for b in pairs:
                    ins = ts(x3[:, b, :], x2[:, b, :], fmv[:, b, 0:1], frs[:, b, :], ALU.subtract, ALU.mult)
                ins.then_inc(S["x3_ready"], 1)
                dve.wait_ge(S["gate_ps"], i + 1)
                ln(tt(lg[:, :, :], ps_b[:, 64:64 + 2 * NE].rearrange("p (b e) -> p b e", b=2),
                      bcast(bgb[:, :].unsqueeze(1), [P, 2, NE]), ALU.add), carry=True)
                for b in pairs:
                    ins = v.max(top[:, b, :], lg[:, b, :])
                ln(ins, carry=True)
                for b in pairs:
                    v.max_index(topi[:, b, :], top[:, b, :], lg[:, b, :])
                tt(gw[:, :, 0:1], top[:, :, 1:2], top[:, :, 0:1], ALU.subtract).then_inc(S["gate_d"], 1)
                dve.wait_ge(S["gate_d"], i + 1)
                ln(v.tensor_copy(topf[:, :, :], topi[:, :, :]))
                dve.wait_ge(S["gate_e"], i + 1)
                ln(ts(gw[:, :, 2:3], gw[:, :, 1:2], 1.0, None, ALU.add))
                ln(v.reciprocal(gw[:, :, 3:4], gw[:, :, 2:3]))
                ln(tt(gw[:, :, 2:3], gw[:, :, 1:2], gw[:, :, 3:4], ALU.mult))
                for b in pairs:
                    ts(wd[:, b, :], iotae[:, :], topf[:, b, 0:1], gw[:, b, 3:4], ALU.is_equal, ALU.mult)
                    ins = ts(wd2[:, b, :], iotae[:, :], topf[:, b, 1:2], gw[:, b, 2:3], ALU.is_equal, ALU.mult)
                ln(ins)
                tt(wd[:, :, :], wd[:, :, :], wd2[:, :, :], ALU.add).then_inc(S["wd_ready"], 1)
                dve.wait_ge(S["wd_ready"], i + 1)
                for e in range(NE):
                    dve.wait_ge(S["y_ps"], 8 * i + e + 1)
                    for b in pairs:
                        ins = stt(x2[:, b, :], ps_y[:, e % 2, b, :], wd[:, b, e:e + 1], x2[:, b, :], ALU.mult, ALU.add)
                    ins.then_inc(S["y_used"], 1)
                    dve.wait_ge(S["y_used"], 8 * i + e + 3)
                dve.wait_ge(S["b2_ps"], i + 1)
                ln(tt(x2[:, :, :], x2[:, :, :], ps_a[:, :, :], ALU.add))
                dve.sem_inc(S["out_ready"], 1)
                dve.sem_inc(S["ffn_step"], 1)
                assert ln.n[0] == FFN, ln.n[0]


def kernel(**inputs):
    import numpy as np
    import concourse.bacc as bacc
    from concourse.bass_utils import run_bass_kernel_spmd as run

    nc = bacc.Bacc("TRN2", target_bir_lowering=False, num_devices=1)
    arrays = {k: np.ascontiguousarray(v) for k, v in inputs.items()}
    arrays["x"] = np.concatenate([arrays["x"], np.zeros((NP - N, D), arrays["x"].dtype)])
    arrays["src"] = np.concatenate([arrays["src"], np.zeros(FAST, arrays["src"].dtype)]).reshape(-1, 1)
    arrays["dst"] = np.concatenate([arrays["dst"], np.full(EROWS * P - E, 1 << 20, arrays["dst"].dtype)]).reshape(EROWS, P)
    for k in arrays:
        if "ln_" in k:
            arrays[k] = arrays[k].reshape(-1)
    arrays["L0_gnn_skip"] = arrays["L0_gnn_skip"].reshape(1)
    dram = {k: nc.dram_tensor(k, v.shape, mybir.dt.from_np(v.dtype), kind="ExternalInput").ap() for k, v in arrays.items()}
    out = nc.dram_tensor("out", (NP, D), F32, kind="ExternalOutput").ap()
    build(nc, dram, out)
    r = run(nc, [arrays], core_ids=[0])
    return r.results[0]["out"][:N]
```

```python
from contextlib import ExitStack

import concourse.bass as bass
from concourse import mybir

F32 = mybir.dt.float32
I32 = mybir.dt.int32
U32 = mybir.dt.uint32
ALU = mybir.AluOpType
ACT = mybir.ActivationFunctionType
X = mybir.AxisListType.X

P = 128
N = 6250
E = 200000
D = 256
H = 8
DK = D // H
HALVES = D // P
NT = 50
RT = -(-N // P)
NP = NT * P
SLOTS = 8
GROUPS = 8
FAST = SLOTS * GROUPS
UNROLL = 3
BLOCKS = 13
EROWS = BLOCKS * P
SCHED = 512
SKIP = 65536.0
PASSES = -(-RT * GROUPS // UNROLL)
NEG = -1.0e30
LN_EPS = 1e-5
NE = 8
HID = 1024
HC = HID // P
TOK = 2 * P
NB = 5
CAP = NP + TOK
LEAST = -(-2 * NP // TOK)
MOST = LEAST + NE
TABLE = 64
KINDS = GROUPS + 2
PW = FAST + 2
AT_BLOCK, AT_START, AT_SORT, AT_RETURN = 3, 7, 8, 20
PJ = 9
ATT = 30
SPL = 12
RTL = 18


def bcast(ap, dims):
    return ap.to_broadcast(dims)


def build(nc, a, out):
    kvd = nc.dram_tensor("kv_table", (NP, 2 * D), F32, kind="Internal").ap()
    xntd = nc.dram_tensor("xn_transposed", (NT, P, D), F32, kind="Internal").ap()
    aggd = nc.dram_tensor("aggregated", (NP, D), F32, kind="Internal").ap()
    rpd = nc.dram_tensor("row_pointers", ((NT + 1) * P, 1), I32, kind="Internal").ap()
    firstd = nc.dram_tensor("block_firsts", (BLOCKS, P), I32, kind="Internal").ap()
    sortd = nc.dram_tensor("sorted_nodes", (NP, PW), I32, kind="Internal").ap()
    qd = nc.dram_tensor("sorted_q", (NP, D), F32, kind="Internal").ap()
    x2d = nc.dram_tensor("residual", (NP, D), F32, kind="Internal").ap()
    xsd = nc.dram_tensor("routed_rows", (NE * CAP + TOK, D), F32, kind="Internal").ap()
    ysd = nc.dram_tensor("expert_rows", (MOST * TOK, D), F32, kind="Internal").ap()
    schedd = nc.dram_tensor("schedule", (SCHED, 1), I32, kind="Internal").ap()

    with ExitStack() as root:
        root.enter_context(nc.allow_non_contiguous_dma(reason="columns of a few thousand entries, once"))
        def sb(ctx, name, shape, dt=F32):
            return ctx.enter_context(nc.sbuf_tensor(name, shape, dt))

        def pb(ctx, name, shape, dt=F32):
            return ctx.enter_context(nc.psum_tensor(name, shape, dt))

        def sem(name):
            return root.enter_context(nc.semaphore(name))

        ident = sb(root, "ident", [P, P])
        ones = sb(root, "ones", [P, P])
        a_fold = sb(root, "a_fold", [P, HALVES, D])
        mix_w = sb(root, "mix_w", [P, HALVES, P])
        aba = sb(root, "aba", [P, D])
        small = sb(root, "small", [P, 16])
        alpha = small[:, 0:1]
        two_minus_alpha = small[:, 1:2]
        eps_ln = small[:, 2:3]
        zero_col = small[:, 3:4]
        below = sb(root, "below", [P, P])
        place_i = sb(root, "place_i", [P, NT + NB], I32)
        valid = sb(root, "valid", [P, NT])

        att = ExitStack()
        qtab = sb(att, "qtab", [P, NT, D])
        start_f = sb(att, "start_f", [P, NT])
        deg_f = sb(att, "deg_f", [P, NT])
        counts = sb(att, "counts", [1, 4], I32)
        over_n = sb(att, "over_n", [1, 2 * NT], I32)
        sched = sb(att, "sched", [1, SCHED], I32)
        idx_tab = sb(att, "idx_tab", [P, NT * FAST], I32)
        neg_tab = sb(att, "neg_tab", [P, NT * FAST])

        pro = ExitStack()
        wq = sb(pro, "wq", [P, HALVES, D])
        wkv = sb(pro, "wkv", [P, HALVES, 2 * D])
        bias = sb(pro, "bias", [P, 3 * D])
        kln_wc = sb(pro, "kln_wc", [P, HALVES])
        kln_bc = sb(pro, "kln_bc", [P, HALVES])
        vln_wb = sb(pro, "vln_wb", [P, D])
        vln_bb = sb(pro, "vln_bb", [P, D])
        head_mask = sb(pro, "head_mask", [P, P])

        pre = ExitStack()
        w_raw = sb(pre, "w_raw", [P, 4, HALVES, D])
        b_col = sb(pre, "b_col", [P, 4, HALVES])
        rel = sb(pre, "rel", [P, 2, HALVES, P])
        pri = sb(pre, "pri", [P, HALVES])
        qdiag = sb(pre, "qdiag", [P, HALVES, P])
        adiag = sb(pre, "adiag", [P, P])
        sup_i = sb(pre, "sup_i", [P, BLOCKS], I32)
        sup_f = sb(pre, "sup_f", [P, BLOCKS])
        is_sup = sb(pre, "is_sup", [P, NT, BLOCKS])
        sup_b = sb(pre, "sup_b", [P, NT])
        sup_bi = sb(pre, "sup_bi", [P, NT], I32)
        junk = sb(pre, "junk", [P, SCHED])
        node_i = sb(pre, "node_i", [P, NT], I32)
        node_f = sb(pre, "node_f", [P, NT])
        coarse = sb(pre, "coarse", [P, NT])
        counts_t = sb(pre, "counts_t", [P, KINDS * NT])
        block_f = sb(pre, "block_f", [P, NT])
        block_i = sb(pre, "block_i", [P, NT], I32)
        rows = sb(pre, "rows", [P, NT, P], I32)
        fine = sb(pre, "fine", [P, NT])
        start_i = sb(pre, "start_i", [P, NT + 1], I32)
        end_i = sb(pre, "end_i", [P, NT], I32)
        end_f = sb(pre, "end_f", [P, NT])
        slot_i = sb(pre, "slot_i", [P, FAST], I32)
        slot_f = sb(pre, "slot_f", [P, FAST])
        fpos_i = sb(pre, "fpos_i", [P, SCHED // P], I32)
        fpos = sb(pre, "fpos", [P, SCHED // P])
        window = sb(pre, "window", [P, NT, PW], I32)
        start_n = sb(pre, "start_n", [P, NT])
        deg_n = sb(pre, "deg_n", [P, NT])
        ngr = sb(pre, "ngr", [P, NT])
        ngr_i = sb(pre, "ngr_i", [P, 2, NT], I32)
        kind = sb(pre, "kind", [P, KINDS * NT])
        before = sb(pre, "before", [P, KINDS * NT])
        rank = sb(pre, "rank", [P, KINDS * NT])
        place_f = sb(pre, "place_f", [P, NT])
        upto = sb(pre, "upto", [NT, NT])
        tmax = sb(pre, "tmax", [NT, 1])
        tint = sb(pre, "tint", [NT, 2], I32)
        tng = sb(pre, "tng", [NT, 4])
        gend = sb(pre, "gend", [P, NT])
        grow = sb(pre, "grow", [P, NT])
        orow = sb(pre, "orow", [P, 2 * NT])
        sch_f = sb(pre, "sch_f", [P, SCHED // P, 4])
        sch_i = sb(pre, "sch_i", [P, SCHED // P, 1], I32)
        k3_i = sb(pre, "k3_i", [1, SCHED], I32)
        k3_f = sb(pre, "k3_f", [1, SCHED])
        cnt_f = sb(pre, "cnt_f", [1, 4])
        ps_small = pb(root, "ps_small", [P, 512])
        pre_ps = ExitStack()
        ps_w = pb(pre_ps, "ps_w", [P, 3, 512])
        pre_ps.close()

        prj = ExitStack()
        xt = sb(prj, "xt", [P, 2, D])
        st6 = sb(prj, "st6", [P, 2, 6])
        mv = sb(prj, "mv", [P, 2, 2])
        rstd = sb(prj, "rstd", [P, 2, 1])
        xn = sb(prj, "xn", [P, 2, D])
        hsum = sb(prj, "hsum", [P, 2, H])
        hss = sb(prj, "hss", [P, 2, H])
        hr = sb(prj, "hr", [P, 2, H])
        xc = sb(prj, "xc", [P, 2, D])
        sq = sb(prj, "sq", [P, 2, D])
        nh = sb(prj, "nh", [P, 2, D])
        xnt = sb(prj, "xnt", [P, 2, HALVES, P])
        kvst = sb(prj, "kvst", [P, 2, 2 * D])
        zeros = sb(prj, "zeros", [P, 512])
        s_col = sb(prj, "s_col", [P, HALVES])
        t_col = sb(prj, "t_col", [P, HALVES])
        mtmp = sb(prj, "mtmp", [P, 4, P])
        prj_ps = ExitStack()
        ps_t = pb(prj_ps, "ps_t", [P, 2, 512])
        ps_q = pb(prj_ps, "ps_q", [P, 2, 512])
        ps_kv = pb(prj_ps, "ps_kv", [P, 2, 512])
        ps_g = pb(prj_ps, "ps_g", [P, 512])
        prj_ps.close()
        prj.close()
        pre.close()
        pro.close()

        acc = sb(att, "acc", [P, NT, D])
        m_tab = sb(att, "m_tab", [P, NT, H])
        z_tab = sb(att, "z_tab", [P, NT, H])
        kv = [sb(att, f"kv{k}", [P, SLOTS, 2 * D]) for k in range(UNROLL)]
        idx = [sb(att, f"idx{k}", [P, SLOTS], I32) for k in range(UNROLL)]
        prod = sb(att, "prod", [P, SLOTS * D])
        wv = sb(att, "wv", [P, SLOTS * D])
        ex = [sb(att, f"ex{k}", [P, SLOTS * H]) for k in range(UNROLL)]
        hneg = [sb(att, f"hneg{k}", [P, H]) for k in range(UNROLL)]
        nmax = [sb(att, f"nmax{k}", [P, H]) for k in range(UNROLL)]
        corr = [sb(att, f"corr{k}", [P, H]) for k in range(UNROLL)]
        zsum = [sb(att, f"zsum{k}", [P, H]) for k in range(UNROLL)]
        o_pos = sb(att, "o_pos", [P, 2])
        o_posi = sb(att, "o_posi", [P, 1], I32)
        o_win = sb(att, "o_win", [P, SLOTS], I32)
        o_msk = sb(att, "o_msk", [P, 2, SLOTS])
        iota8 = sb(att, "iota8", [P, SLOTS])
        att_ps = ExitStack()
        ps_sum = [pb(att_ps, f"ps_sum{k}", [P, 512]) for k in range(UNROLL)]
        att_ps.close()
        att.close()

        w1 = sb(root, "w1", [P, NE, HALVES, HID])
        w2 = sb(root, "w2", [P, NE, HC, D])
        wg = sb(root, "wg", [P, HALVES, NE])
        b1 = sb(root, "b1", [P, NE * HC])
        b1r = sb(root, "b1r", [NE * HC, P])
        b2b = sb(root, "b2b", [P, NE, D])
        bgb = sb(root, "bgb", [P, NE])
        iota_i = sb(root, "iota_i", [P, NE], I32)
        iotae = sb(root, "iotae", [P, NE])
        region = sb(root, "region", [P, NE])
        zrows = sb(root, "zrows", [P, 2, D])
        aidx = sb(root, "aidx", [P, NB], I32)
        route_w = sb(root, "route_w", [P, NT, 2])
        rows_y = sb(root, "rows_y", [P, NT * 2])
        route_r = sb(root, "route_r", [P, NT, 2], I32)
        base = sb(root, "base", [P, NE])
        route_f = sb(root, "route_f", [P, 2, NT * 2])
        tf = sb(root, "tf", [P, 5, NE])
        ti = sb(root, "ti", [P, 4, NE], I32)
        fpos_ei = sb(root, "fpos_ei", [1, TABLE], I32)
        frow = sb(root, "frow", [1, 3, TABLE])
        trow = sb(root, "trow", [1, TABLE], I32)
        cidx = [sb(root, f"cidx{b}", [P, 2], I32) for b in range(2)]
        cy = [sb(root, f"cy{b}", [P, 2, D]) for b in range(2)]
        cx = [sb(root, f"cx{b}", [P, D]) for b in range(2)]
        rt = ExitStack()
        fx = sb(rt, "fx", [P, NB, D])
        fxnt = sb(rt, "fxnt", [P, NB, HALVES, P])
        fagg = sb(rt, "fagg", [P, NB, D])
        faggt = sb(rt, "faggt", [P, NB, HALVES, P])
        x2 = sb(rt, "x2", [P, NB, D])
        x3 = sb(rt, "x3", [P, NB, D])
        x3t = sb(rt, "x3t", [P, NB, HALVES, P])
        fst = sb(rt, "fst", [P, NB, 6])
        fmv = sb(rt, "fmv", [P, NB, 2])
        frs = sb(rt, "frs", [P, NB, 1])
        lg = sb(rt, "lg", [P, NB, NE])
        top = sb(rt, "top", [P, NB, 8])
        topi = sb(rt, "topi", [P, NB, 8], U32)
        topf = sb(rt, "topf", [P, NB, 8])
        gw = sb(rt, "gw", [P, NB, 4])
        pick = sb(rt, "pick", [P, 2, NB, NE])
        both = sb(rt, "both", [P, NB, NE])
        posn = sb(rt, "posn", [P, NB, NE])
        prow = sb(rt, "prow", [P, 2, NB, NE])
        rowf = sb(rt, "rowf", [P, 2, NB])
        rowi = sb(rt, "rowi", [P, 2, NB], I32)
        rt_ps = ExitStack()
        ps_r = pb(rt_ps, "ps_r", [P, NB + 1, D])
        ps_t2 = pb(rt_ps, "ps_t2", [P, NB + 1, D])
        ps_b = pb(rt_ps, "ps_b", [P, 512])
        rt_ps.close()
        rt.close()
        xp = ExitStack()
        xs = sb(xp, "xs", [P, 2, D])
        xst = sb(xp, "xst", [P, HALVES, TOK])
        hid = sb(xp, "hid", [P, HC, TOK])
        yst = sb(xp, "yst", [P, 2, D])
        xp_ps = ExitStack()
        ps_h = pb(xp_ps, "ps_h", [P, 4, 2, TOK])
        ps_y = pb(xp_ps, "ps_y", [P, 2, 512])
        ps_x = pb(xp_ps, "ps_x", [P, 2, D])
        xp_ps.close()
        xp.close()

        names = """sup_in first_out sup_ready sup_rows_in kind_used fold_done kind_ready kind_ps q_ready place_ready sort_out
            sort_in q_out q_in aidx_ready agg_in pool_const w_in small_in dve_pre dve_prj dve_att dve_pjl dve_attl dve_spt
            dve_spl dve_rtl dve_cbl c_free0 c_free1 cx_in0 cx_in1 cy_in0 cy_in1 cr0 cr1 out0 out1 dve_step act_pre pe_pre
            block_ready rows_in start_ready start_out end_in window_in sched_ready sched_out sched_in tables_ready
            pool_step pool_ready xnt_ready kvst_ready st_free xnt_out kv_out x2_free x_in0 x_in1 x_free var_ready
            std_ready xn_ready xt_ps hss_ready hstd_ready nh_ready proj_ps gram_ps mix_ready va_ready vb_ready half_summed
            summed o_idx o_winin o_kvidx o_gath o_sready o_pready o_vready o_sum att_done agg_out agg_ready left w_ffn
            w_ffns fx_in in_free agt_ps agt_sb res_ps var2 std2 x3_ready x3_ps x3_sb gate_ps gate_d gate_e both_ready
            rank_ps rows_ready scattered x2_ready x2_out route_done scat_free tab_ready zero_out xs_in xs_free xs_ps xs_sb
            h_ps h_sb y_ps y_used y_ready y_out y_free experts_done cidx_ready b1_ps b1_sb ffn_const""".split()
        S = {n: sem(n) for n in names}
        idx_ready = [sem(f"idx_ready{k}") for k in range(UNROLL)]
        gathered = [sem(f"gathered{k}") for k in range(UNROLL)]
        s_ready = [sem(f"s_ready{k}") for k in range(UNROLL)]
        p_ready = [sem(f"p_ready{k}") for k in range(UNROLL)]

        def chain(eng, s, i=0, per=0, first=0):
            n = [0]

            def link(ins, carry=False):
                n[0] += 1
                ins.then_inc(s, 1)
                eng.wait_ge(s, i * per + first + n[0])
                if carry:
                    eng.sem_inc(S["dve_step"], 1)

            link.n = n
            return link

        src_rows = a["src"]
        dst_rows = a["dst"]
        block = root.enter_context(nc.Block())

        def gather(pool, dst_ap, table, idx_ap, bound, s):
            pool.indirect_dma_start(out=dst_ap, out_offset=None, in_=table,
                                    in_offset=bass.IndirectOffsetOnAxis(ap=idx_ap, axis=0),
                                    bounds_check=bound, oob_is_err=False).then_inc(s, 16)

        def scatter(pool, table, idx_ap, src_ap, bound, s):
            pool.indirect_dma_start(out=table, out_offset=bass.IndirectOffsetOnAxis(ap=idx_ap, axis=0),
                                    in_=src_ap, in_offset=None, bounds_check=bound, oob_is_err=False).then_inc(s, 16)

        def pool_wait(pool, s, value):
            pool.wait_ge(s, value)
            pool.sem_inc(S["pool_step"], 1)

        @block.sync
        def _(sp):
            sp.dma_start(sup_i[:, :], dst_rows.rearrange("(j q) c -> j q c", q=P)[:, 0, 0].partition_broadcast(P))\
                .then_inc(S["sup_in"], 16)
            sp.dma_start(firstd, dst_rows.rearrange("(j q) c -> j q c", q=P)[:, :, 0]).then_inc(S["first_out"], 16)
            for n, w in enumerate(("Wq", "Wk", "Wv", "Wa")):
                sp.dma_start(w_raw[:, n], a["L0_gnn_" + w].rearrange("(c p) n -> p c n", p=P)).then_inc(S["w_in"], 16)
            for n, b in enumerate(("bq", "bk", "bv")):
                sp.dma_start(b_col[:, n], a["L0_gnn_" + b].rearrange("(c p) -> p c", p=P)).then_inc(S["small_in"], 16)
            sp.dma_start(aba[:, :], a["L0_gnn_ba"].partition_broadcast(P)).then_inc(S["small_in"], 16)
            sp.wait_ge(S["pool_const"], 5)
            for n, r in enumerate(("rel_att", "rel_msg")):
                for h in range(H):
                    o = DK * (h % 4)
                    sp.dma_start(rel[o:o + DK, n, h // 4, o:o + DK], a["L0_gnn_" + r][h]).then_inc(S["small_in"], 16)
            for h in range(H):
                o = DK * (h % 4)
                sp.dma_start(pri[o:o + DK, h // 4:h // 4 + 1],
                             a["L0_gnn_rel_pri"][h:h + 1].partition_broadcast(DK)).then_inc(S["small_in"], 16)
            sp.dma_start(alpha, a["L0_gnn_skip"].partition_broadcast(P)).then_inc(S["small_in"], 16)
            for t, nme in ((kln_wc, "kln_weight"), (kln_bc, "kln_bias")):
                sp.dma_start(t[:, :], a["L0_mix_" + nme].rearrange("(c p) -> p c", p=P)).then_inc(S["small_in"], 16)
            for t, nme in ((vln_wb, "vln_weight"), (vln_bb, "vln_bias")):
                sp.dma_start(t[:, :], a["L0_mix_" + nme].partition_broadcast(P)).then_inc(S["small_in"], 16)
            def load_x(i):
                for b in range(2):
                    sp.dma_start(xt[:, b, :], a["x"][bass.ds((2 * i + b) * P, P), :]).then_inc(S[f"x_in{b}"], 16)

            def store_pair(i):
                for b in range(2):
                    sp.wait_ge(S["xnt_ready"], 2 * i + b + 1)
                    sp.dma_start(xntd[bass.ds(2 * i + b, 1)].rearrange("t p f -> p (t f)"),
                                 xnt[:, b].rearrange("p c f -> p (c f)")).then_inc(S["xnt_out"], 16)
                for b in range(2):
                    sp.wait_ge(S["kvst_ready"], 2 * i + b + 1)
                    sp.dma_start(kvd[bass.ds((2 * i + b) * P, P), :], kvst[:, b, :]).then_inc(S["kv_out"], 16)
                sp.wait_ge(S["xnt_out"], 32 * i + 32)
                sp.wait_ge(S["kv_out"], 32 * i + 32)
                sp.sem_inc(S["st_free"], 1)

            def move_pairs(lo, hi):
                with sp.Fori(lo, hi) as i:
                    sp.wait_ge(S["x_free"], i + 1)
                    load_x(i + 1)
                    store_pair(i)

            load_x(0)
            sp.sem_inc(S["st_free"], 1)
            move_pairs(0, AT_START)
            sp.wait_ge(S["start_ready"], 1)
            sp.dma_start(rpd.rearrange("(t p) o -> p (t o)", p=P), start_i[:, :]).then_inc(S["start_out"], 16)
            sp.wait_ge(S["start_out"], 16)
            sp.dma_start(end_i[:, :], rpd[1:NP + 1, :].rearrange("(t p) o -> p (t o)", p=P)).then_inc(S["end_in"], 16)
            move_pairs(AT_START, AT_RETURN)
            sp.wait_ge(S["sort_out"], 16 * NT)
            sp.dma_start(window[:, :, :], sortd.rearrange("(t p) w -> p t w", p=P)).then_inc(S["sort_in"], 16)
            move_pairs(AT_RETURN, NT // 2 - 1)
            store_pair(NT // 2 - 1)
            sp.wait_ge(S["sched_ready"], 1)
            sp.dma_start(schedd.rearrange("(c p) w -> p c w", p=P), sch_i[:, :, :]).then_inc(S["sched_out"], 16)
            sp.wait_ge(S["sched_out"], 16)
            sp.dma_start(sched[:, :], schedd.rearrange("(a f) w -> a (f w)", a=1)).then_inc(S["sched_in"], 16)
            sp.wait_ge(S["q_out"], 16 * NT)
            sp.dma_start(qtab[:, :, :], qd.rearrange("(t p) f -> p t f", p=P)).then_inc(S["q_in"], 16)
            sp.wait_ge(S["att_done"], 1)
            sp.dma_start(aggd.rearrange("(t p) f -> p t f", p=P), acc[:, :, :]).then_inc(S["agg_out"], 16)
            sp.wait_ge(S["agg_out"], 16)
            sp.wait_ge(S["left"], 3)
            sp.sem_inc(S["agg_ready"], 1)
            sp.dma_start(wg[:, :, :], a["L0_ffn_Wg"].rearrange("(c p) n -> p c n", p=P)).then_inc(S["w_ffns"], 16)
            sp.dma_start(b1r[:, :], a["L0_ffn_b1"].rearrange("e (c p) -> (e c) p", p=P)).then_inc(S["w_ffns"], 16)
            sp.dma_start(bgb[:, :], a["L0_ffn_bg"].partition_broadcast(P)).then_inc(S["w_ffns"], 16)
            sp.dma_start(b2b[:, :, :], a["L0_ffn_b2"].partition_broadcast(P)).then_inc(S["w_ffns"], 16)

            def load(i):
                sp.dma_start(fxnt[:, :, :, :], xntd[bass.ds(NB * i, NB)].rearrange("t p (c f) -> p t c f", c=HALVES))\
                    .then_inc(S["fx_in"], 16)
                sp.dma_start(fx[:, :, :], a["x"][bass.ds(NB * P * i, NB * P), :].rearrange("(t p) f -> p t f", p=P))\
                    .then_inc(S["fx_in"], 16)

            def store(i):
                sp.wait_ge(S["x2_ready"], i + 1)
                sp.dma_start(x2d[bass.ds(NB * P * i, NB * P), :].rearrange("(t p) f -> p t f", p=P), x2[:, :, :])\
                    .then_inc(S["x2_out"], 16)
                sp.wait_ge(S["x2_out"], 16 * i + 16)
                sp.sem_inc(S["x2_free"], 1)

            sp.sem_inc(S["x2_free"], 1)
            load(0)
            for e in range(NE):
                sp.dma_start(w1[:, e], a["L0_ffn_W1"][e].rearrange("(c p) n -> p c n", p=P)).then_inc(S["w_ffn"], 16)
                sp.dma_start(w2[:, e], a["L0_ffn_W2"][e].rearrange("(c p) n -> p c n", p=P)).then_inc(S["w_ffn"], 16)
            with sp.Fori(0, NT // NB - 1) as i:
                sp.wait_ge(S["in_free"], i + 1)
                load(i + 1)
                store(i)
            store(NT // NB - 1)
            sp.wait_ge(S["tab_ready"], 1)
            for e in range(NE):
                row = sp.value_load(ti[0:1, 2, e:e + 1], min_val=0, max_val=NE * CAP)
                sp.dma_start(xsd[bass.ds(row, TOK), :].rearrange("(b p) f -> p b f", p=P), zrows[:, :, :])\
                    .then_inc(S["zero_out"], 16)
            for t in range(LEAST, MOST):
                sp.dma_start(ysd[t * TOK:(t + 1) * TOK, :].rearrange("(b p) f -> p b f", p=P), zrows[:, :, :])\
                    .then_inc(S["zero_out"], 16)
            sp.wait_ge(S["zero_out"], 16 * (NE + MOST - LEAST))
            sp.wait_ge(S["route_done"], 3)

            def tile_row(f):
                return sp.value_load(trow[0:1, bass.ds(f, 1)], min_val=0, max_val=NE * CAP - TOK)

            def load_rows(f):
                sp.wait_ge(S["xs_free"], f + 1)
                sp.dma_start(xs[:, :, :], xsd[bass.ds(tile_row(f), TOK), :].rearrange("(b p) f -> p b f", p=P))\
                    .then_inc(S["xs_in"], 16)

            tiles = sp.value_load(ti[0:1, 3, 0:1], min_val=NE, max_val=MOST)
            sp.sem_inc(S["y_free"], 1)
            load_rows(0)
            with sp.Fori(0, tiles) as f:
                load_rows(f + 1)
                sp.wait_ge(S["y_ready"], f + 1)
                sp.dma_start(ysd[bass.ds(f * TOK, TOK), :].rearrange("(b p) f -> p b f", p=P), yst[:, :, :])\
                    .then_inc(S["y_out"], 16)
                sp.wait_ge(S["y_out"], 16 * f + 16)
                sp.sem_inc(S["y_free"], 1)
            sp.sem_inc(S["experts_done"], 1)
            with sp.Fori(0, NT // 2) as i:
                for b in range(2):
                    sp.wait_ge(S[f"c_free{b}"], i + 1)
                    sp.dma_start(cx[b][:, :], x2d[bass.ds((2 * i + b) * P, P), :]).then_inc(S[f"cx_in{b}"], 16)
            sp.wait_ge(S["out0"], 16 * (NT // 2))
            sp.wait_ge(S["out1"], 16 * (NT // 2))

        @block.gpsimd
        def _(pool):
            g = nc.gpsimd
            g.memset(ident[:, :], 0.0).then_inc(S["pool_const"], 1)
            g.memset(ones[:, :], 1.0).then_inc(S["pool_const"], 1)
            g.memset(rel[:, :, :, :], 0.0).then_inc(S["pool_const"], 1)
            g.iota(node_i[:, :], [[P, NT]], base=0, channel_multiplier=1).then_inc(S["pool_const"], 1)
            g.iota(slot_i[:, :], [[1, FAST]], base=0, channel_multiplier=0).then_inc(S["pool_const"], 1)
            g.iota(fpos_i[:, :], [[P, SCHED // P]], base=0, channel_multiplier=1).then_inc(S["pool_const"], 1)
            g.iota(k3_i[:, :], [[UNROLL, SCHED]], base=0, channel_multiplier=0).then_inc(S["pool_const"], 1)
            g.memset(upto[:, :], 1.0).then_inc(S["pool_const"], 1)
            g.memset(head_mask[:, :], 1.0).then_inc(S["pool_const"], 1)
            g.memset(start_i[:, NT:NT + 1], E).then_inc(S["pool_const"], 1)
            g.memset(below[:, :], 1.0).then_inc(S["pool_const"], 1)
            pool.wait_ge(S["pool_const"], 11)
            g.affine_select(out=ident[:, :], in_=ident[:, :], compare_op=ALU.not_equal, fill=1.0, base=0,
                            pattern=[[-1, P]], channel_multiplier=1).then_inc(S["pool_const"], 1)
            g.affine_select(out=upto[:, :], in_=upto[:, :], compare_op=ALU.is_ge, fill=0.0, base=0,
                            pattern=[[1, NT]], channel_multiplier=-1).then_inc(S["pool_const"], 1)
            g.affine_select(out=below[:, :], in_=below[:, :], compare_op=ALU.is_ge, fill=0.0, base=-1,
                            pattern=[[1, P]], channel_multiplier=-1).then_inc(S["pool_const"], 1)
            hm = head_mask[:, :].rearrange("p (h d) -> p h d", h=4)
            g.affine_select(out=hm, in_=hm, compare_op=ALU.is_ge, fill=0.0, base=0,
                            pattern=[[-DK, 4], [0, DK]], channel_multiplier=1).then_inc(S["pool_const"], 1)
            pool.wait_ge(S["pool_const"], 15)
            g.affine_select(out=hm, in_=hm, compare_op=ALU.is_ge, fill=0.0, base=DK - 1,
                            pattern=[[DK, 4], [0, DK]], channel_multiplier=-1).then_inc(S["pool_const"], 1)
            pool.wait_ge(S["first_out"], 16)
            pool.wait_ge(S["sup_ready"], 1)
            for t in range(NT):
                gather(pool, rows[:, t, :], firstd, sup_bi[:, t:t + 1], BLOCKS - 1, S["sup_rows_in"])
            pool.wait_ge(S["block_ready"], 1)
            for t in range(NT):
                gather(pool, rows[:, t, :], dst_rows, block_i[:, t:t + 1], EROWS - 1, S["rows_in"])
            pool.wait_ge(S["start_ready"], 1)
            for t in range(NT):
                gather(pool, window[:, t, 0:FAST], src_rows, start_i[:, t:t + 1], E, S["window_in"])
            pool.wait_ge(S["place_ready"], 1)
            pool.wait_ge(S["window_in"], 16 * NT)
            for t in range(NT):
                scatter(pool, sortd, place_i[:, t:t + 1], window[:, t, :], NP - 1, S["sort_out"])
            for t in range(NT):
                pool.wait_ge(S["q_ready"], t + 1)
                scatter(pool, qd, place_i[:, t:t + 1], qtab[:, t, :], NP - 1, S["q_out"])
            pool.wait_ge(S["mix_ready"], 1)
            for k in range(UNROLL):
                g.memset(kv[k][:, :, :], 0.0).then_inc(S["pool_ready"], 1)
            for s in range(SLOTS):
                g.memset(iota8[:, s:s + 1], float(s)).then_inc(S["pool_ready"], 1)
            pool.wait_ge(S["pool_ready"], UNROLL + SLOTS)
            pool.wait_ge(S["tables_ready"], 1)
            passes = pool.value_load(counts[0:1, 0:1], min_val=1, max_val=PASSES)
            with pool.Fori(0, passes) as i:
                for k in range(UNROLL):
                    pool_wait(pool, idx_ready[k], i + 1)
                    pool_wait(pool, S["vb_ready"], UNROLL * i + k + 1)
                    for s in range(SLOTS):
                        gather(pool, kv[k][:, s, :], kvd, idx[k][:, s:s + 1], N - 1, gathered[k])
            flag = pool.value_load(counts[0:1, 1:2], min_val=0, max_val=1)
            with pool.If(flag > 0):
                with pool.Fori(0, NT) as t:
                    n = pool.value_load(over_n[0:1, bass.ds(t, 1)], min_val=1, max_val=E // SLOTS + 1)
                    n0 = pool.value_load(over_n[0:1, bass.ds(t + NT, 1)], min_val=0, max_val=E // SLOTS + NT)
                    with pool.Fori(0, n) as i:
                        pool_wait(pool, S["o_idx"], n0 + i + 1)
                        gather(pool, o_win[:, :], src_rows, o_posi[:, 0:1], E, S["o_winin"])
                        pool_wait(pool, S["o_kvidx"], n0 + i + 1)
                        for s in range(SLOTS):
                            gather(pool, kv[0][:, s, :], kvd, idx[0][:, s:s + 1], N - 1, S["o_gath"])
            pool.sem_inc(S["left"], 1)
            pool.wait_ge(S["agg_ready"], 1)
            g.iota(iota_i[:, :], [[1, NE]], base=0, channel_multiplier=0).then_inc(S["ffn_const"], 1)
            g.iota(fpos_ei[:, :], [[1, TABLE]], base=0, channel_multiplier=0).then_inc(S["ffn_const"], 1)
            g.memset(zrows[:, :, :], 0.0).then_inc(S["ffn_const"], 1)
            pool.sem_inc(S["scat_free"], 1)
            def fetch_agg():
                for b in range(NB):
                    gather(pool, fagg[:, b, :], aggd, aidx[:, b:b + 1], NP - 1, S["agg_in"])

            pool.wait_ge(S["aidx_ready"], 1)
            fetch_agg()
            with pool.Fori(0, NT // NB) as i:
                pool_wait(pool, S["aidx_ready"], i + 2)
                fetch_agg()
                pool_wait(pool, S["rows_ready"], i + 1)
                for b in range(NB):
                    for j in range(2):
                        scatter(pool, xsd, rowi[:, j, b:b + 1], x3[:, b, :], NE * CAP - 1, S["scattered"])
                pool_wait(pool, S["scattered"], 32 * NB * i + 32 * NB)
                pool.sem_inc(S["scat_free"], 1)
            pool.wait_ge(S["agg_in"], 16 * NB * (NT // NB + 1))
            pool.sem_inc(S["route_done"], 1)
            pool.wait_ge(S["experts_done"], 1)
            with pool.Fori(0, NT // 2) as i:
                for b in range(2):
                    pool_wait(pool, S["cidx_ready"], 2 * i + b + 1)
                    for j in range(2):
                        gather(pool, cy[b][:, j, :], ysd, cidx[b][:, j:j + 1], MOST * TOK - 1, S[f"cy_in{b}"])

        @block.tensor
        def _(pe):
            mm = nc.tensor.matmul
            pe.wait_ge(S["w_in"], 64)
            pe.wait_ge(S["small_in"], 16 * 33)
            pe.wait_ge(S["dve_pre"], 1)
            for half in range(HALVES):
                cin = slice(half * P, (half + 1) * P)
                for hc in range(HALVES):
                    for n in range(3):
                        r = qdiag[:, hc] if n == 0 else rel[:, n - 1, hc]
                        ins = mm(ps_w[:, n, half * D + hc * P:half * D + (hc + 1) * P], w_raw[:, n, hc, cin], r,
                                 start=True, stop=True)
            ins.then_inc(S["pe_pre"], 1)
            for half in range(HALVES):
                cin = slice(half * P, (half + 1) * P)
                for hc in range(HALVES):
                    ins = mm(ps_small[:, half * D + hc * P:half * D + (hc + 1) * P], w_raw[:, 3, hc, cin], adiag[:, :],
                             start=True, stop=True)
            ins.then_inc(S["pe_pre"], 1)
            pe.wait_ge(S["dve_pre"], 2)
            for n in range(3):
                for hc in range(HALVES):
                    r = qdiag[:, hc] if n == 0 else rel[:, n - 1, hc]
                    ins = mm(ps_w[:, n, hc * P:(hc + 1) * P], bcast(b_col[:, n, hc:hc + 1], [P, P]), r,
                             start=True, stop=True)
            ins.then_inc(S["pe_pre"], 1)
            pe.wait_ge(S["fold_done"], 1)
            mm(ps_g[:, :], zeros[:, 0:P], zeros[:, :], start=True, stop=False, skip_group_check=True).then_inc(S["gram_ps"], 1)

            def project(lo, hi):
                with pe.Fori(lo, hi) as i:
                    for b in range(2):
                        pe.wait_ge(S["xn_ready"], 2 * i + b + 1)
                        for c in range(HALVES):
                            ins = nc.tensor.transpose(ps_t[:, b, c * P:(c + 1) * P], xn[:, b, c * P:(c + 1) * P], ident[:, :])
                        ins.then_inc(S["xt_ps"], 1)
                    for b in range(2):
                        pe.wait_ge(S["xnt_ready"], 2 * i + b + 1)
                        for c in range(HALVES):
                            mm(ps_q[:, b, 0:D], xnt[:, b, c, :], wq[:, c, :], start=(c == 0), stop=(c == HALVES - 1))
                        for c in range(HALVES):
                            ins = mm(ps_kv[:, b, :], xnt[:, b, c, :], wkv[:, c, :], start=(c == 0), stop=(c == HALVES - 1))
                        ins.then_inc(S["proj_ps"], 1)
                    for b in range(2):
                        pe.wait_ge(S["nh_ready"], 2 * i + b + 1)
                        for c in range(HALVES):
                            cs = slice(c * P, (c + 1) * P)
                            mm(ps_g[:, cs], nh[:, b, cs], nh[:, b, cs], start=False, stop=False, skip_group_check=True)
                        mm(ps_g[:, D:2 * D], ones[:, :], nh[:, b, :], start=False, stop=False,
                           skip_group_check=True).then_inc(S["gram_ps"], 1)

            project(0, AT_SORT)
            pe.wait_ge(S["kind_ready"], 1)
            mm(ps_small[:, 0:KINDS * NT], below[:, :], kind[:, :], start=True, stop=True).then_inc(S["kind_ps"], 1)
            pe.wait_ge(S["kind_used"], 1)
            mm(ps_small[:, 0:KINDS * NT], ones[:, :], kind[:, :], start=True, stop=True).then_inc(S["kind_ps"], 1)
            project(AT_SORT, NT // 2)
            pe.wait_ge(S["dve_pre"], 3)
            nc.tensor.transpose(ps_small[0:NT, 0:P], deg_f[:, :], ident[:, :]).then_inc(S["pe_pre"], 1)
            pe.wait_ge(S["dve_pre"], 4)
            mm(ps_small[:, 128:128 + NT], bcast(tng[:, 0:1], [NT, P]), upto[:, :], start=True, stop=True)
            mm(ps_small[:, 192:192 + NT], bcast(tng[:, 0:1], [NT, P]), ident[0:NT, 0:NT], start=True, stop=True)
            mm(ps_small[:, 256:256 + NT], bcast(tng[:, 1:2], [NT, P]), upto[:, :], start=True, stop=True)
            mm(ps_small[:, 320:320 + NT], bcast(tng[:, 1:2], [NT, P]), ident[0:NT, 0:NT], start=True, stop=True)
            mm(ps_small[:, 384:385], bcast(tng[:, 3:4], [NT, P]), ones[0:NT, 0:1], start=True, stop=True)\
                .then_inc(S["pe_pre"], 1)

            pe.wait_ge(S["tables_ready"], 1)
            for k in range(UNROLL):
                ins = mm(ps_sum[k][:, 0:D], ones[:, :], acc[:, 0, :], start=True, stop=True)
            ins.then_inc(S["summed"], 1)

            def add_slots(k, slots):
                for s in slots:
                    ins = mm(ps_sum[k][:, 0:D], ident[:, :], wv[:, s * D:(s + 1) * D], start=(s == 0), stop=(s == SLOTS - 1))
                return ins

            def add_group(k, n):
                pe.wait_ge(S["va_ready"], n + 1)
                add_slots(k, range(SLOTS // 2)).then_inc(S["half_summed"], 1)
                pe.wait_ge(S["vb_ready"], n + 3)
                add_slots(k, range(SLOTS // 2, SLOTS)).then_inc(S["summed"], 1)

            pe.sem_inc(S["half_summed"], 1)
            passes = pe.value_load(counts[0:1, 0:1], min_val=1, max_val=PASSES)
            with pe.Fori(0, passes) as i:
                for k in range(UNROLL):
                    add_group((k - 1) % UNROLL, UNROLL * i + k)
            add_group(UNROLL - 1, UNROLL * passes)
            flag = pe.value_load(counts[0:1, 1:2], min_val=0, max_val=1)
            with pe.If(flag > 0):
                with pe.Fori(0, NT) as t:
                    n = pe.value_load(over_n[0:1, bass.ds(t, 1)], min_val=1, max_val=E // SLOTS + 1)
                    n0 = pe.value_load(over_n[0:1, bass.ds(t + NT, 1)], min_val=0, max_val=E // SLOTS + NT)
                    with pe.Fori(0, n) as i:
                        pe.wait_ge(S["o_vready"], n0 + i + 1)
                        add_slots(0, range(SLOTS)).then_inc(S["o_sum"], 1)
            pe.sem_inc(S["left"], 1)
            pe.wait_ge(S["agg_ready"], 1)
            pe.wait_ge(S["w_ffns"], 64)
            nc.tensor.transpose(ps_b[:, 0:NE * HC], b1r[:, :], ident[0:NE * HC, 0:NE * HC]).then_inc(S["b1_ps"], 1)
            pe.wait_ge(S["b1_sb"], 1)
            with pe.Fori(0, NT // NB) as i:
                pe.wait_ge(S["agg_in"], 16 * NB * i + 16 * NB)
                for b in range(NB):
                    for c in range(HALVES):
                        ins = nc.tensor.transpose(ps_t2[:, b, c * P:(c + 1) * P], fagg[:, b, c * P:(c + 1) * P], ident[:, :])
                ins.then_inc(S["agt_ps"], 1)
                pe.wait_ge(S["agt_sb"], i + 1)
                pe.wait_ge(S["fx_in"], 32 * i + 32)
                for b in range(NB):
                    for c in range(HALVES):
                        mm(ps_r[:, b, :], faggt[:, b, c, :], a_fold[:, c, :], start=(c == 0), stop=False, skip_group_check=True)
                    for c in range(HALVES):
                        ins = mm(ps_r[:, b, c * P:(c + 1) * P], fxnt[:, b, c, :], mix_w[:, c, :], start=False,
                                 stop=(c == 1), skip_group_check=True)
                ins.then_inc(S["res_ps"], 1)
                pe.wait_ge(S["x3_ready"], i + 1)
                for b in range(NB):
                    for c in range(HALVES):
                        ins = nc.tensor.transpose(ps_t2[:, b, c * P:(c + 1) * P], x3[:, b, c * P:(c + 1) * P], ident[:, :])
                ins.then_inc(S["x3_ps"], 1)
                pe.wait_ge(S["x3_sb"], i + 1)
                for b in range(NB):
                    for c in range(HALVES):
                        ins = mm(ps_b[:, b * NE:(b + 1) * NE], x3t[:, b, c, :], wg[:, c, :],
                                 start=(c == 0), stop=(c == HALVES - 1), skip_group_check=True)
                ins.then_inc(S["gate_ps"], 1)
                pe.wait_ge(S["both_ready"], i + 1)
                sel = both[:, :, :].rearrange("p b e -> p (b e)")
                mm(ps_b[:, 64:64 + NB * NE], below[:, :], sel, start=True, stop=True)
                mm(ps_b[:, 128:128 + NB * NE], ones[:, :], sel, start=True, stop=True).then_inc(S["rank_ps"], 1)
            pe.sem_inc(S["route_done"], 1)
            pe.wait_ge(S["tab_ready"], 1)
            pe.wait_ge(S["w_ffn"], 16 * 2 * NE)
            pe.sem_inc(S["xs_free"], 1)

            def turn(f):
                pe.wait_ge(S["xs_in"], 16 * f + 16)
                for b in range(2):
                    for c in range(HALVES):
                        ins = nc.tensor.transpose(ps_x[:, c, b * P:(b + 1) * P], xs[:, b, c * P:(c + 1) * P], ident[:, :])
                ins.then_inc(S["xs_ps"], 1)

            turn(0)
            for e in range(NE):
                n = pe.value_load(ti[0:1, 0, e:e + 1], min_val=1, max_val=CAP // TOK)
                n0 = pe.value_load(ti[0:1, 1, e:e + 1], min_val=0, max_val=TABLE - 1)
                with pe.Fori(0, n) as i:
                    f = n0 + i
                    pe.wait_ge(S["xs_sb"], f + 1)
                    for q in range(HC // 2):
                        pe.wait_ge(S["h_sb"], 4 * f + q + 1)
                        for j in range(2):
                            c0 = (2 * q + j) * P
                            for c in range(HALVES):
                                ins = mm(ps_h[:, q, j, :], w1[:, e, c, c0:c0 + P], xst[:, c, :],
                                         start=(c == 0), stop=(c == HALVES - 1), skip_group_check=True)
                        ins.then_inc(S["h_ps"], 1)
                    turn(f + 1)
                    pe.wait_ge(S["h_sb"], 4 * f + 8)
                    for b in range(2):
                        pe.wait_ge(S["y_used"], 2 * f + b + 1)
                        for c in range(HC):
                            ins = mm(ps_y[:, b, 0:D], hid[:, c, b * P:(b + 1) * P], w2[:, e, c, :],
                                     start=(c == 0), stop=(c == HC - 1))
                        ins.then_inc(S["y_ps"], 1)

        @block.scalar
        def _(act):
            ac = nc.scalar.activation
            act.wait_ge(S["small_in"], 16 * 33)
            ac(alpha, alpha, ACT.Exp, scale=-1.0).then_inc(S["act_pre"], 1)
            act.wait_ge(S["fold_done"], 1)
            with act.Fori(0, NT // 2) as i:
                for b in range(2):
                    act.wait_ge(S["var_ready"], 2 * i + b + 1)
                    ac(rstd[:, b, :], mv[:, b, 1:2], ACT.Sqrt, bias=eps_ln).then_inc(S["std_ready"], 1)
                for b in range(2):
                    act.wait_ge(S["xt_ps"], 2 * i + b + 1)
                    act.wait_ge(S["st_free"], i + 1)
                    ac(xnt[:, b], ps_t[:, b, 0:D].rearrange("p (c f) -> p c f", c=HALVES), ACT.Copy).then_inc(S["xnt_ready"], 1)
                for b in range(2):
                    act.wait_ge(S["hss_ready"], 2 * i + b + 1)
                    ac(hss[:, b, :], hss[:, b, :], ACT.Sqrt, bias=zero_col, scale=1.0 / (DK - 1)).then_inc(S["hstd_ready"], 1)
            act.wait_ge(S["tables_ready"], 1)
            def exponentials(k, done):
                for h in range(H):
                    col = ex[k][:, h::H]
                    ac(col, col, ACT.Exp, bias=nmax[k][:, h:h + 1], accum_out=zsum[k][:, h:h + 1])
                ac(corr[k][:, :], corr[k][:, :], ACT.Exp).then_inc(done, 1)

            def stage(k, entry):
                place = act.value_load(sched[0:1, bass.ds(entry, 1)], min_val=0, max_val=NT * GROUPS - 1)
                nc.scalar.copy(idx[k][:, :], idx_tab[:, bass.ds(place * SLOTS, SLOTS)]).then_inc(idx_ready[k], 1)

            for k in range(UNROLL):
                stage(k, k + 2)
            passes = act.value_load(counts[0:1, 0:1], min_val=1, max_val=PASSES)
            act.sem_inc(p_ready[UNROLL - 1], 1)
            with act.Fori(0, passes) as i:
                for k in range(UNROLL):
                    act.wait_ge(gathered[k], 16 * SLOTS * i + 16 * SLOTS)
                    stage(k, UNROLL * i + UNROLL + 2 + k)
                    act.wait_ge(s_ready[k], i + 1)
                    exponentials(k, p_ready[k])
            flag = act.value_load(counts[0:1, 1:2], min_val=0, max_val=1)
            with act.If(flag > 0):
                with act.Fori(0, NT) as t:
                    n = act.value_load(over_n[0:1, bass.ds(t, 1)], min_val=1, max_val=E // SLOTS + 1)
                    n0 = act.value_load(over_n[0:1, bass.ds(t + NT, 1)], min_val=0, max_val=E // SLOTS + NT)
                    with act.Fori(0, n) as i:
                        act.wait_ge(S["o_sready"], n0 + i + 1)
                        exponentials(0, S["o_pready"])
            act.sem_inc(S["left"], 1)
            act.wait_ge(S["agg_ready"], 1)
            act.wait_ge(S["b1_ps"], 1)
            ac(b1[:, :], ps_b[:, 0:NE * HC], ACT.Copy).then_inc(S["b1_sb"], 1)
            nc.scalar.copy(aidx[:, :], place_i[:, 0:NB]).then_inc(S["aidx_ready"], 1)
            with act.Fori(0, NT // NB) as i:
                act.wait_ge(S["agt_ps"], i + 1)
                nc.scalar.copy(aidx[:, :], place_i[:, bass.ds(NB * i + NB, NB)]).then_inc(S["aidx_ready"], 1)
                ac(faggt[:, :, :, :], ps_t2[:, 0:NB, :].rearrange("p b (c f) -> p b c f", c=HALVES), ACT.Copy)\
                    .then_inc(S["agt_sb"], 1)
                act.wait_ge(S["var2"], i + 1)
                ac(frs[:, :, :], fmv[:, :, 1:2], ACT.Sqrt, bias=eps_ln).then_inc(S["std2"], 1)
                act.wait_ge(S["x3_ps"], i + 1)
                ac(x3t[:, :, :, :], ps_t2[:, 0:NB, :].rearrange("p b (c f) -> p b c f", c=HALVES), ACT.Copy)\
                    .then_inc(S["x3_sb"], 1)
                act.wait_ge(S["gate_d"], i + 1)
                ac(gw[:, :, 1:2], gw[:, :, 0:1], ACT.Exp).then_inc(S["gate_e"], 1)
            act.wait_ge(S["tab_ready"], 1)
            act.wait_ge(S["route_done"], 3)
            act.sem_inc(S["h_sb"], 4)

            def turned(f):
                act.wait_ge(S["xs_ps"], f + 1)
                ac(xst[:, :, :], ps_x[:, :, :], ACT.Copy).then_inc(S["xs_sb"], 1)

            turned(0)
            act.sem_inc(S["xs_free"], 1)
            for e in range(NE):
                n = act.value_load(ti[0:1, 0, e:e + 1], min_val=1, max_val=CAP // TOK)
                n0 = act.value_load(ti[0:1, 1, e:e + 1], min_val=0, max_val=TABLE - 1)
                with act.Fori(0, n) as i:
                    f = n0 + i
                    for q in range(HC // 2):
                        act.wait_ge(S["h_ps"], 4 * f + q + 1)
                        for j in range(2):
                            c = 2 * q + j
                            ins = ac(hid[:, c, :], ps_h[:, q, j, :], ACT.Gelu, bias=b1[:, e * HC + c:e * HC + c + 1])
                        ins.then_inc(S["h_sb"], 1)
                    turned(f + 1)
                    act.sem_inc(S["xs_free"], 1)
            with act.Fori(0, NT // 2) as i:
                for b in range(2):
                    act.wait_ge(S[f"cr{b}"], i + 1)
                    act.dma_start(out[bass.ds((2 * i + b) * P, P), :], cx[b][:, :]).then_inc(S[f"out{b}"], 16)
                for b in range(2):
                    act.wait_ge(S[f"out{b}"], 16 * i + 16)
                    act.sem_inc(S[f"c_free{b}"], 1)

        @block.vector
        def _(dve):
            v = nc.vector
            tt, ts, stt, red = v.tensor_tensor, v.tensor_scalar, v.scalar_tensor_tensor, v.tensor_reduce
            link = chain(dve, S["dve_prj"])
            dve.wait_ge(S["pool_const"], 16)
            link(v.memset(small[:, 2:4], 0.0))
            link(v.memset(eps_ln, LN_EPS))
            v.memset(zeros[:, :], 0.0)
            dve.wait_ge(S["sup_in"], 16)
            v.tensor_copy(node_f[:, :], node_i[:, :])
            link(v.tensor_copy(sup_f[:, :], sup_i[:, :]))
            link(tt(is_sup[:, :, :], bcast(sup_f[:, :].unsqueeze(1), [P, NT, BLOCKS]),
                    bcast(node_f[:, :].unsqueeze(2), [P, NT, BLOCKS]), ALU.is_lt))
            link(red(sup_b[:, :], is_sup[:, :, :], X, ALU.add))
            link(ts(sup_b[:, :], sup_b[:, :], -1.0, 0.0, ALU.add, ALU.max))
            v.tensor_copy(sup_bi[:, :], sup_b[:, :]).then_inc(S["sup_ready"], 1)
            dve.wait_ge(S["small_in"], 16 * 33)
            dve.wait_ge(S["act_pre"], 1)
            link(ts(alpha, alpha, 1.0, None, ALU.add))
            link(v.reciprocal(alpha, alpha))
            link(ts(two_minus_alpha, alpha, -1.0, 2.0, ALU.mult, ALU.add))
            link(ts(aba[:, :], aba[:, :], alpha, None, ALU.mult))
            link(ts(pri[:, :], pri[:, :], float(DK) ** -0.5, None, ALU.mult))
            for hc in range(HALVES):
                ts(qdiag[:, hc, :], ident[:, :], pri[:, hc:hc + 1], None, ALU.mult)
            ts(adiag[:, :], ident[:, :], alpha, None, ALU.mult).then_inc(S["dve_pre"], 1)
            dve.wait_ge(S["pe_pre"], 2)
            v.tensor_copy(wq[:, :, :], ps_w[:, 0, :].rearrange("p (c n) -> p c n", c=HALVES))
            v.tensor_copy(wkv[:, :, 0:D], ps_w[:, 1, :].rearrange("p (c n) -> p c n", c=HALVES))
            v.tensor_copy(wkv[:, :, D:2 * D], ps_w[:, 2, :].rearrange("p (c n) -> p c n", c=HALVES))
            v.tensor_copy(a_fold[:, :, :], ps_small[:, :].rearrange("p (c n) -> p c n", c=HALVES)).then_inc(S["dve_pre"], 1)
            dve.wait_ge(S["pe_pre"], 3)
            link(v.tensor_copy(bias[:, :].rearrange("p (a n) -> p a n", a=3), ps_w[:, :, 0:D]))
            dve.sem_inc(S["fold_done"], 1)

            pairs = range(2)

            def project(lo, hi):
                with dve.Fori(lo, hi) as i:
                    pl = chain(dve, S["dve_pjl"], i, PJ)
                    for b in pairs:
                        dve.wait_ge(S[f"x_in{b}"], 16 * i + 16)
                        ins = v.bn_stats(st6[:, b, :], xt[:, b, :])
                    pl(ins, carry=True)
                    for b in pairs:
                        v.bn_aggr(mv[:, b, :], st6[:, b, :]).then_inc(S["var_ready"], 1)
                    for b in pairs:
                        dve.wait_ge(S["std_ready"], 2 * i + b + 1)
                        pl(v.reciprocal(rstd[:, b, :], rstd[:, b, :]))
                        dve.wait_ge(S["var_ready"], 2 * i + b + 1)
                        ts(xn[:, b, :], xt[:, b, :], mv[:, b, 0:1], rstd[:, b, :], ALU.subtract, ALU.mult)\
                            .then_inc(S["xn_ready"], 1)
                    dve.wait_ge(S["xn_ready"], 2 * i + 2)
                    dve.sem_inc(S["x_free"], 1)
                    xn4 = xn[:, :, :].rearrange("p b (h d) -> p b h d", h=H)
                    for b in pairs:
                        ins = red(hsum[:, b, :], xn4[:, b], X, ALU.add)
                    pl(ins)
                    pl(ts(hsum[:, :, :], hsum[:, :, :], 1.0 / DK, None, ALU.mult))
                    for b in pairs:
                        ins = tt(xc[:, b, :].rearrange("p (h d) -> p h d", h=H), xn4[:, b],
                                 bcast(hsum[:, b, :].unsqueeze(2), [P, H, DK]), ALU.subtract)
                    pl(ins)
                    pl(tt(sq[:, :, :], xc[:, :, :], xc[:, :, :], ALU.mult))
                    for b in pairs:
                        red(hss[:, b, :], sq[:, b, :].rearrange("p (h d) -> p h d", h=H), X, ALU.add)\
                            .then_inc(S["hss_ready"], 1)
                    dve.wait_ge(S["hstd_ready"], 2 * i + 2)
                    pl(ts(hss[:, :, :], hss[:, :, :], LN_EPS, None, ALU.add))
                    pl(v.reciprocal(hr[:, :, :], hss[:, :, :]))
                    dve.wait_ge(S["gram_ps"], 2 * i + 1)
                    for b in pairs:
                        tt(nh[:, b, :].rearrange("p (h d) -> p h d", h=H), xc[:, b, :].rearrange("p (h d) -> p h d", h=H),
                           bcast(hr[:, b, :].unsqueeze(2), [P, H, DK]), ALU.mult).then_inc(S["nh_ready"], 1)
                    for b in pairs:
                        dve.wait_ge(S["proj_ps"], 2 * i + b + 1)
                        tt(qtab[:, bass.ds(2 * i + b, 1), :].rearrange("p a f -> p (a f)"), ps_q[:, b, 0:D], bias[:, 0:D], ALU.add)\
                            .then_inc(S["q_ready"], 1)
                        dve.wait_ge(S["st_free"], i + 1)
                        tt(kvst[:, b, :], ps_kv[:, b, :], bias[:, D:3 * D], ALU.add).then_inc(S["kvst_ready"], 1)
                    assert pl.n[0] == PJ, pl.n[0]

            def count_below(counted, first):
                with dve.Fori(0, NT) as t:
                    ts(junk[:, 0:P], rows[:, bass.ds(t, 1), :].rearrange("p a c -> p (a c)"), node_f[:, bass.ds(t, 1)], 0.0,
                       ALU.is_lt, ALU.add, accum_out=counted[:, bass.ds(t, 1)]).then_inc(S["dve_att"], 1)
                    dve.wait_ge(S["dve_att"], first + t + 1)

            project(0, AT_BLOCK)
            dve.wait_ge(S["sup_rows_in"], 16 * NT)
            count_below(coarse, 0)
            link(stt(block_f[:, :], sup_b[:, :], float(P), coarse[:, :], ALU.mult, ALU.add))
            link(ts(block_f[:, :], block_f[:, :], -1.0, 0.0, ALU.add, ALU.max))
            v.tensor_copy(block_i[:, :], block_f[:, :]).then_inc(S["block_ready"], 1)
            project(AT_BLOCK, AT_START)
            dve.wait_ge(S["rows_in"], 16 * NT)
            count_below(fine, NT)
            link(stt(start_n[:, :], block_f[:, :], float(P), fine[:, :], ALU.mult, ALU.add))
            v.tensor_copy(start_i[:, 0:NT], start_n[:, :]).then_inc(S["start_ready"], 1)
            v.tensor_copy(window[:, :, FAST:FAST + 1], start_n[:, :].unsqueeze(2))
            v.memset(place_i[:, NT:NT + NB], 0)
            v.memset(junk[:, 0:KINDS * NT], 1.0)
            project(AT_START, AT_SORT)
            dve.wait_ge(S["end_in"], 16)
            link(v.tensor_copy(end_f[:, :], end_i[:, :]))
            link(tt(deg_n[:, :], end_f[:, :], start_n[:, :], ALU.subtract))
            v.tensor_copy(window[:, :, FAST + 1:PW], deg_n[:, :].unsqueeze(2))
            link(ts(ngr_i[:, 0, :], deg_n[:, :], float(SLOTS - 1), None, ALU.add))
            link(ts(ngr_i[:, 1, :], ngr_i[:, 0, :], 3, None, ALU.logical_shift_right))
            link(v.tensor_copy(ngr[:, :], ngr_i[:, 1, :]))
            link(ts(ngr[:, :], ngr[:, :], float(KINDS - 1), None, ALU.min))
            for j in range(KINDS):
                ins = ts(kind[:, j * NT:(j + 1) * NT], ngr[:, :], float(KINDS - 1 - j), None, ALU.is_equal)
            ins.then_inc(S["kind_ready"], 1)
            dve.wait_ge(S["kind_ps"], 1)
            v.tensor_copy(rank[:, :], ps_small[:, 0:KINDS * NT]).then_inc(S["kind_used"], 1)
            dve.wait_ge(S["kind_ps"], 2)
            link(v.tensor_copy(counts_t[:, :], ps_small[:, 0:KINDS * NT]))
            link(v.tensor_tensor_scan(before[:, :], junk[:, 0:KINDS * NT], counts_t[:, :], 0.0, ALU.mult, ALU.add))
            link(tt(before[:, :], before[:, :], counts_t[:, :], ALU.subtract))
            link(tt(before[:, :], before[:, :], rank[:, :], ALU.add))
            link(tt(before[:, :], before[:, :], kind[:, :], ALU.mult))
            link(red(place_f[:, :], before[:, :].rearrange("p (j t) -> p t j", j=KINDS), X, ALU.add))
            v.tensor_copy(place_i[:, 0:NT], place_f[:, :]).then_inc(S["place_ready"], 1)
            project(AT_SORT, NT // 2)
            dve.wait_ge(S["sort_in"], 16)
            v.tensor_copy(start_f[:, :].unsqueeze(2), window[:, :, FAST:FAST + 1])
            link(v.tensor_copy(deg_f[:, :].unsqueeze(2), window[:, :, FAST + 1:PW]))
            ts(valid[:, :], deg_f[:, :], 0.5, None, ALU.is_gt).then_inc(S["dve_pre"], 1)
            dve.wait_ge(S["pe_pre"], 4)
            link(red(tmax[:, :], ps_small[0:NT, 0:P], X, ALU.max))
            link(ts(tint[:, 0:1], tmax[:, :], float(SLOTS - 1), None, ALU.add))
            link(ts(tint[:, 1:2], tint[:, 0:1], 3, None, ALU.logical_shift_right))
            link(v.tensor_copy(tng[:, 2:3], tint[:, 1:2]))
            link(ts(tng[:, 0:1], tng[:, 2:3], 1.0, float(GROUPS), ALU.max, ALU.min))
            link(ts(tng[:, 3:4], tng[:, 2:3], -float(GROUPS), 0.0, ALU.add, ALU.max))
            ts(tng[:, 1:2], tng[:, 3:4], 1.0, None, ALU.max).then_inc(S["dve_pre"], 1)
            dve.wait_ge(S["pe_pre"], 5)
            v.tensor_copy(gend[:, :], ps_small[:, 128:128 + NT])
            v.tensor_copy(grow[:, :], ps_small[:, 192:192 + NT])
            v.tensor_copy(orow[:, 0:NT], ps_small[:, 256:256 + NT])
            link(v.tensor_copy(orow[:, NT:2 * NT], ps_small[:, 320:320 + NT]))
            v.tensor_copy(over_n[:, 0:NT], orow[0:1, NT:2 * NT])
            link(tt(over_n[:, NT:2 * NT], orow[0:1, 0:NT], orow[0:1, NT:2 * NT], ALU.subtract))
            link(ts(fpos[:, :], fpos_i[:, :], -2.0, None, ALU.add))
            for c in range(SCHED // P):
                link(ts(junk[:, 0:RT], gend[:, 0:RT], fpos[:, c:c + 1], 0.0, ALU.is_le, ALU.add,
                        accum_out=sch_f[:, c, 0:1]))
                link(stt(junk[:, 0:RT], gend[:, 0:RT], fpos[:, c:c + 1], grow[:, 0:RT], ALU.is_le, ALU.mult,
                         accum_out=sch_f[:, c, 1:2]))
                link(tt(sch_f[:, c, 2:3], fpos[:, c:c + 1], sch_f[:, c, 1:2], ALU.subtract))
            link(ts(sch_f[:, :, 2], sch_f[:, :, 2], float(GROUPS - 1), 0.0, ALU.min, ALU.max))
            link(stt(sch_f[:, :, 3], sch_f[:, :, 0], float(GROUPS), sch_f[:, :, 2], ALU.mult, ALU.add))
            v.tensor_copy(sch_i[:, :, 0], sch_f[:, :, 3]).then_inc(S["sched_ready"], 1)
            link(v.tensor_copy(k3_f[:, :], k3_i[:, :]))
            link(ts(junk[0:1, 0:SCHED], k3_f[:, :], gend[0:1, RT - 1:RT], 0.0, ALU.is_lt, ALU.add, accum_out=cnt_f[:, 0:1]))
            link(ts(cnt_f[:, 1:2], ps_small[0:1, 384:385], 0.5, None, ALU.is_gt))
            link(v.tensor_copy(counts[:, 0:2], cnt_f[:, 0:2]))
            link(v.tensor_copy(slot_f[:, :], slot_i[:, :]))
            neg3 = neg_tab[:, :].rearrange("p (t s) -> p t s", t=NT)
            link(tt(neg3, bcast(slot_f[:, :].unsqueeze(1), [P, NT, FAST]), bcast(deg_f[:, :].unsqueeze(2), [P, NT, FAST]),
                    ALU.is_ge))
            link(stt(idx_tab[:, :].rearrange("p (t s) -> p t s", t=NT), neg3, SKIP, window[:, :, 0:FAST], ALU.mult, ALU.add))
            link(ts(neg_tab[:, :], neg_tab[:, :], NEG, None, ALU.mult))
            dve.wait_ge(S["sched_in"], 16)
            dve.wait_ge(S["gram_ps"], NT + 1)
            for c in range(HALVES):
                cs = slice(c * P, (c + 1) * P)
                sums = ps_g[:, D + c * P:D + (c + 1) * P]
                link(stt(mtmp[:, 0, :], sums, 1.0, ident[:, :], ALU.mult, ALU.mult, accum_out=s_col[:, c:c + 1]))
                link(tt(t_col[:, c:c + 1], kln_wc[:, c:c + 1], s_col[:, c:c + 1], ALU.mult))
                link(tt(mtmp[:, 0, :], ps_g[:, cs], vln_wb[:, cs], ALU.mult))
                link(ts(mtmp[:, 0, :], mtmp[:, 0, :], kln_wc[:, c:c + 1], None, ALU.mult))
                link(stt(mtmp[:, 1, :], vln_bb[:, cs], t_col[:, c:c + 1], mtmp[:, 0, :], ALU.mult, ALU.add))
                link(tt(mtmp[:, 2, :], sums, vln_wb[:, cs], ALU.mult))
                link(stt(mtmp[:, 3, :], vln_bb[:, cs], float(N), mtmp[:, 2, :], ALU.mult, ALU.add))
                link(stt(mtmp[:, 0, :], mtmp[:, 3, :], kln_bc[:, c:c + 1], mtmp[:, 1, :], ALU.mult, ALU.add))
                link(stt(mtmp[:, 1, :], mtmp[:, 0, :], 1.0 / N, head_mask[:, :], ALU.mult, ALU.mult))
                link(stt(mix_w[:, c, :], ident[:, :], two_minus_alpha, mtmp[:, 1, :], ALU.mult, ALU.add))
            dve.wait_ge(S["st_free"], NT // 2 + 1)
            dve.sem_inc(S["mix_ready"], 1)
            v.memset(m_tab[:, :, :], -NEG)
            v.memset(z_tab[:, :, :], 0.0)
            v.memset(o_win[:, :], 0)
            link(v.memset(acc[:, :, :], 0.0))
            dve.sem_inc(S["tables_ready"], 1)

            def column(tab, t, w):
                return tab[:, bass.ds(t, 1), :].rearrange("p a f -> p (a f)")

            def e3(k):
                return ex[k][:, :].rearrange("p (s h) -> p s h", s=SLOTS)

            def heads(ap):
                return ap.rearrange("p (h d) -> p h d", h=H)

            def times_q(k, t):
                return tt(prod[:, :].rearrange("p (s f) -> p s f", s=SLOTS), kv[k][:, :, 0:D],
                          bcast(qtab[:, bass.ds(t, 1), :], [P, SLOTS, D]), ALU.mult)

            def scores(k):
                return red(ex[k][:, :], prod[:, :].rearrange("p (a d) -> p a d", d=DK), X, ALU.add)

            def mask(k, neg):
                return tt(e3(k), e3(k), bcast(neg.unsqueeze(2), [P, SLOTS, H]), ALU.add)

            def minus_max(k):
                return red(hneg[k][:, :], e3(k).rearrange("p s h -> p h s"), X, ALU.max, negate=True)

            def running(k, t):
                return tt(nmax[k][:, :], hneg[k][:, :], column(m_tab, t, H), ALU.min)

            def rescale(k, t):
                return tt(corr[k][:, :], nmax[k][:, :], column(m_tab, t, H), ALU.subtract)

            def keep_max(k, t):
                return ts(column(m_tab, t, H), nmax[k][:, :], 1.0, None, ALU.mult)

            def weigh(k, part):
                sl = slice(part * SLOTS // 2, (part + 1) * SLOTS // 2)
                return tt(wv[:, :].rearrange("p (s h d) -> p s h d", s=SLOTS, h=H)[:, sl],
                          kv[k][:, sl, D:2 * D].rearrange("p s (h d) -> p s h d", h=H),
                          bcast(e3(k)[:, sl].unsqueeze(3), [P, SLOTS // 2, H, DK]), ALU.mult)

            def z_scale(k, t):
                return tt(column(z_tab, t, H), column(z_tab, t, H), corr[k][:, :], ALU.mult)

            def z_add(k, t):
                return tt(column(z_tab, t, H), column(z_tab, t, H), zsum[k][:, :], ALU.add)

            def acc_scale(k, t):
                o3 = heads(column(acc, t, D))
                return tt(o3, o3, bcast(corr[k][:, :].unsqueeze(2), [P, H, DK]), ALU.mult)

            def acc_add(k, t):
                return tt(column(acc, t, D), column(acc, t, D), ps_sum[k][:, 0:D], ALU.add)

            def group(entry):
                return dve.value_load(sched[0:1, bass.ds(entry, 1)], min_val=0, max_val=NT * GROUPS - 1)

            def tile_of(place):
                return place // GROUPS

            passes = dve.value_load(counts[0:1, 0:1], min_val=1, max_val=PASSES)
            for k in range(UNROLL):
                v.memset(corr[k][:, :], 0.0)
                v.memset(zsum[k][:, :], 0.0)
                link(v.memset(ex[k][:, :], 0.0))
            dve.wait_ge(S["q_in"], 16)
            dve.wait_ge(S["pool_ready"], UNROLL + SLOTS)
            dve.sem_inc(S["vb_ready"], 2)
            with dve.Fori(0, passes) as i:
                n = [0]

                def step(ins):
                    ins.then_inc(S["dve_attl"], 1)
                    n[0] += 1
                    return n[0]

                def after(m):
                    dve.wait_ge(S["dve_attl"], i * ATT + m)

                place = {0: group(UNROLL * i + 2)}
                for k in range(UNROLL):
                    k1, k2 = (k - 1) % UNROLL, (k - 2) % UNROLL
                    dve.wait_ge(gathered[k], 16 * SLOTS * i + 16 * SLOTS)
                    a_prod = step(times_q(k, tile_of(place[k])))
                    for j in ([-2, -1] if k == 0 else []) + ([k + 1] if k + 1 < UNROLL else []):
                        place[j] = group(UNROLL * i + 2 + j)
                    t, t1, t2 = (tile_of(place[k - j]) for j in range(3))
                    after(a_prod)
                    a_red = step(scores(k))
                    dve.wait_ge(p_ready[k1], i + 1)
                    dve.wait_ge(S["half_summed"], UNROLL * i + k + 1)
                    weigh(k1, 0).then_inc(S["va_ready"], 1)
                    after(a_red)
                    a_mask = step(mask(k, neg_tab[:, bass.ds(place[k] * SLOTS, SLOTS)]))
                    dve.wait_ge(S["summed"], UNROLL * i + k + 1)
                    weigh(k1, 1).then_inc(S["vb_ready"], 1)
                    a_acc = step(acc_scale(k2, t2))
                    after(a_acc)
                    step(acc_add(k2, t2))
                    a_z = step(z_scale(k1, t1))
                    after(a_mask)
                    a_max = step(minus_max(k))
                    after(a_z)
                    step(z_add(k1, t1))
                    after(a_max)
                    a_min = step(running(k, t))
                    after(a_min)
                    a_corr = step(rescale(k, t))
                    after(a_corr)
                    keep_max(k, t).then_inc(s_ready[k], 1)
                assert n[0] == ATT, n[0]
            last = UNROLL * passes
            t2, t1 = tile_of(group(last)), tile_of(group(last + 1))
            k2, k1 = UNROLL - 2, UNROLL - 1
            dve.wait_ge(S["summed"], last + 1)
            link(acc_scale(k2, t2))
            link(acc_add(k2, t2))
            dve.wait_ge(p_ready[k1], passes + 1)
            weigh(k1, 0).then_inc(S["va_ready"], 1)
            weigh(k1, 1).then_inc(S["vb_ready"], 1)
            link(z_scale(k1, t1))
            link(z_add(k1, t1))
            dve.wait_ge(S["summed"], last + 2)
            link(acc_scale(k1, t1))
            link(acc_add(k1, t1))
            flag = dve.value_load(counts[0:1, 1:2], min_val=0, max_val=1)
            with dve.If(flag > 0):
                with dve.Fori(0, NT) as t:
                    n = dve.value_load(over_n[0:1, bass.ds(t, 1)], min_val=1, max_val=E // SLOTS + 1)
                    n0 = dve.value_load(over_n[0:1, bass.ds(t + NT, 1)], min_val=0, max_val=E // SLOTS + NT)
                    lt = chain(dve, S["dve_spt"], t, 2)
                    lt(ts(o_pos[:, 0:1], start_f[:, bass.ds(t, 1)], float(FAST), None, ALU.add))
                    lt(ts(o_pos[:, 1:2], deg_f[:, bass.ds(t, 1)], -float(FAST), None, ALU.add), carry=True)
                    with dve.Fori(0, n) as i:
                        ln = chain(dve, S["dve_spl"], n0 + i, SPL)
                        v.tensor_copy(o_posi[:, :], o_pos[:, 0:1]).then_inc(S["o_idx"], 1)
                        ln(ts(o_msk[:, 0, :], iota8[:, :], o_pos[:, 1:2], None, ALU.is_ge))
                        ts(o_msk[:, 1, :], o_msk[:, 0, :], NEG, None, ALU.mult)
                        dve.wait_ge(S["o_winin"], 16 * (n0 + i) + 16)
                        stt(idx[0][:, :], o_msk[:, 0, :], SKIP, o_win[:, :], ALU.mult, ALU.add).then_inc(S["o_kvidx"], 1)
                        ts(o_pos[:, 0:1], o_pos[:, 0:1], float(SLOTS), None, ALU.add)
                        ln(ts(o_pos[:, 1:2], o_pos[:, 1:2], -float(SLOTS), None, ALU.add))
                        dve.wait_ge(S["o_gath"], 16 * SLOTS * (n0 + i) + 16 * SLOTS)
                        ln(times_q(0, t))
                        ln(scores(0))
                        ln(mask(0, o_msk[:, 1, :]))
                        ln(minus_max(0))
                        ln(running(0, t))
                        ln(rescale(0, t))
                        keep_max(0, t).then_inc(S["o_sready"], 1)
                        dve.wait_ge(S["o_pready"], n0 + i + 1)
                        weigh(0, 0)
                        weigh(0, 1).then_inc(S["o_vready"], 1)
                        ln(z_scale(0, t))
                        ln(z_add(0, t))
                        dve.wait_ge(S["o_sum"], n0 + i + 1)
                        ln(acc_scale(0, t))
                        ln(acc_add(0, t))
                        assert ln.n[0] == SPL, ln.n[0]
            link(ts(z_tab[:, :, :], z_tab[:, :, :], 0.5, None, ALU.max))
            link(v.reciprocal(z_tab[:, :, :], z_tab[:, :, :]))
            link(tt(z_tab[:, :, :], z_tab[:, :, :], bcast(valid[:, :].unsqueeze(2), [P, NT, H]), ALU.mult))
            acc4 = acc[:, :, :].rearrange("p t (h d) -> p (t h) d", h=H)
            link(tt(acc4, acc4, bcast(z_tab[:, :, :].rearrange("p t h -> p (t h)").unsqueeze(2), [P, NT * H, DK]), ALU.mult))
            dve.sem_inc(S["att_done"], 1)

            dve.wait_ge(S["agg_ready"], 1)
            dve.wait_ge(S["ffn_const"], 3)
            dve.wait_ge(S["w_ffns"], 64)
            link(v.tensor_copy(iotae[:, :], iota_i[:, :]))
            link(ts(region[:, :], iotae[:, :], float(CAP), None, ALU.mult))
            link(v.memset(base[:, :], 0.0))
            tiles_b = range(NB)
            with dve.Fori(0, NT // NB) as i:
                ln = chain(dve, S["dve_rtl"], i, RTL)
                dve.wait_ge(S["res_ps"], i + 1)
                dve.wait_ge(S["fx_in"], 32 * i + 32)
                dve.wait_ge(S["x2_free"], i + 1)
                ln(tt(x2[:, :, :], ps_r[:, 0:NB, :], fx[:, :, :], ALU.add))
                dve.sem_inc(S["in_free"], 1)
                ln(tt(x2[:, :, :], x2[:, :, :], bcast(aba[:, :].unsqueeze(1), [P, NB, D]), ALU.add))
                dve.sem_inc(S["x2_ready"], 1)
                for b in tiles_b:
                    ins = v.bn_stats(fst[:, b, :], x2[:, b, :])
                ln(ins, carry=True)
                for b in tiles_b:
                    ins = v.bn_aggr(fmv[:, b, :], fst[:, b, :])
                ins.then_inc(S["var2"], 1)
                dve.wait_ge(S["std2"], i + 1)
                ln(v.reciprocal(frs[:, :, :], frs[:, :, :]))
                dve.wait_ge(S["scat_free"], i + 1)
                for b in tiles_b:
                    ins = ts(x3[:, b, :], x2[:, b, :], fmv[:, b, 0:1], frs[:, b, :], ALU.subtract, ALU.mult)
                ins.then_inc(S["x3_ready"], 1)
                dve.wait_ge(S["gate_ps"], i + 1)
                ln(tt(lg[:, :, :], ps_b[:, 0:NB * NE].rearrange("p (b e) -> p b e", b=NB),
                      bcast(bgb[:, :].unsqueeze(1), [P, NB, NE]), ALU.add), carry=True)
                for b in tiles_b:
                    ins = v.max(top[:, b, :], lg[:, b, :])
                ln(ins, carry=True)
                for b in tiles_b:
                    ins = v.max_index(topi[:, b, :], top[:, b, :], lg[:, b, :])
                tt(gw[:, :, 0:1], top[:, :, 1:2], top[:, :, 0:1], ALU.subtract).then_inc(S["gate_d"], 1)
                dve.wait_ge(S["gate_d"], i + 1)
                ln(v.tensor_copy(topf[:, :, :], topi[:, :, :]))
                for j in range(2):
                    ins = tt(pick[:, j], bcast(iotae[:, :].unsqueeze(1), [P, NB, NE]),
                             bcast(topf[:, :, j:j + 1], [P, NB, NE]), ALU.is_equal)
                ln(ins)
                tt(both[:, :, :], pick[:, 0], pick[:, 1], ALU.add).then_inc(S["both_ready"], 1)
                dve.wait_ge(S["gate_e"], i + 1)
                ln(ts(gw[:, :, 2:3], gw[:, :, 1:2], 1.0, None, ALU.add))
                ln(v.reciprocal(gw[:, :, 3:4], gw[:, :, 2:3]))
                v.tensor_copy(route_w[:, bass.ds(NB * i, NB), 0:1], gw[:, :, 3:4])
                tt(route_w[:, bass.ds(NB * i, NB), 1:2], gw[:, :, 1:2], gw[:, :, 3:4], ALU.mult)
                dve.wait_ge(S["rank_ps"], i + 1)
                for b in tiles_b:
                    tt(posn[:, b, :], ps_b[:, 64 + b * NE:64 + (b + 1) * NE], base[:, :], ALU.add)
                    ln(tt(base[:, :], ps_b[:, 128 + b * NE:128 + (b + 1) * NE], base[:, :], ALU.add))
                ln(tt(posn[:, :, :], posn[:, :, :], bcast(region[:, :].unsqueeze(1), [P, NB, NE]), ALU.add))
                for j in range(2):
                    ins = tt(prow[:, j], pick[:, j], posn[:, :, :], ALU.mult)
                ln(ins)
                ln(red(rowf[:, :, :], prow[:, :, :, :], X, ALU.add))
                v.tensor_copy(route_f[:, 0, bass.ds(2 * NB * i, 2 * NB)].rearrange("p (t j) -> p j t", j=2), rowf[:, :, :])
                v.tensor_copy(rowi[:, :, :], rowf[:, :, :]).then_inc(S["rows_ready"], 1)
                assert ln.n[0] == RTL, ln.n[0]
            cnt, tn, tend, gain, zr = (tf[:, j, :] for j in range(5))
            dve.wait_ge(S["rows_ready"], NT // NB)
            link(ts(cnt, base[:, :], float(TOK - 1), None, ALU.add))
            link(v.tensor_copy(ti[:, 0, :], cnt))
            link(ts(ti[:, 1, :], ti[:, 0, :], TOK.bit_length() - 1, None, ALU.logical_shift_right))
            link(v.tensor_copy(tn, ti[:, 1, :]))
            link(ts(tn, tn, 1.0, None, ALU.max))
            link(v.tensor_tensor_scan(tend, ones[:, 0:NE], tn, 0.0, ALU.mult, ALU.add))
            link(ts(gain, tn, -float(TOK), float(CAP), ALU.mult, ALU.add))
            link(tt(zr, region[:, :], base[:, :], ALU.add))
            v.tensor_copy(ti[:, 0, :], tn)
            v.tensor_copy(ti[:, 2, :], zr)
            v.tensor_copy(ti[:, 3, 0:1], tend[:, NE - 1:NE])
            link(tt(ti[:, 1, :], tend, tn, ALU.subtract))
            pos_f, row_f, add_f = (frow[0:1, j, :] for j in range(3))
            link(v.tensor_copy(pos_f, fpos_ei[:, :]))
            link(ts(row_f, pos_f, float(TOK), None, ALU.mult))
            for e in range(NE - 1):
                link(ts(add_f, pos_f, tend[0:1, e:e + 1], gain[0:1, e:e + 1], ALU.is_ge, ALU.mult))
                link(tt(row_f, row_f, add_f, ALU.add))
            link(ts(add_f, pos_f, tend[0:1, NE - 1:NE], None, ALU.is_lt))
            link(tt(row_f, row_f, add_f, ALU.mult))
            link(v.tensor_copy(trow[:, :], row_f))
            dve.sem_inc(S["route_done"], 1)
            dve.sem_inc(S["tab_ready"], 1)
            for e in range(NE - 1):
                link(ts(route_f[:, 1, :], route_f[:, 0, :], float(CAP * (e + 1)), gain[:, e:e + 1], ALU.is_ge, ALU.mult))
                if e == 0:
                    link(tt(rows_y[:, :], route_f[:, 0, :], route_f[:, 1, :], ALU.subtract))
                else:
                    link(tt(rows_y[:, :], rows_y[:, :], route_f[:, 1, :], ALU.subtract))
            link(v.tensor_copy(route_r[:, :, :].rearrange("p t j -> p (t j)"), rows_y[:, :]))

            dve.sem_inc(S["y_used"], 2)
            dve.wait_ge(S["route_done"], 3)
            for e in range(NE):
                n = dve.value_load(ti[0:1, 0, e:e + 1], min_val=1, max_val=CAP // TOK)
                n0 = dve.value_load(ti[0:1, 1, e:e + 1], min_val=0, max_val=TABLE - 1)
                with dve.Fori(0, n) as i:
                    f = n0 + i
                    dve.wait_ge(S["y_free"], f + 1)
                    for b in pairs:
                        dve.wait_ge(S["y_ps"], 2 * f + b + 1)
                        tt(yst[:, b, :], ps_y[:, b, 0:D], b2b[:, e, :], ALU.add).then_inc(S["y_used"], 1)
                    dve.wait_ge(S["y_used"], 2 * f + 4)
                    dve.sem_inc(S["y_ready"], 1)

            dve.wait_ge(S["experts_done"], 1)
            dve.sem_inc(S["c_free0"], 1)
            dve.sem_inc(S["c_free1"], 1)

            def combine(b, i):
                dve.wait_ge(S[f"cy_in{b}"], 32 * i + 32)
                dve.wait_ge(S[f"cx_in{b}"], 16 * i + 16)
                for j in range(2):
                    w = route_w[:, bass.ds(2 * i + b, 1), j:j + 1].rearrange("p a j -> p (a j)")
                    stt(cx[b][:, :], cy[b][:, j, :], w, cx[b][:, :], ALU.mult, ALU.add)\
                        .then_inc(S["dve_cbl" if j == 0 else f"cr{b}"], 1)
                    if j == 0:
                        dve.wait_ge(S["dve_cbl"], 2 * i + b + 1)
                dve.wait_ge(S[f"cr{b}"], i + 1)

            def next_rows(b, t):
                v.tensor_copy(cidx[b][:, :], route_r[:, bass.ds(t, 1), :].rearrange("p a j -> p (a j)"))\
                    .then_inc(S["cidx_ready"], 1)

            next_rows(0, 0)
            next_rows(1, 1)
            with dve.Fori(0, NT // 2 - 1) as i:
                for b in pairs:
                    combine(b, i)
                    next_rows(b, 2 * i + 2 + b)
            for b in pairs:
                combine(b, NT // 2 - 1)


def kernel(**inputs):
    import numpy as np
    import concourse.bacc as bacc
    from concourse.bass_utils import run_bass_kernel_spmd as run

    nc = bacc.Bacc("TRN2", target_bir_lowering=False, num_devices=1)
    arrays = {k: np.ascontiguousarray(v) for k, v in inputs.items()}
    arrays["x"] = np.concatenate([arrays["x"], np.zeros((NP - N, D), arrays["x"].dtype)])
    arrays["src"] = np.concatenate([arrays["src"], np.zeros(FAST, arrays["src"].dtype)]).reshape(-1, 1)
    arrays["dst"] = np.concatenate([arrays["dst"], np.full(EROWS * P - E, 1 << 20, arrays["dst"].dtype)]).reshape(EROWS, P)
    for k in arrays:
        if "ln_" in k:
            arrays[k] = arrays[k].reshape(-1)
    arrays["L0_gnn_skip"] = arrays["L0_gnn_skip"].reshape(1)
    dram = {k: nc.dram_tensor(k, v.shape, mybir.dt.from_np(v.dtype), kind="ExternalInput").ap() for k, v in arrays.items()}
    out = nc.dram_tensor("out", (NP, D), F32, kind="ExternalOutput").ap()
    build(nc, dram, out)
    r = run(nc, [arrays], core_ids=[0])
    return r.results[0]["out"][:N]
```

```python
from contextlib import ExitStack

import concourse.bass as bass
from concourse import mybir

F32 = mybir.dt.float32
I32 = mybir.dt.int32
U32 = mybir.dt.uint32
ALU = mybir.AluOpType
ACT = mybir.ActivationFunctionType
X = mybir.AxisListType.X

P = 128
N = 6250
E = 200000
D = 256
H = 8
DK = D // H
HALVES = D // P
NT = 50
RT = -(-N // P)
NP = NT * P
SLOTS = 8
GROUPS = 8
FAST = SLOTS * GROUPS
UNROLL = 4
BLOCKS = 13
EROWS = BLOCKS * P
SCHED = 512
SKIP = 65536.0
PASSES = -(-RT * GROUPS // UNROLL)
NEG = -1.0e30
MASK = 1.0e26
LN_EPS = 1e-5
NE = 8
HID = 1024
HC = HID // P
TOK = 2 * P
NB = 5
BANKS = ((0, 2), (2, 4), (4, 5))
NG = len(BANKS)
CAP = NP + TOK
LEAST = -(-2 * NP // TOK)
MOST = LEAST + NE
TABLE = 64
SW = D + H
TC = 10
EARLY = NE // 2
CB = 5
KINDS = GROUPS + 2
PW = FAST + 2
AT_BLOCK, AT_START, AT_SORT, AT_RETURN = 3, 8, 9, 18
PJ = 9
ATT = 7 * UNROLL
SPL = 9
RTL = 17


def bcast(ap, dims):
    return ap.to_broadcast(dims)


def build(nc, a, out):
    kvd = nc.dram_tensor("kv_table", (NP, 2 * D), F32, kind="Internal").ap()
    xntd = nc.dram_tensor("xn_transposed", (NT, P, D), F32, kind="Internal").ap()
    aggd = nc.dram_tensor("aggregated", (NP, D), F32, kind="Internal").ap()
    rpd = nc.dram_tensor("row_pointers", ((NT + 1) * P, 1), I32, kind="Internal").ap()
    firstd = nc.dram_tensor("block_firsts", (BLOCKS, P), I32, kind="Internal").ap()
    sortd = nc.dram_tensor("sorted_nodes", (NP, PW), I32, kind="Internal").ap()
    qd = nc.dram_tensor("sorted_q", (NP, D), F32, kind="Internal").ap()
    x2d = nc.dram_tensor("residual", (NP, D), F32, kind="Internal").ap()
    xsd = nc.dram_tensor("routed_rows", (NE * CAP + TOK, D), F32, kind="Internal").ap()
    ysd = nc.dram_tensor("expert_rows", (MOST * TOK, D), F32, kind="Internal").ap()
    schedd = nc.dram_tensor("schedule", (SCHED, 1), I32, kind="Internal").ap()

    with ExitStack() as root:
        root.enter_context(nc.allow_non_contiguous_dma(reason="columns of a few thousand entries, once"))
        def sb(ctx, name, shape, dt=F32):
            return ctx.enter_context(nc.sbuf_tensor(name, shape, dt))

        def pb(ctx, name, shape, dt=F32):
            return ctx.enter_context(nc.psum_tensor(name, shape, dt))

        def sem(name):
            return root.enter_context(nc.semaphore(name))

        ident = sb(root, "ident", [P, P])
        ones = sb(root, "ones", [P, P])
        a_fold = sb(root, "a_fold", [P, HALVES, D])
        mix_w = sb(root, "mix_w", [P, HALVES, P])
        aba = sb(root, "aba", [P, D])
        small = sb(root, "small", [P, 16])
        alpha = small[:, 0:1]
        two_minus_alpha = small[:, 1:2]
        eps_ln = small[:, 2:3]
        zero_col = small[:, 3:4]
        half_skip = small[:, 4:5]
        below = sb(root, "below", [P, P])
        place_i = sb(root, "place_i", [P, NT + 2 * NB], I32)
        valid = sb(root, "valid", [P, NT])

        att = ExitStack()
        qtab = sb(att, "qtab", [P, NT, D])
        start_f = sb(att, "start_f", [P, NT])
        deg_f = sb(att, "deg_f", [P, NT])
        counts = sb(att, "counts", [1, 4], I32)
        over_n = sb(att, "over_n", [1, 2 * NT], I32)
        sched = sb(att, "sched", [1, SCHED], I32)
        idx_tab = sb(att, "idx_tab", [P, NT * FAST], I32)

        pro = ExitStack()
        wq = sb(pro, "wq", [P, HALVES, D])
        wkv = sb(pro, "wkv", [P, HALVES, 2 * D])
        bias = sb(pro, "bias", [P, 3 * D])
        kln_wc = sb(pro, "kln_wc", [P, HALVES])
        kln_bc = sb(pro, "kln_bc", [P, HALVES])
        vln_wb = sb(pro, "vln_wb", [P, D])
        vln_bb = sb(pro, "vln_bb", [P, D])
        head_mask = sb(pro, "head_mask", [P, P])

        pre = ExitStack()
        w_raw = sb(pre, "w_raw", [P, 4, HALVES, D])
        b_col = sb(pre, "b_col", [P, 4, HALVES])
        rel = sb(pre, "rel", [P, 2, HALVES, P])
        pri = sb(pre, "pri", [P, HALVES])
        qdiag = sb(pre, "qdiag", [P, HALVES, P])
        adiag = sb(pre, "adiag", [P, P])
        sup_i = sb(pre, "sup_i", [P, BLOCKS], I32)
        sup_f = sb(pre, "sup_f", [P, BLOCKS])
        is_sup = sb(pre, "is_sup", [P, NT, BLOCKS])
        sup_b = sb(pre, "sup_b", [P, NT])
        sup_bi = sb(pre, "sup_bi", [P, NT], I32)
        junk = sb(pre, "junk", [P, SCHED])
        node_i = sb(pre, "node_i", [P, NT], I32)
        node_f = sb(pre, "node_f", [P, NT])
        coarse = sb(pre, "coarse", [P, NT])
        counts_t = sb(pre, "counts_t", [P, KINDS * NT])
        block_f = sb(pre, "block_f", [P, NT])
        block_i = sb(pre, "block_i", [P, NT], I32)
        rows = sb(pre, "rows", [P, NT, P], I32)
        fine = sb(pre, "fine", [P, NT])
        start_i = sb(pre, "start_i", [P, NT + 1], I32)
        end_i = sb(pre, "end_i", [P, NT], I32)
        end_f = sb(pre, "end_f", [P, NT])
        slot_i = sb(pre, "slot_i", [P, FAST], I32)
        slot_f = sb(pre, "slot_f", [P, FAST])
        fpos_i = sb(pre, "fpos_i", [P, SCHED // P], I32)
        fpos = sb(pre, "fpos", [P, SCHED // P])
        window = sb(pre, "window", [P, NT, PW], I32)
        start_n = sb(pre, "start_n", [P, NT])
        deg_n = sb(pre, "deg_n", [P, NT])
        ngr = sb(pre, "ngr", [P, NT])
        ngr_i = sb(pre, "ngr_i", [P, 2, NT], I32)
        kind = sb(pre, "kind", [P, KINDS * NT])
        before = sb(pre, "before", [P, KINDS * NT])
        rank = sb(pre, "rank", [P, KINDS * NT])
        place_f = sb(pre, "place_f", [P, NT])
        upto = sb(pre, "upto", [NT, NT])
        tmax = sb(pre, "tmax", [NT, 1])
        tint = sb(pre, "tint", [NT, 2], I32)
        tng = sb(pre, "tng", [NT, 4])
        gend = sb(pre, "gend", [P, NT])
        grow = sb(pre, "grow", [P, NT])
        orow = sb(pre, "orow", [P, 2 * NT])
        sch_f = sb(pre, "sch_f", [P, SCHED // P, 4])
        sch_i = sb(pre, "sch_i", [P, SCHED // P, 1], I32)
        k3_i = sb(pre, "k3_i", [1, SCHED], I32)
        k3_f = sb(pre, "k3_f", [1, SCHED])
        cnt_f = sb(pre, "cnt_f", [1, 4])
        ps_small = pb(root, "ps_small", [P, 512])
        pre_ps = ExitStack()
        ps_w = pb(pre_ps, "ps_w", [P, 3, 512])
        pre_ps.close()

        prj = ExitStack()
        xt = sb(prj, "xt", [P, 2, D])
        st6 = sb(prj, "st6", [P, 2, 6])
        mv = sb(prj, "mv", [P, 2, 2])
        rstd = sb(prj, "rstd", [P, 2, 1])
        xn = sb(prj, "xn", [P, 2, D])
        hsum = sb(prj, "hsum", [P, 2, H])
        hss = sb(prj, "hss", [P, 2, H])
        hr = sb(prj, "hr", [P, 2, H])
        xc = sb(prj, "xc", [P, 2, D])
        sq = sb(prj, "sq", [P, 2, D])
        nh = sb(prj, "nh", [P, 2, D])
        xnt = sb(prj, "xnt", [P, 2, HALVES, P])
        kvst = sb(prj, "kvst", [P, 2, 2 * D])
        neg_tab = sb(prj, "neg_tab", [P, NT * FAST])
        zeros = sb(prj, "zeros", [P, 512])
        s_col = sb(prj, "s_col", [P, HALVES])
        t_col = sb(prj, "t_col", [P, HALVES])
        mtmp = sb(prj, "mtmp", [P, 4, P])
        prj_ps = ExitStack()
        ps_t = pb(prj_ps, "ps_t", [P, 2, 512])
        ps_q = pb(prj_ps, "ps_q", [P, 2, 512])
        ps_kv = pb(prj_ps, "ps_kv", [P, 2, 512])
        ps_g = pb(prj_ps, "ps_g", [P, 512])
        prj_ps.close()
        prj.close()
        pre.close()
        pro.close()

        acc = sb(att, "acc", [P, NT, SW])
        m_tab = sb(att, "m_tab", [P, NT, H])
        kv = [sb(att, f"kv{k}", [P, SLOTS, 2 * D]) for k in range(UNROLL)]
        idx = [sb(att, f"idx{k}", [P, SLOTS], I32) for k in range(UNROLL)]
        prod = sb(att, "prod", [P, SLOTS * D])
        wv = sb(att, "wv", [P, SLOTS * D])
        msk = [sb(att, f"msk{k}", [P, SLOTS]) for k in range(UNROLL)]
        ex = [sb(att, f"ex{k}", [P, SLOTS * H]) for k in range(UNROLL)]
        hneg = [sb(att, f"hneg{k}", [P, H]) for k in range(UNROLL)]
        nmax = [sb(att, f"nmax{k}", [P, H]) for k in range(UNROLL)]
        corr = [sb(att, f"corr{k}", [P, H]) for k in range(UNROLL)]
        zsum = [sb(att, f"zsum{k}", [P, H]) for k in range(UNROLL)]
        o_pos = sb(att, "o_pos", [P, 2])
        o_posi = sb(att, "o_posi", [P, 1], I32)
        o_win = sb(att, "o_win", [P, SLOTS], I32)
        o_msk = sb(att, "o_msk", [P, 2, SLOTS])
        iota8 = sb(att, "iota8", [P, SLOTS])
        att_ps = ExitStack()
        ps_sum = [pb(att_ps, f"ps_sum{k}", [P, 512]) for k in range(UNROLL)]
        att_ps.close()
        att.close()

        w1 = sb(root, "w1", [P, NE, HALVES, HID])
        w2 = sb(root, "w2", [P, NE, HC, D])
        wg = sb(root, "wg", [P, HALVES, NE])
        b1 = sb(root, "b1", [P, NE * HC])
        b1r = sb(root, "b1r", [NE * HC, P])
        b2b = sb(root, "b2b", [P, NE, D])
        bgb = sb(root, "bgb", [P, NE])
        iota_i = sb(root, "iota_i", [P, NE], I32)
        iotae = sb(root, "iotae", [P, NE])
        region = sb(root, "region", [P, NE])
        zrows = sb(root, "zrows", [P, 2, D])
        aidx = sb(root, "aidx", [P, NB], I32)
        route_w = sb(root, "route_w", [P, NT, 2])
        rows_y = sb(root, "rows_y", [P, NT * 2])
        route_r = sb(root, "route_r", [P, NT, 2], I32)
        base = sb(root, "base", [P, NE])
        route_f = sb(root, "route_f", [P, 2, NT * 2])
        tf = sb(root, "tf", [P, 5, NE])
        ti = sb(root, "ti", [P, 4, NE], I32)
        fpos_ei = sb(root, "fpos_ei", [1, TABLE], I32)
        frow = sb(root, "frow", [1, 3, TABLE])
        trow = sb(root, "trow", [1, TABLE], I32)
        cidx = [sb(root, f"cidx{b}", [P, 2], I32) for b in range(CB)]
        cy = [sb(root, f"cy{b}", [P, 2, D]) for b in range(CB)]
        cx = [sb(root, f"cx{b}", [P, D]) for b in range(CB)]
        rt = ExitStack()
        fx = sb(rt, "fx", [P, NB, D])
        fxnt = sb(rt, "fxnt", [P, NB, HALVES, P])
        fagg = sb(rt, "fagg", [P, NB, D])
        faggt = sb(rt, "faggt", [P, NB, HALVES, P])
        x2 = sb(rt, "x2", [P, NB, D])
        x3 = sb(rt, "x3", [P, NB, D])
        x3t = sb(rt, "x3t", [P, NB, HALVES, P])
        fst = sb(rt, "fst", [P, NB, 6])
        fmv = sb(rt, "fmv", [P, NB, 2])
        frs = sb(rt, "frs", [P, NB, 1])
        lg = sb(rt, "lg", [P, NB, NE])
        top = sb(rt, "top", [P, NB, 8])
        topi = sb(rt, "topi", [P, NB, 8], U32)
        topf = sb(rt, "topf", [P, NB, 8])
        gw = sb(rt, "gw", [P, NB, 4])
        pick = sb(rt, "pick", [P, 2, NB, NE])
        both = sb(rt, "both", [P, NB, NE])
        posn = sb(rt, "posn", [P, NB, NE])
        prow = sb(rt, "prow", [P, 2, NB, NE])
        rowf = sb(rt, "rowf", [P, 2, NB])
        rowi = sb(rt, "rowi", [P, 2, NB], I32)
        rt_ps = ExitStack()
        ps_r = pb(rt_ps, "ps_r", [P, NB + 1, D])
        ps_t2 = pb(rt_ps, "ps_t2", [P, NB + 1, D])
        ps_b = pb(rt_ps, "ps_b", [P, 512])
        rt_ps.close()
        rt.close()
        xp = ExitStack()
        xs = sb(xp, "xs", [P, 2, D])
        xst = sb(xp, "xst", [P, HALVES, TOK])
        hid = sb(xp, "hid", [P, HC, TOK])
        yst = sb(xp, "yst", [P, 2, D])
        xp_ps = ExitStack()
        ps_h = pb(xp_ps, "ps_h", [P, 4, 2, TOK])
        ps_y = pb(xp_ps, "ps_y", [P, 2, 512])
        ps_x = pb(xp_ps, "ps_x", [P, 2, D])
        xp_ps.close()
        xp.close()

        names = """w_late kv_zeroed msk_ready c_free c_done cidx_ready sup_in first_out sup_ready sup_rows_in kind_used fold_done
            kind_ready kind_ps q_ready place_ready sort_out sort_in q_out q_in aidx_ready agg_in pool_const w_in small_in
            dve_pre dve_prj dve_pjl dve_attl dve_spt dve_spl dve_rtl dve_cbl dve_step act_pre pe_pre block_ready rows_in
            start_ready start_out end_in window_in sched_ready sched_out sched_in tables_ready pool_step pool_ready
            xnt_ready kvst_ready st_free xnt_out kv_out x2_free x_in0 x_in1 x_free var_ready std_ready xn_ready xt_ps
            hss_ready hstd_ready nh_ready proj_ps gram_ps mix_ready va_ready vb_ready half_summed summed o_idx o_winin
            o_kvidx o_gath o_sready o_pready o_vready o_sum att_done agg_out agg_ready left w_ffn w_ffns fx_in in_free
            agt_ps agt_sb res_ps var2 std2 x3_ready x3_ps x3_sb gate_ps gate_d gate_e both_ready rank_ps rows_ready
            x2_ready x2_out route_done scat_free tab_ready zero_out xs_in xs_free xs_ps xs_sb h_ps h_sb y_ps y_used
            y_ready y_out y_free experts_done b1_ps b1_sb ffn_const""".split()
        S = {n: sem(n) for n in names}
        idx_ready = [sem(f"idx_ready{k}") for k in range(UNROLL)]
        gathered = [sem(f"gathered{k}") for k in range(UNROLL)]
        s_ready = [sem(f"s_ready{k}") for k in range(UNROLL)]
        p_ready = [sem(f"p_ready{k}") for k in range(UNROLL)]
        scattered = [sem(f"scattered{g}") for g in range(NG)]
        cx_in = [sem(f"cx_in{b}") for b in range(CB)]
        cy_in = [sem(f"cy_in{b}") for b in range(CB)]
        out_in = [sem(f"out_in{b}") for b in range(CB)]

        def chain(eng, s, i=0, per=0, first=0):
            n = [0]

            def link(ins, carry=False):
                n[0] += 1
                ins.then_inc(s, 1)
                eng.wait_ge(s, i * per + first + n[0])
                if carry:
                    eng.sem_inc(S["dve_step"], 1)

            link.n = n
            return link

        src_rows = a["src"]
        dst_rows = a["dst"]
        block = root.enter_context(nc.Block())

        def gather(pool, dst_ap, table, idx_ap, bound, s):
            pool.indirect_dma_start(out=dst_ap, out_offset=None, in_=table,
                                    in_offset=bass.IndirectOffsetOnAxis(ap=idx_ap, axis=0),
                                    bounds_check=bound, oob_is_err=False).then_inc(s, 16)

        def scatter(pool, table, idx_ap, src_ap, bound, s):
            pool.indirect_dma_start(out=table, out_offset=bass.IndirectOffsetOnAxis(ap=idx_ap, axis=0),
                                    in_=src_ap, in_offset=None, bounds_check=bound, oob_is_err=False).then_inc(s, 16)

        def pool_wait(pool, s, value):
            pool.wait_ge(s, value)
            pool.sem_inc(S["pool_step"], 1)

        @block.sync
        def _(sp):
            sp.dma_start(sup_i[:, :], dst_rows.rearrange("(j q) c -> j q c", q=P)[:, 0, 0].partition_broadcast(P))\
                .then_inc(S["sup_in"], 16)
            sp.dma_start(firstd, dst_rows.rearrange("(j q) c -> j q c", q=P)[:, :, 0]).then_inc(S["first_out"], 16)
            for n, w in enumerate(("Wq", "Wk", "Wv", "Wa")):
                sp.dma_start(w_raw[:, n], a["L0_gnn_" + w].rearrange("(c p) n -> p c n", p=P)).then_inc(S["w_in"], 16)
            for n, b in enumerate(("bq", "bk", "bv")):
                sp.dma_start(b_col[:, n], a["L0_gnn_" + b].rearrange("(c p) -> p c", p=P)).then_inc(S["small_in"], 16)
            sp.dma_start(aba[:, :], a["L0_gnn_ba"].partition_broadcast(P)).then_inc(S["small_in"], 16)
            sp.wait_ge(S["pool_const"], 5)
            for n, r in enumerate(("rel_att", "rel_msg")):
                for h in range(H):
                    o = DK * (h % 4)
                    sp.dma_start(rel[o:o + DK, n, h // 4, o:o + DK], a["L0_gnn_" + r][h]).then_inc(S["small_in"], 16)
            for h in range(H):
                o = DK * (h % 4)
                sp.dma_start(pri[o:o + DK, h // 4:h // 4 + 1],
                             a["L0_gnn_rel_pri"][h:h + 1].partition_broadcast(DK)).then_inc(S["small_in"], 16)
            sp.dma_start(alpha, a["L0_gnn_skip"].partition_broadcast(P)).then_inc(S["small_in"], 16)
            for t, nme in ((kln_wc, "kln_weight"), (kln_bc, "kln_bias")):
                sp.dma_start(t[:, :], a["L0_mix_" + nme].rearrange("(c p) -> p c", p=P)).then_inc(S["small_in"], 16)
            for t, nme in ((vln_wb, "vln_weight"), (vln_bb, "vln_bias")):
                sp.dma_start(t[:, :], a["L0_mix_" + nme].partition_broadcast(P)).then_inc(S["small_in"], 16)
            def load_x(i):
                for b in range(2):
                    sp.dma_start(xt[:, b, :], a["x"][bass.ds((2 * i + b) * P, P), :]).then_inc(S[f"x_in{b}"], 16)

            def store_pair(i):
                for b in range(2):
                    sp.wait_ge(S["xnt_ready"], 2 * i + b + 1)
                    sp.dma_start(xntd[bass.ds(2 * i + b, 1)].rearrange("t p f -> p (t f)"),
                                 xnt[:, b].rearrange("p c f -> p (c f)")).then_inc(S["xnt_out"], 16)
                for b in range(2):
                    sp.wait_ge(S["kvst_ready"], 2 * i + b + 1)
                    sp.dma_start(kvd[bass.ds((2 * i + b) * P, P), :], kvst[:, b, :]).then_inc(S["kv_out"], 16)
                sp.wait_ge(S["xnt_out"], 32 * i + 32)
                sp.wait_ge(S["kv_out"], 32 * i + 32)
                sp.sem_inc(S["st_free"], 1)

            def move_pairs(lo, hi):
                with sp.Fori(lo, hi) as i:
                    sp.wait_ge(S["x_free"], i + 1)
                    load_x(i + 1)
                    store_pair(i)

            load_x(0)
            sp.sem_inc(S["st_free"], 1)
            move_pairs(0, AT_START)
            sp.wait_ge(S["start_ready"], 1)
            sp.dma_start(rpd.rearrange("(t p) o -> p (t o)", p=P), start_i[:, :]).then_inc(S["start_out"], 16)
            sp.wait_ge(S["start_out"], 16)
            sp.dma_start(end_i[:, :], rpd[1:NP + 1, :].rearrange("(t p) o -> p (t o)", p=P)).then_inc(S["end_in"], 16)
            move_pairs(AT_START, AT_RETURN)
            sp.wait_ge(S["sort_out"], 16 * NT)
            sp.dma_start(window[:, :, :], sortd.rearrange("(t p) w -> p t w", p=P)).then_inc(S["sort_in"], 16)
            move_pairs(AT_RETURN, NT // 2 - 1)
            store_pair(NT // 2 - 1)
            sp.wait_ge(S["sched_ready"], 1)
            sp.dma_start(schedd.rearrange("(c p) w -> p c w", p=P), sch_i[:, :, :]).then_inc(S["sched_out"], 16)
            sp.wait_ge(S["sched_out"], 16)
            sp.dma_start(sched[:, :], schedd.rearrange("(a f) w -> a (f w)", a=1)).then_inc(S["sched_in"], 16)
            sp.wait_ge(S["q_out"], 16 * NT)
            sp.dma_start(qtab[:, :, :], qd.rearrange("(t p) f -> p t f", p=P)).then_inc(S["q_in"], 16)
            for c in range(NT // TC):
                sp.wait_ge(S["att_done"], c + 1)
                sp.dma_start(aggd[c * TC * P:(c + 1) * TC * P, :].rearrange("(t p) f -> p t f", p=P),
                             qtab[:, c * TC:(c + 1) * TC, :]).then_inc(S["agg_out"], 16)
            sp.wait_ge(S["agg_out"], 16 * (NT // TC))
            sp.wait_ge(S["left"], 3)
            sp.sem_inc(S["agg_ready"], 1)
            sp.dma_start(wg[:, :, :], a["L0_ffn_Wg"].rearrange("(c p) n -> p c n", p=P)).then_inc(S["w_ffns"], 16)
            sp.dma_start(b1r[:, :], a["L0_ffn_b1"].rearrange("e (c p) -> (e c) p", p=P)).then_inc(S["w_ffns"], 16)
            sp.dma_start(bgb[:, :], a["L0_ffn_bg"].partition_broadcast(P)).then_inc(S["w_ffns"], 16)
            sp.dma_start(b2b[:, :, :], a["L0_ffn_b2"].partition_broadcast(P)).then_inc(S["w_ffns"], 16)

            def load(i):
                sp.dma_start(fxnt[:, :, :, :], xntd[bass.ds(NB * i, NB)].rearrange("t p (c f) -> p t c f", c=HALVES))\
                    .then_inc(S["fx_in"], 16)
                sp.dma_start(fx[:, :, :], a["x"][bass.ds(NB * P * i, NB * P), :].rearrange("(t p) f -> p t f", p=P))\
                    .then_inc(S["fx_in"], 16)

            def store(i):
                sp.wait_ge(S["x2_ready"], NG * i + NG)
                sp.dma_start(x2d[bass.ds(NB * P * i, NB * P), :].rearrange("(t p) f -> p t f", p=P), x2[:, :, :])\
                    .then_inc(S["x2_out"], 16)
                sp.wait_ge(S["x2_out"], 16 * i + 16)
                sp.sem_inc(S["x2_free"], 1)

            sp.sem_inc(S["x2_free"], 1)
            load(0)
            sp.wait_ge(S["ffn_const"], 3)
            for t in range(LEAST, MOST):
                sp.dma_start(ysd[t * TOK:(t + 1) * TOK, :].rearrange("(b p) f -> p b f", p=P), zrows[:, :, :])\
                    .then_inc(S["zero_out"], 16)
            with sp.Fori(0, EARLY) as i:
                sp.wait_ge(S["in_free"], i + 1)
                load(i + 1)
                for w, name in ((w1, "L0_ffn_W1"), (w2, "L0_ffn_W2")):
                    sp.dma_start(w[:, bass.ds(i, 1)].rearrange("p e c n -> p (e c) n"),
                                 a[name][bass.ds(i, 1)].rearrange("e (c p) n -> p (e c) n", p=P)).then_inc(S["w_ffn"], 16)
                store(i)
            with sp.Fori(EARLY, NT // NB - 1) as i:
                sp.wait_ge(S["in_free"], i + 1)
                load(i + 1)
                store(i)
            store(NT // NB - 1)
            sp.wait_ge(S["tab_ready"], 1)
            for e in range(0, NE, 2):
                row = sp.value_load(ti[0:1, 2, e:e + 1], min_val=0, max_val=NE * CAP)
                sp.dma_start(xsd[bass.ds(row, TOK), :].rearrange("(b p) f -> p b f", p=P), zrows[:, :, :])\
                    .then_inc(S["zero_out"], 16)
            sp.wait_ge(S["zero_out"], 16 * (NE + MOST - LEAST))
            sp.wait_ge(S["route_done"], 3)

            def tile_row(f):
                return sp.value_load(trow[0:1, bass.ds(f, 1)], min_val=0, max_val=NE * CAP - TOK)

            def load_rows(f):
                sp.wait_ge(S["xs_free"], f + 1)
                sp.dma_start(xs[:, :, :], xsd[bass.ds(tile_row(f), TOK), :].rearrange("(b p) f -> p b f", p=P))\
                    .then_inc(S["xs_in"], 16)

            tiles = sp.value_load(ti[0:1, 3, 0:1], min_val=NE, max_val=MOST)
            sp.sem_inc(S["y_free"], 1)
            load_rows(0)
            load_rows(1)
            with sp.Fori(0, tiles) as f:
                sp.wait_ge(S["y_ready"], f + 1)
                sp.dma_start(ysd[bass.ds(f * TOK, TOK), :].rearrange("(b p) f -> p b f", p=P), yst[:, :, :])\
                    .then_inc(S["y_out"], 16)
                load_rows(f + 2)
                sp.wait_ge(S["y_out"], 16 * f + 16)
                sp.sem_inc(S["y_free"], 1)
            sp.sem_inc(S["experts_done"], 1)
            with sp.Fori(0, NT // CB) as i:
                for b in range(CB):
                    sp.wait_ge(S["c_free"], CB * i + b + 1)
                    sp.dma_start(cx[b][:, :], x2d[bass.ds((CB * i + b) * P, P), :]).then_inc(cx_in[b], 16)
            for b in range(CB):
                sp.wait_ge(out_in[b], 16 * (NT // CB))

        @block.gpsimd
        def _(pool):
            g = nc.gpsimd
            g.memset(ident[:, :], 0.0).then_inc(S["pool_const"], 1)
            g.memset(ones[:, :], 1.0).then_inc(S["pool_const"], 1)
            g.memset(rel[:, :, :, :], 0.0).then_inc(S["pool_const"], 1)
            g.iota(node_i[:, :], [[P, NT]], base=0, channel_multiplier=1).then_inc(S["pool_const"], 1)
            g.iota(slot_i[:, :], [[1, FAST]], base=0, channel_multiplier=0).then_inc(S["pool_const"], 1)
            g.iota(fpos_i[:, :], [[P, SCHED // P]], base=0, channel_multiplier=1).then_inc(S["pool_const"], 1)
            g.iota(k3_i[:, :], [[UNROLL, SCHED]], base=0, channel_multiplier=0).then_inc(S["pool_const"], 1)
            g.memset(upto[:, :], 1.0).then_inc(S["pool_const"], 1)
            g.memset(head_mask[:, :], 1.0).then_inc(S["pool_const"], 1)
            g.memset(start_i[:, NT:NT + 1], E).then_inc(S["pool_const"], 1)
            g.memset(below[:, :], 1.0).then_inc(S["pool_const"], 1)
            pool.wait_ge(S["pool_const"], 11)
            g.affine_select(out=ident[:, :], in_=ident[:, :], compare_op=ALU.not_equal, fill=1.0, base=0,
                            pattern=[[-1, P]], channel_multiplier=1).then_inc(S["pool_const"], 1)
            g.affine_select(out=upto[:, :], in_=upto[:, :], compare_op=ALU.is_ge, fill=0.0, base=0,
                            pattern=[[1, NT]], channel_multiplier=-1).then_inc(S["pool_const"], 1)
            g.affine_select(out=below[:, :], in_=below[:, :], compare_op=ALU.is_ge, fill=0.0, base=-1,
                            pattern=[[1, P]], channel_multiplier=-1).then_inc(S["pool_const"], 1)
            hm = head_mask[:, :].rearrange("p (h d) -> p h d", h=4)
            g.affine_select(out=hm, in_=hm, compare_op=ALU.is_ge, fill=0.0, base=0,
                            pattern=[[-DK, 4], [0, DK]], channel_multiplier=1).then_inc(S["pool_const"], 1)
            pool.wait_ge(S["pool_const"], 15)
            g.affine_select(out=hm, in_=hm, compare_op=ALU.is_ge, fill=0.0, base=DK - 1,
                            pattern=[[DK, 4], [0, DK]], channel_multiplier=-1).then_inc(S["pool_const"], 1)
            pool.wait_ge(S["first_out"], 16)
            pool.wait_ge(S["sup_ready"], 1)
            for t in range(NT):
                gather(pool, rows[:, t, :], firstd, sup_bi[:, t:t + 1], BLOCKS - 1, S["sup_rows_in"])
            pool.wait_ge(S["block_ready"], 1)
            for t in range(NT):
                gather(pool, rows[:, t, :], dst_rows, block_i[:, t:t + 1], EROWS - 1, S["rows_in"])
            pool.wait_ge(S["start_ready"], 1)
            for t in range(NT):
                gather(pool, window[:, t, 0:FAST], src_rows, start_i[:, t:t + 1], E, S["window_in"])
            pool.wait_ge(S["place_ready"], 1)
            pool.wait_ge(S["window_in"], 16 * NT)
            for t in range(NT):
                scatter(pool, sortd, place_i[:, t:t + 1], window[:, t, :], NP - 1, S["sort_out"])
            for t in range(NT):
                pool.wait_ge(S["q_ready"], t + 1)
                scatter(pool, qd, place_i[:, t:t + 1], qtab[:, t, :], NP - 1, S["q_out"])
            pool.wait_ge(S["mix_ready"], 1)
            for k in range(UNROLL // 2):
                g.memset(kv[k][:, :, :], 0.0).then_inc(S["pool_ready"], 1)
            for s in range(SLOTS):
                g.memset(iota8[:, s:s + 1], float(s)).then_inc(S["pool_ready"], 1)
            pool.wait_ge(S["pool_ready"], UNROLL // 2 + SLOTS)
            pool.wait_ge(S["kv_zeroed"], UNROLL - UNROLL // 2)
            passes = pool.value_load(counts[0:1, 0:1], min_val=1, max_val=PASSES)
            with pool.Fori(0, passes) as i:
                for k in range(UNROLL):
                    pool_wait(pool, idx_ready[k], i + 1)
                    pool_wait(pool, S["vb_ready"], UNROLL * i + k + 1)
                    for s in range(SLOTS):
                        gather(pool, kv[k][:, s, :], kvd, idx[k][:, s:s + 1], N - 1, gathered[k])
            flag = pool.value_load(counts[0:1, 1:2], min_val=0, max_val=1)
            with pool.If(flag > 0):
                with pool.Fori(0, NT) as t:
                    n = pool.value_load(over_n[0:1, bass.ds(t, 1)], min_val=1, max_val=E // SLOTS + 1)
                    n0 = pool.value_load(over_n[0:1, bass.ds(t + NT, 1)], min_val=0, max_val=E // SLOTS + NT)
                    with pool.Fori(0, n) as i:
                        pool_wait(pool, S["o_idx"], n0 + i + 1)
                        gather(pool, o_win[:, :], src_rows, o_posi[:, 0:1], E, S["o_winin"])
                        pool_wait(pool, S["o_kvidx"], n0 + i + 1)
                        for s in range(SLOTS):
                            gather(pool, kv[0][:, s, :], kvd, idx[0][:, s:s + 1], N - 1, S["o_gath"])
            pool.sem_inc(S["left"], 1)
            pool.wait_ge(S["agg_ready"], 1)
            g.iota(iota_i[:, :], [[1, NE]], base=0, channel_multiplier=0).then_inc(S["ffn_const"], 1)
            g.iota(fpos_ei[:, :], [[1, TABLE]], base=0, channel_multiplier=0).then_inc(S["ffn_const"], 1)
            g.memset(zrows[:, :, :], 0.0).then_inc(S["ffn_const"], 1)
            pool.sem_inc(S["scat_free"], NG)
            def fetch_agg():
                for b in range(NB):
                    gather(pool, fagg[:, b, :], aggd, aidx[:, b:b + 1], NP - 1, S["agg_in"])

            pool.wait_ge(S["aidx_ready"], 1)
            fetch_agg()
            with pool.Fori(0, NT // NB) as i:
                pool_wait(pool, S["aidx_ready"], i + 2)
                fetch_agg()
                pool_wait(pool, S["rows_ready"], i + 1)
                for g, (lo, hi) in enumerate(BANKS):
                    for b in range(lo, hi):
                        for j in range(2):
                            scatter(pool, xsd, rowi[:, j, b:b + 1], x3[:, b, :], NE * CAP - 1, scattered[g])
                for g, (lo, hi) in enumerate(BANKS):
                    pool_wait(pool, scattered[g], 32 * (hi - lo) * (i + 1))
                    pool.sem_inc(S["scat_free"], 1)
            pool.wait_ge(S["agg_in"], 16 * NB * (NT // NB + 1))
            pool.sem_inc(S["route_done"], 1)
            pool.wait_ge(S["experts_done"], 1)
            with pool.Fori(0, NT // CB) as i:
                for b in range(CB):
                    pool_wait(pool, S["cidx_ready"], CB * i + b + 1)
                    for j in range(2):
                        gather(pool, cy[b][:, j, :], ysd, cidx[b][:, j:j + 1], MOST * TOK - 1, cy_in[b])

        @block.tensor
        def _(pe):
            mm = nc.tensor.matmul
            pe.wait_ge(S["w_in"], 64)
            pe.wait_ge(S["small_in"], 16 * 33)
            pe.wait_ge(S["dve_pre"], 1)
            for half in range(HALVES):
                cin = slice(half * P, (half + 1) * P)
                for hc in range(HALVES):
                    for n in range(3):
                        r = qdiag[:, hc] if n == 0 else rel[:, n - 1, hc]
                        ins = mm(ps_w[:, n, half * D + hc * P:half * D + (hc + 1) * P], w_raw[:, n, hc, cin], r,
                                 start=True, stop=True)
            ins.then_inc(S["pe_pre"], 1)
            for half in range(HALVES):
                cin = slice(half * P, (half + 1) * P)
                for hc in range(HALVES):
                    ins = mm(ps_small[:, half * D + hc * P:half * D + (hc + 1) * P], w_raw[:, 3, hc, cin], adiag[:, :],
                             start=True, stop=True)
            ins.then_inc(S["pe_pre"], 1)
            pe.wait_ge(S["dve_pre"], 2)
            for n in range(3):
                for hc in range(HALVES):
                    r = qdiag[:, hc] if n == 0 else rel[:, n - 1, hc]
                    ins = mm(ps_w[:, n, hc * P:(hc + 1) * P], bcast(b_col[:, n, hc:hc + 1], [P, P]), r,
                             start=True, stop=True)
            ins.then_inc(S["pe_pre"], 1)
            pe.wait_ge(S["fold_done"], 1)
            mm(ps_g[:, :], zeros[:, 0:P], zeros[:, :], start=True, stop=False, skip_group_check=True).then_inc(S["gram_ps"], 1)

            def project(lo, hi):
                with pe.Fori(lo, hi) as i:
                    for b in range(2):
                        pe.wait_ge(S["xn_ready"], 2 * i + b + 1)
                        for c in range(HALVES):
                            ins = nc.tensor.transpose(ps_t[:, b, c * P:(c + 1) * P], xn[:, b, c * P:(c + 1) * P], ident[:, :])
                        ins.then_inc(S["xt_ps"], 1)
                    for b in range(2):
                        pe.wait_ge(S["xnt_ready"], 2 * i + b + 1)
                        for c in range(HALVES):
                            mm(ps_q[:, b, 0:D], xnt[:, b, c, :], wq[:, c, :], start=(c == 0), stop=(c == HALVES - 1))
                        for c in range(HALVES):
                            ins = mm(ps_kv[:, b, :], xnt[:, b, c, :], wkv[:, c, :], start=(c == 0), stop=(c == HALVES - 1))
                        ins.then_inc(S["proj_ps"], 1)
                    for b in range(2):
                        pe.wait_ge(S["nh_ready"], 2 * i + b + 1)
                        for c in range(HALVES):
                            cs = slice(c * P, (c + 1) * P)
                            mm(ps_g[:, cs], nh[:, b, cs], nh[:, b, cs], start=False, stop=False, skip_group_check=True)
                        mm(ps_g[:, D:2 * D], ones[:, :], nh[:, b, :], start=False, stop=False,
                           skip_group_check=True).then_inc(S["gram_ps"], 1)

            project(0, AT_SORT)
            pe.wait_ge(S["kind_ready"], 1)
            mm(ps_small[:, 0:KINDS * NT], below[:, :], kind[:, :], start=True, stop=True).then_inc(S["kind_ps"], 1)
            pe.wait_ge(S["kind_used"], 1)
            mm(ps_small[:, 0:KINDS * NT], ones[:, :], kind[:, :], start=True, stop=True).then_inc(S["kind_ps"], 1)
            project(AT_SORT, NT // 2)
            pe.wait_ge(S["dve_pre"], 3)
            nc.tensor.transpose(ps_small[0:NT, 0:P], deg_f[:, :], ident[:, :]).then_inc(S["pe_pre"], 1)
            pe.wait_ge(S["dve_pre"], 4)
            mm(ps_small[:, 128:128 + NT], bcast(tng[:, 0:1], [NT, P]), upto[:, :], start=True, stop=True)
            mm(ps_small[:, 192:192 + NT], bcast(tng[:, 0:1], [NT, P]), ident[0:NT, 0:NT], start=True, stop=True)
            mm(ps_small[:, 256:256 + NT], bcast(tng[:, 1:2], [NT, P]), upto[:, :], start=True, stop=True)
            mm(ps_small[:, 320:320 + NT], bcast(tng[:, 1:2], [NT, P]), ident[0:NT, 0:NT], start=True, stop=True)
            mm(ps_small[:, 384:385], bcast(tng[:, 3:4], [NT, P]), ones[0:NT, 0:1], start=True, stop=True)\
                .then_inc(S["pe_pre"], 1)

            pe.wait_ge(S["tables_ready"], 1)
            for k in range(UNROLL):
                ins = mm(ps_sum[k][:, 0:SW], ones[:, :], acc[:, 0, :], start=True, stop=True)
            ins.then_inc(S["summed"], 1)

            def add_slots(k, slots):
                if slots[0] == 0:
                    mm(ps_sum[k][:, D:SW], ident[:, :], zsum[k][:, :], start=True, stop=True)
                for s in slots:
                    ins = mm(ps_sum[k][:, 0:D], ident[:, :], wv[:, s * D:(s + 1) * D], start=(s == 0), stop=(s == SLOTS - 1))
                return ins

            def add_group(k, n):
                pe.wait_ge(S["va_ready"], n + 1)
                add_slots(k, range(SLOTS // 2)).then_inc(S["half_summed"], 1)
                pe.wait_ge(S["vb_ready"], n + UNROLL)
                add_slots(k, range(SLOTS // 2, SLOTS)).then_inc(S["summed"], 1)

            pe.sem_inc(S["half_summed"], 1)
            passes = pe.value_load(counts[0:1, 0:1], min_val=1, max_val=PASSES)
            with pe.Fori(0, passes) as i:
                for k in range(UNROLL):
                    add_group((k - 1) % UNROLL, UNROLL * i + k)
            add_group(UNROLL - 1, UNROLL * passes)
            flag = pe.value_load(counts[0:1, 1:2], min_val=0, max_val=1)
            with pe.If(flag > 0):
                with pe.Fori(0, NT) as t:
                    n = pe.value_load(over_n[0:1, bass.ds(t, 1)], min_val=1, max_val=E // SLOTS + 1)
                    n0 = pe.value_load(over_n[0:1, bass.ds(t + NT, 1)], min_val=0, max_val=E // SLOTS + NT)
                    with pe.Fori(0, n) as i:
                        pe.wait_ge(S["o_vready"], n0 + i + 1)
                        add_slots(0, range(SLOTS)).then_inc(S["o_sum"], 1)
            pe.sem_inc(S["left"], 1)
            pe.wait_ge(S["agg_ready"], 1)
            pe.wait_ge(S["w_ffns"], 64)
            nc.tensor.transpose(ps_b[:, 0:NE * HC], b1r[:, :], ident[0:NE * HC, 0:NE * HC]).then_inc(S["b1_ps"], 1)
            pe.wait_ge(S["b1_sb"], 1)
            def turn_agg(i):
                pe.wait_ge(S["agg_in"], 16 * NB * i + 16 * NB)
                for lo, hi in BANKS:
                    for b in range(lo, hi):
                        for c in range(HALVES):
                            ins = nc.tensor.transpose(ps_t2[:, b, c * P:(c + 1) * P], fagg[:, b, c * P:(c + 1) * P], ident[:, :])
                    ins.then_inc(S["agt_ps"], 1)

            turn_agg(0)
            with pe.Fori(0, NT // NB) as i:
                pe.wait_ge(S["fx_in"], 32 * i + 32)
                for g, (lo, hi) in enumerate(BANKS):
                    pe.wait_ge(S["agt_sb"], NG * i + g + 1)
                    for b in range(lo, hi):
                        for c in range(HALVES):
                            mm(ps_r[:, b, :], faggt[:, b, c, :], a_fold[:, c, :], start=(c == 0), stop=False, skip_group_check=True)
                        for c in range(HALVES):
                            ins = mm(ps_r[:, b, c * P:(c + 1) * P], fxnt[:, b, c, :], mix_w[:, c, :], start=False,
                                     stop=(c == 1), skip_group_check=True)
                    ins.then_inc(S["res_ps"], 1)
                for g, (lo, hi) in enumerate(BANKS):
                    pe.wait_ge(S["x3_ready"], NG * i + g + 1)
                    for b in range(lo, hi):
                        for c in range(HALVES):
                            ins = nc.tensor.transpose(ps_t2[:, b, c * P:(c + 1) * P], x3[:, b, c * P:(c + 1) * P], ident[:, :])
                    ins.then_inc(S["x3_ps"], 1)
                for g, (lo, hi) in enumerate(BANKS):
                    pe.wait_ge(S["x3_sb"], NG * i + g + 1)
                    for b in range(lo, hi):
                        for c in range(HALVES):
                            ins = mm(ps_b[:, b * NE:(b + 1) * NE], x3t[:, b, c, :], wg[:, c, :],
                                     start=(c == 0), stop=(c == HALVES - 1), skip_group_check=True)
                ins.then_inc(S["gate_ps"], 1)
                turn_agg(i + 1)
                pe.wait_ge(S["both_ready"], i + 1)
                sel = both[:, :, :].rearrange("p b e -> p (b e)")
                mm(ps_b[:, 64:64 + NB * NE], below[:, :], sel, start=True, stop=True)
                mm(ps_b[:, 128:128 + NB * NE], ones[:, :], sel, start=True, stop=True).then_inc(S["rank_ps"], 1)
            pe.sem_inc(S["route_done"], 1)
            pe.wait_ge(S["tab_ready"], 1)
            pe.wait_ge(S["w_ffn"], 32 * EARLY)
            pe.sem_inc(S["xs_free"], 1)

            def turn(f):
                pe.wait_ge(S["xs_in"], 16 * f + 16)
                for b in range(2):
                    for c in range(HALVES):
                        ins = nc.tensor.transpose(ps_x[:, c, b * P:(b + 1) * P], xs[:, b, c * P:(c + 1) * P], ident[:, :])
                ins.then_inc(S["xs_ps"], 1)

            turn(0)
            for e in range(NE):
                if e == EARLY:
                    pe.wait_ge(S["w_late"], 32 * (NE - EARLY))
                n = pe.value_load(ti[0:1, 0, e:e + 1], min_val=1, max_val=CAP // TOK)
                n0 = pe.value_load(ti[0:1, 1, e:e + 1], min_val=0, max_val=TABLE - 1)
                with pe.Fori(0, n) as i:
                    f = n0 + i
                    pe.wait_ge(S["xs_sb"], f + 1)
                    for q in range(HC // 2):
                        pe.wait_ge(S["h_sb"], 4 * f + q + 1)
                        for j in range(2):
                            c0 = (2 * q + j) * P
                            for c in range(HALVES):
                                ins = mm(ps_h[:, q, j, :], w1[:, e, c, c0:c0 + P], xst[:, c, :],
                                         start=(c == 0), stop=(c == HALVES - 1), skip_group_check=True)
                        ins.then_inc(S["h_ps"], 1)
                    turn(f + 1)
                    for b in range(2):
                        pe.wait_ge(S["y_used"], 2 * f + b + 1)
                        for c in range(HC):
                            if b == 0 and c % 2 == 0:
                                pe.wait_ge(S["h_sb"], 4 * f + 5 + c // 2)
                            ins = mm(ps_y[:, b, 0:D], hid[:, c, b * P:(b + 1) * P], w2[:, e, c, :],
                                     start=(c == 0), stop=(c == HC - 1))
                        ins.then_inc(S["y_ps"], 1)

        @block.scalar
        def _(act):
            ac = nc.scalar.activation
            act.wait_ge(S["small_in"], 16 * 33)
            ac(alpha, alpha, ACT.Exp, scale=-1.0).then_inc(S["act_pre"], 1)
            act.wait_ge(S["fold_done"], 1)
            with act.Fori(0, NT // 2) as i:
                for b in range(2):
                    act.wait_ge(S["var_ready"], 2 * i + b + 1)
                    ac(rstd[:, b, :], mv[:, b, 1:2], ACT.Sqrt, bias=eps_ln).then_inc(S["std_ready"], 1)
                for b in range(2):
                    act.wait_ge(S["xt_ps"], 2 * i + b + 1)
                    act.wait_ge(S["st_free"], i + 1)
                    ac(xnt[:, b], ps_t[:, b, 0:D].rearrange("p (c f) -> p c f", c=HALVES), ACT.Copy).then_inc(S["xnt_ready"], 1)
                for b in range(2):
                    act.wait_ge(S["hss_ready"], 2 * i + b + 1)
                    ac(hss[:, b, :], hss[:, b, :], ACT.Sqrt, bias=zero_col, scale=1.0 / (DK - 1)).then_inc(S["hstd_ready"], 1)
            act.wait_ge(S["mix_ready"], 1)
            def exponentials(k, t, done):
                nc.scalar.copy(m_tab[:, bass.ds(t, 1), :].rearrange("p a h -> p (a h)"), nmax[k][:, :])
                for h in range(H):
                    col = ex[k][:, h::H]
                    ac(col, col, ACT.Exp, bias=nmax[k][:, h:h + 1], accum_out=zsum[k][:, h:h + 1])
                ac(corr[k][:, :], corr[k][:, :], ACT.Exp).then_inc(done, 1)

            def stage(k, entry):
                place = act.value_load(sched[0:1, bass.ds(entry, 1)], min_val=0, max_val=NT * GROUPS - 1)
                nc.scalar.copy(idx[k][:, :], idx_tab[:, bass.ds(place * SLOTS, SLOTS)]).then_inc(idx_ready[k], 1)

            def empty_slots(k):
                return ac(msk[k][:, :], idx[k][:, :], ACT.Relu, scale=MASK, bias=half_skip)

            for k in range(UNROLL):
                stage(k, k + 2)
            for k in range(UNROLL // 2, UNROLL):
                ac(kv[k][:, :, :], bcast(zero_col.unsqueeze(2), [P, SLOTS, 2 * D]), ACT.Copy).then_inc(S["kv_zeroed"], 1)
            act.wait_ge(idx_ready[UNROLL - 1], 1)
            for k in range(UNROLL):
                ins = empty_slots(k)
            ins.then_inc(S["msk_ready"], 1)
            passes = act.value_load(counts[0:1, 0:1], min_val=1, max_val=PASSES)
            act.sem_inc(p_ready[UNROLL - 1], 1)
            with act.Fori(0, passes) as i:
                for k in range(UNROLL):
                    act.wait_ge(gathered[k], 16 * SLOTS * i + 16 * SLOTS)
                    stage(k, UNROLL * i + UNROLL + 2 + k)
                    place = act.value_load(sched[0:1, bass.ds(UNROLL * i + 2 + k, 1)], min_val=0, max_val=NT * GROUPS - 1)
                    act.wait_ge(s_ready[k], i + 1)
                    exponentials(k, place // GROUPS, p_ready[k])
                    act.wait_ge(idx_ready[k], i + 2)
                    empty_slots(k)
            flag = act.value_load(counts[0:1, 1:2], min_val=0, max_val=1)
            with act.If(flag > 0):
                with act.Fori(0, NT) as t:
                    n = act.value_load(over_n[0:1, bass.ds(t, 1)], min_val=1, max_val=E // SLOTS + 1)
                    n0 = act.value_load(over_n[0:1, bass.ds(t + NT, 1)], min_val=0, max_val=E // SLOTS + NT)
                    with act.Fori(0, n) as i:
                        act.wait_ge(S["o_sready"], n0 + i + 1)
                        exponentials(0, t, S["o_pready"])
            act.sem_inc(S["left"], 1)
            act.wait_ge(S["agg_ready"], 1)
            def stage_places(i):
                nc.scalar.copy(aidx[:, :], place_i[:, bass.ds(NB * i, NB)]).then_inc(S["aidx_ready"], 1)

            def turned_agg(i):
                for g, (lo, hi) in enumerate(BANKS):
                    act.wait_ge(S["agt_ps"], NG * i + g + 1)
                    ac(faggt[:, lo:hi, :, :], ps_t2[:, lo:hi, :].rearrange("p b (c f) -> p b c f", c=HALVES), ACT.Copy)\
                        .then_inc(S["agt_sb"], 1)

            nc.scalar.copy(aidx[:, :], place_i[:, 0:NB]).then_inc(S["aidx_ready"], 1)
            act.wait_ge(S["b1_ps"], 1)
            ac(b1[:, :], ps_b[:, 0:NE * HC], ACT.Copy).then_inc(S["b1_sb"], 1)
            turned_agg(0)
            nc.scalar.copy(aidx[:, :], place_i[:, NB:2 * NB]).then_inc(S["aidx_ready"], 1)
            with act.Fori(0, NT // NB) as i:
                act.wait_ge(S["var2"], i + 1)
                ac(frs[:, :, :], fmv[:, :, 1:2], ACT.Sqrt, bias=eps_ln).then_inc(S["std2"], 1)
                for g, (lo, hi) in enumerate(BANKS):
                    act.wait_ge(S["x3_ps"], NG * i + g + 1)
                    ac(x3t[:, lo:hi, :, :], ps_t2[:, lo:hi, :].rearrange("p b (c f) -> p b c f", c=HALVES), ACT.Copy)\
                        .then_inc(S["x3_sb"], 1)
                act.wait_ge(S["gate_d"], i + 1)
                ac(gw[:, :, 1:2], gw[:, :, 0:1], ACT.Exp).then_inc(S["gate_e"], 1)
                turned_agg(i + 1)
                stage_places(i + 2)
            act.wait_ge(S["tab_ready"], 1)
            for e in range(1, NE, 2):
                row = act.value_load(ti[0:1, 2, e:e + 1], min_val=0, max_val=NE * CAP)
                act.dma_start(xsd[bass.ds(row, TOK), :].rearrange("(b p) f -> p b f", p=P), zrows[:, :, :])\
                    .then_inc(S["zero_out"], 16)
            act.wait_ge(S["route_done"], 3)
            act.sem_inc(S["h_sb"], 4)

            def turned(f):
                act.wait_ge(S["xs_ps"], f + 1)
                ac(xst[:, :, :], ps_x[:, :, :], ACT.Copy).then_inc(S["xs_sb"], 1)

            turned(0)
            act.sem_inc(S["xs_free"], 1)
            for e in range(NE):
                if e + EARLY < NE:
                    for w, name in ((w1, "L0_ffn_W1"), (w2, "L0_ffn_W2")):
                        act.dma_start(w[:, e + EARLY], a[name][e + EARLY].rearrange("(c p) n -> p c n", p=P)).then_inc(S["w_late"], 16)
                n = act.value_load(ti[0:1, 0, e:e + 1], min_val=1, max_val=CAP // TOK)
                n0 = act.value_load(ti[0:1, 1, e:e + 1], min_val=0, max_val=TABLE - 1)
                with act.Fori(0, n) as i:
                    f = n0 + i
                    for q in range(HC // 2):
                        act.wait_ge(S["h_ps"], 4 * f + q + 1)
                        for j in range(2):
                            c = 2 * q + j
                            ins = ac(hid[:, c, :], ps_h[:, q, j, :], ACT.Gelu, bias=b1[:, e * HC + c:e * HC + c + 1])
                        ins.then_inc(S["h_sb"], 1)
                    turned(f + 1)
                    act.sem_inc(S["xs_free"], 1)
            act.wait_ge(S["experts_done"], 1)
            act.sem_inc(S["c_free"], CB)
            with act.Fori(0, NT // CB) as i:
                for b in range(CB):
                    act.wait_ge(S["c_done"], CB * i + b + 1)
                    act.dma_start(out[bass.ds((CB * i + b) * P, P), :], cx[b][:, :]).then_inc(out_in[b], 16)
                for b in range(CB):
                    act.wait_ge(out_in[b], 16 * i + 16)
                    act.sem_inc(S["c_free"], 1)

        @block.vector
        def _(dve):
            v = nc.vector
            tt, ts, stt, red = v.tensor_tensor, v.tensor_scalar, v.scalar_tensor_tensor, v.tensor_reduce
            link = chain(dve, S["dve_prj"])
            dve.wait_ge(S["pool_const"], 16)
            link(v.memset(small[:, 2:4], 0.0))
            link(v.memset(eps_ln, LN_EPS))
            link(v.memset(half_skip, -MASK * SKIP / 2))
            v.memset(zeros[:, :], 0.0)
            dve.wait_ge(S["sup_in"], 16)
            v.tensor_copy(node_f[:, :], node_i[:, :])
            link(v.tensor_copy(sup_f[:, :], sup_i[:, :]))
            link(tt(is_sup[:, :, :], bcast(sup_f[:, :].unsqueeze(1), [P, NT, BLOCKS]),
                    bcast(node_f[:, :].unsqueeze(2), [P, NT, BLOCKS]), ALU.is_lt))
            link(red(sup_b[:, :], is_sup[:, :, :], X, ALU.add))
            link(ts(sup_b[:, :], sup_b[:, :], -1.0, 0.0, ALU.add, ALU.max))
            v.tensor_copy(sup_bi[:, :], sup_b[:, :]).then_inc(S["sup_ready"], 1)
            dve.wait_ge(S["small_in"], 16 * 33)
            dve.wait_ge(S["act_pre"], 1)
            link(ts(alpha, alpha, 1.0, None, ALU.add))
            link(v.reciprocal(alpha, alpha))
            link(ts(two_minus_alpha, alpha, -1.0, 2.0, ALU.mult, ALU.add))
            link(ts(aba[:, :], aba[:, :], alpha, None, ALU.mult))
            link(ts(pri[:, :], pri[:, :], float(DK) ** -0.5, None, ALU.mult))
            for hc in range(HALVES):
                ts(qdiag[:, hc, :], ident[:, :], pri[:, hc:hc + 1], None, ALU.mult)
            ts(adiag[:, :], ident[:, :], alpha, None, ALU.mult).then_inc(S["dve_pre"], 1)
            dve.wait_ge(S["pe_pre"], 2)
            v.tensor_copy(wq[:, :, :], ps_w[:, 0, :].rearrange("p (c n) -> p c n", c=HALVES))
            v.tensor_copy(wkv[:, :, 0:D], ps_w[:, 1, :].rearrange("p (c n) -> p c n", c=HALVES))
            for c in range(HALVES):
                v.tensor_copy(wkv[:, c, D:2 * D].rearrange("p (d h) -> p h d", h=H),
                              ps_w[:, 2, c * D:(c + 1) * D].rearrange("p (h d) -> p h d", h=H))
            v.tensor_copy(a_fold[:, :, :], ps_small[:, :].rearrange("p (c n) -> p c n", c=HALVES)).then_inc(S["dve_pre"], 1)
            dve.wait_ge(S["pe_pre"], 3)
            v.tensor_copy(bias[:, 2 * D:3 * D].rearrange("p (d h) -> p h d", h=H), ps_w[:, 2, 0:D].rearrange("p (h d) -> p h d", h=H))
            link(v.tensor_copy(bias[:, 0:2 * D].rearrange("p (a n) -> p a n", a=2), ps_w[:, 0:2, 0:D]))
            dve.sem_inc(S["fold_done"], 1)

            pairs = range(2)

            def project(lo, hi):
                with dve.Fori(lo, hi) as i:
                    pl = chain(dve, S["dve_pjl"], i, PJ)
                    for b in pairs:
                        dve.wait_ge(S[f"x_in{b}"], 16 * i + 16)
                        ins = v.bn_stats(st6[:, b, :], xt[:, b, :])
                    pl(ins, carry=True)
                    for b in pairs:
                        v.bn_aggr(mv[:, b, :], st6[:, b, :]).then_inc(S["var_ready"], 1)
                    for b in pairs:
                        dve.wait_ge(S["std_ready"], 2 * i + b + 1)
                        pl(v.reciprocal(rstd[:, b, :], rstd[:, b, :]))
                        dve.wait_ge(S["var_ready"], 2 * i + b + 1)
                        ts(xn[:, b, :], xt[:, b, :], mv[:, b, 0:1], rstd[:, b, :], ALU.subtract, ALU.mult)\
                            .then_inc(S["xn_ready"], 1)
                    dve.wait_ge(S["xn_ready"], 2 * i + 2)
                    dve.sem_inc(S["x_free"], 1)
                    xn4 = xn[:, :, :].rearrange("p b (h d) -> p b h d", h=H)
                    for b in pairs:
                        ins = red(hsum[:, b, :], xn4[:, b], X, ALU.add)
                    pl(ins)
                    pl(ts(hsum[:, :, :], hsum[:, :, :], 1.0 / DK, None, ALU.mult))
                    for b in pairs:
                        ins = tt(xc[:, b, :].rearrange("p (h d) -> p h d", h=H), xn4[:, b],
                                 bcast(hsum[:, b, :].unsqueeze(2), [P, H, DK]), ALU.subtract)
                    pl(ins)
                    pl(tt(sq[:, :, :], xc[:, :, :], xc[:, :, :], ALU.mult))
                    for b in pairs:
                        red(hss[:, b, :], sq[:, b, :].rearrange("p (h d) -> p h d", h=H), X, ALU.add)\
                            .then_inc(S["hss_ready"], 1)
                    dve.wait_ge(S["hstd_ready"], 2 * i + 2)
                    pl(ts(hss[:, :, :], hss[:, :, :], LN_EPS, None, ALU.add))
                    pl(v.reciprocal(hr[:, :, :], hss[:, :, :]))
                    dve.wait_ge(S["gram_ps"], 2 * i + 1)
                    for b in pairs:
                        tt(nh[:, b, :].rearrange("p (h d) -> p h d", h=H), xc[:, b, :].rearrange("p (h d) -> p h d", h=H),
                           bcast(hr[:, b, :].unsqueeze(2), [P, H, DK]), ALU.mult).then_inc(S["nh_ready"], 1)
                    for b in pairs:
                        dve.wait_ge(S["proj_ps"], 2 * i + b + 1)
                        tt(qtab[:, bass.ds(2 * i + b, 1), :].rearrange("p a f -> p (a f)"), ps_q[:, b, 0:D], bias[:, 0:D], ALU.add)\
                            .then_inc(S["q_ready"], 1)
                        dve.wait_ge(S["st_free"], i + 1)
                        tt(kvst[:, b, :], ps_kv[:, b, :], bias[:, D:3 * D], ALU.add).then_inc(S["kvst_ready"], 1)
                    assert pl.n[0] == PJ, pl.n[0]

            def count_below(counted):
                link(tt(rows[:, :, :], rows[:, :, :], bcast(node_f[:, :].unsqueeze(2), [P, NT, P]), ALU.is_lt))
                link(red(counted[:, :], rows[:, :, :], X, ALU.add))

            project(0, AT_BLOCK)
            dve.wait_ge(S["sup_rows_in"], 16 * NT)
            count_below(coarse)
            link(stt(block_f[:, :], sup_b[:, :], float(P), coarse[:, :], ALU.mult, ALU.add))
            link(ts(block_f[:, :], block_f[:, :], -1.0, 0.0, ALU.add, ALU.max))
            v.tensor_copy(block_i[:, :], block_f[:, :]).then_inc(S["block_ready"], 1)
            project(AT_BLOCK, AT_START)
            dve.wait_ge(S["rows_in"], 16 * NT)
            count_below(fine)
            link(stt(start_n[:, :], block_f[:, :], float(P), fine[:, :], ALU.mult, ALU.add))
            v.tensor_copy(start_i[:, 0:NT], start_n[:, :]).then_inc(S["start_ready"], 1)
            v.tensor_copy(window[:, :, FAST:FAST + 1], start_n[:, :].unsqueeze(2))
            v.memset(place_i[:, NT:NT + 2 * NB], 0)
            v.memset(junk[:, 0:KINDS * NT], 1.0)
            project(AT_START, AT_SORT)
            dve.wait_ge(S["end_in"], 16)
            link(v.tensor_copy(end_f[:, :], end_i[:, :]))
            link(tt(deg_n[:, :], end_f[:, :], start_n[:, :], ALU.subtract))
            v.tensor_copy(window[:, :, FAST + 1:PW], deg_n[:, :].unsqueeze(2))
            link(ts(ngr_i[:, 0, :], deg_n[:, :], float(SLOTS - 1), None, ALU.add))
            link(ts(ngr_i[:, 1, :], ngr_i[:, 0, :], 3, None, ALU.logical_shift_right))
            link(v.tensor_copy(ngr[:, :], ngr_i[:, 1, :]))
            link(ts(ngr[:, :], ngr[:, :], float(KINDS - 1), None, ALU.min))
            for j in range(KINDS):
                ins = ts(kind[:, j * NT:(j + 1) * NT], ngr[:, :], float(KINDS - 1 - j), None, ALU.is_equal)
            ins.then_inc(S["kind_ready"], 1)
            dve.wait_ge(S["kind_ps"], 1)
            v.tensor_copy(rank[:, :], ps_small[:, 0:KINDS * NT]).then_inc(S["kind_used"], 1)
            dve.wait_ge(S["kind_ps"], 2)
            link(v.tensor_copy(counts_t[:, :], ps_small[:, 0:KINDS * NT]))
            link(v.tensor_tensor_scan(before[:, :], junk[:, 0:KINDS * NT], counts_t[:, :], 0.0, ALU.mult, ALU.add))
            link(tt(before[:, :], before[:, :], counts_t[:, :], ALU.subtract))
            link(tt(before[:, :], before[:, :], rank[:, :], ALU.add))
            link(tt(before[:, :], before[:, :], kind[:, :], ALU.mult))
            link(red(place_f[:, :], before[:, :].rearrange("p (j t) -> p t j", j=KINDS), X, ALU.add))
            v.tensor_copy(place_i[:, 0:NT], place_f[:, :]).then_inc(S["place_ready"], 1)
            project(AT_SORT, NT // 2)
            dve.wait_ge(S["sort_in"], 16)
            v.tensor_copy(start_f[:, :].unsqueeze(2), window[:, :, FAST:FAST + 1])
            link(v.tensor_copy(deg_f[:, :].unsqueeze(2), window[:, :, FAST + 1:PW]))
            ts(valid[:, :], deg_f[:, :], 0.5, None, ALU.is_gt).then_inc(S["dve_pre"], 1)
            dve.wait_ge(S["pe_pre"], 4)
            link(red(tmax[:, :], ps_small[0:NT, 0:P], X, ALU.max))
            link(ts(tint[:, 0:1], tmax[:, :], float(SLOTS - 1), None, ALU.add))
            link(ts(tint[:, 1:2], tint[:, 0:1], 3, None, ALU.logical_shift_right))
            link(v.tensor_copy(tng[:, 2:3], tint[:, 1:2]))
            link(ts(tng[:, 0:1], tng[:, 2:3], 1.0, float(GROUPS), ALU.max, ALU.min))
            link(ts(tng[:, 3:4], tng[:, 2:3], -float(GROUPS), 0.0, ALU.add, ALU.max))
            ts(tng[:, 1:2], tng[:, 3:4], 1.0, None, ALU.max).then_inc(S["dve_pre"], 1)
            dve.wait_ge(S["pe_pre"], 5)
            v.tensor_copy(gend[:, :], ps_small[:, 128:128 + NT])
            v.tensor_copy(grow[:, :], ps_small[:, 192:192 + NT])
            v.tensor_copy(orow[:, 0:NT], ps_small[:, 256:256 + NT])
            link(v.tensor_copy(orow[:, NT:2 * NT], ps_small[:, 320:320 + NT]))
            v.tensor_copy(over_n[:, 0:NT], orow[0:1, NT:2 * NT])
            link(tt(over_n[:, NT:2 * NT], orow[0:1, 0:NT], orow[0:1, NT:2 * NT], ALU.subtract))
            link(ts(fpos[:, :], fpos_i[:, :], -2.0, None, ALU.add))
            for c in range(SCHED // P):
                link(ts(junk[:, 0:RT], gend[:, 0:RT], fpos[:, c:c + 1], 0.0, ALU.is_le, ALU.add,
                        accum_out=sch_f[:, c, 0:1]))
                link(stt(junk[:, 0:RT], gend[:, 0:RT], fpos[:, c:c + 1], grow[:, 0:RT], ALU.is_le, ALU.mult,
                         accum_out=sch_f[:, c, 1:2]))
                link(tt(sch_f[:, c, 2:3], fpos[:, c:c + 1], sch_f[:, c, 1:2], ALU.subtract))
            link(ts(sch_f[:, :, 2], sch_f[:, :, 2], float(GROUPS - 1), 0.0, ALU.min, ALU.max))
            link(stt(sch_f[:, :, 3], sch_f[:, :, 0], float(GROUPS), sch_f[:, :, 2], ALU.mult, ALU.add))
            v.tensor_copy(sch_i[:, :, 0], sch_f[:, :, 3]).then_inc(S["sched_ready"], 1)
            link(v.tensor_copy(k3_f[:, :], k3_i[:, :]))
            link(ts(junk[0:1, 0:SCHED], k3_f[:, :], gend[0:1, RT - 1:RT], 0.0, ALU.is_lt, ALU.add, accum_out=cnt_f[:, 0:1]))
            link(ts(cnt_f[:, 1:2], ps_small[0:1, 384:385], 0.5, None, ALU.is_gt))
            link(v.tensor_copy(counts[:, 0:2], cnt_f[:, 0:2]))
            link(v.tensor_copy(slot_f[:, :], slot_i[:, :]))
            neg3 = neg_tab[:, :].rearrange("p (t s) -> p t s", t=NT)
            link(tt(neg3, bcast(slot_f[:, :].unsqueeze(1), [P, NT, FAST]), bcast(deg_f[:, :].unsqueeze(2), [P, NT, FAST]),
                    ALU.is_ge))
            link(stt(idx_tab[:, :].rearrange("p (t s) -> p t s", t=NT), neg3, SKIP, window[:, :, 0:FAST], ALU.mult, ALU.add))
            dve.wait_ge(S["gram_ps"], NT + 1)
            for c in range(HALVES):
                cs = slice(c * P, (c + 1) * P)
                sums = ps_g[:, D + c * P:D + (c + 1) * P]
                link(stt(mtmp[:, 0, :], sums, 1.0, ident[:, :], ALU.mult, ALU.mult, accum_out=s_col[:, c:c + 1]))
                link(tt(t_col[:, c:c + 1], kln_wc[:, c:c + 1], s_col[:, c:c + 1], ALU.mult))
                link(tt(mtmp[:, 0, :], ps_g[:, cs], vln_wb[:, cs], ALU.mult))
                link(ts(mtmp[:, 0, :], mtmp[:, 0, :], kln_wc[:, c:c + 1], None, ALU.mult))
                link(stt(mtmp[:, 1, :], vln_bb[:, cs], t_col[:, c:c + 1], mtmp[:, 0, :], ALU.mult, ALU.add))
                link(tt(mtmp[:, 2, :], sums, vln_wb[:, cs], ALU.mult))
                link(stt(mtmp[:, 3, :], vln_bb[:, cs], float(N), mtmp[:, 2, :], ALU.mult, ALU.add))
                link(stt(mtmp[:, 0, :], mtmp[:, 3, :], kln_bc[:, c:c + 1], mtmp[:, 1, :], ALU.mult, ALU.add))
                link(stt(mtmp[:, 1, :], mtmp[:, 0, :], 1.0 / N, head_mask[:, :], ALU.mult, ALU.mult))
                link(stt(mix_w[:, c, :], ident[:, :], two_minus_alpha, mtmp[:, 1, :], ALU.mult, ALU.add))
            dve.wait_ge(S["sched_in"], 16)
            dve.wait_ge(S["st_free"], NT // 2 + 1)
            dve.sem_inc(S["mix_ready"], 1)
            v.memset(m_tab[:, :, :], -NEG)
            v.memset(o_win[:, :], 0)
            link(v.memset(acc[:, :, :], 0.0))
            dve.sem_inc(S["tables_ready"], 1)

            def column(tab, t, w):
                return tab[:, bass.ds(t, 1), :].rearrange("p a f -> p (a f)")

            def e3(k):
                return ex[k][:, :].rearrange("p (s h) -> p s h", s=SLOTS)

            def times_q(k, t):
                return tt(prod[:, :].rearrange("p (s f) -> p s f", s=SLOTS), kv[k][:, :, 0:D],
                          bcast(qtab[:, bass.ds(t, 1), :], [P, SLOTS, D]), ALU.mult)

            def scores(k):
                return red(ex[k][:, :], prod[:, :].rearrange("p (a d) -> p a d", d=DK), X, ALU.add)

            def mask(k, neg):
                return tt(e3(k), e3(k), bcast(neg.unsqueeze(2), [P, SLOTS, H]), ALU.subtract)

            def minus_max(k):
                return red(hneg[k][:, :], e3(k).rearrange("p s h -> p h s"), X, ALU.max, negate=True)

            def running(k, t):
                return tt(nmax[k][:, :], hneg[k][:, :], column(m_tab, t, H), ALU.min)

            def rescale(k, t):
                return tt(corr[k][:, :], nmax[k][:, :], column(m_tab, t, H), ALU.subtract)

            def weigh(k, part):
                sl = slice(part * SLOTS // 2, (part + 1) * SLOTS // 2)
                return tt(wv[:, :].rearrange("p (s d h) -> p s d h", s=SLOTS, h=H)[:, sl],
                          kv[k][:, sl, D:2 * D].rearrange("p s (d h) -> p s d h", h=H),
                          bcast(e3(k)[:, sl].unsqueeze(2), [P, SLOTS // 2, DK, H]), ALU.mult)

            def acc_scale(k, t):
                o3 = column(acc, t, SW).rearrange("p (d h) -> p d h", h=H)
                return tt(o3, o3, bcast(corr[k][:, :].unsqueeze(1), [P, DK + 1, H]), ALU.mult)

            def acc_add(k, t):
                return tt(column(acc, t, SW), column(acc, t, SW), ps_sum[k][:, 0:SW], ALU.add)

            def group(entry):
                return dve.value_load(sched[0:1, bass.ds(entry, 1)], min_val=0, max_val=NT * GROUPS - 1)

            def tile_of(place):
                return place // GROUPS

            passes = dve.value_load(counts[0:1, 0:1], min_val=1, max_val=PASSES)
            for k in range(UNROLL):
                v.memset(corr[k][:, :], 0.0)
                v.memset(zsum[k][:, :], 0.0)
                link(v.memset(ex[k][:, :], 0.0))
            dve.wait_ge(S["msk_ready"], 1)
            dve.wait_ge(S["q_in"], 16)
            dve.wait_ge(S["pool_ready"], UNROLL // 2 + SLOTS)
            dve.wait_ge(S["kv_zeroed"], UNROLL - UNROLL // 2)
            dve.sem_inc(S["vb_ready"], UNROLL - 1)
            with dve.Fori(0, passes) as i:
                n = [0]

                def step(ins):
                    ins.then_inc(S["dve_attl"], 1)
                    n[0] += 1
                    return n[0]

                def after(m):
                    dve.wait_ge(S["dve_attl"], i * ATT + m)

                place = {0: group(UNROLL * i + 2)}
                for k in range(UNROLL):
                    k1, k2 = (k - 1) % UNROLL, (k - 2) % UNROLL
                    dve.wait_ge(gathered[k], 16 * SLOTS * i + 16 * SLOTS)
                    a_prod = step(times_q(k, tile_of(place[k])))
                    for j in ([-2, -1] if k == 0 else []) + ([k + 1] if k + 1 < UNROLL else []):
                        place[j] = group(UNROLL * i + 2 + j)
                    t, t2 = tile_of(place[k]), tile_of(place[k - 2])
                    after(a_prod)
                    a_red = step(scores(k))
                    dve.wait_ge(p_ready[k1], i + 1)
                    dve.wait_ge(S["half_summed"], UNROLL * i + k + 1)
                    weigh(k1, 0).then_inc(S["va_ready"], 1)
                    after(a_red)
                    a_mask = step(mask(k, msk[k][:, :]))
                    dve.wait_ge(S["summed"], UNROLL * i + k + 1)
                    weigh(k1, 1).then_inc(S["vb_ready"], 1)
                    a_acc = step(acc_scale(k2, t2))
                    after(a_acc)
                    step(acc_add(k2, t2))
                    after(a_mask)
                    a_max = step(minus_max(k))
                    after(a_max)
                    a_min = step(running(k, t))
                    after(a_min)
                    rescale(k, t).then_inc(s_ready[k], 1)
                assert n[0] == ATT, n[0]
            last = UNROLL * passes
            t2, t1 = tile_of(group(last)), tile_of(group(last + 1))
            k2, k1 = UNROLL - 2, UNROLL - 1
            dve.wait_ge(S["summed"], last + 1)
            link(acc_scale(k2, t2))
            link(acc_add(k2, t2))
            dve.wait_ge(p_ready[k1], passes + 1)
            weigh(k1, 0).then_inc(S["va_ready"], 1)
            weigh(k1, 1).then_inc(S["vb_ready"], 1)
            dve.wait_ge(S["summed"], last + 2)
            link(acc_scale(k1, t1))
            link(acc_add(k1, t1))
            flag = dve.value_load(counts[0:1, 1:2], min_val=0, max_val=1)
            with dve.If(flag > 0):
                with dve.Fori(0, NT) as t:
                    n = dve.value_load(over_n[0:1, bass.ds(t, 1)], min_val=1, max_val=E // SLOTS + 1)
                    n0 = dve.value_load(over_n[0:1, bass.ds(t + NT, 1)], min_val=0, max_val=E // SLOTS + NT)
                    lt = chain(dve, S["dve_spt"], t, 2)
                    lt(ts(o_pos[:, 0:1], start_f[:, bass.ds(t, 1)], float(FAST), None, ALU.add))
                    lt(ts(o_pos[:, 1:2], deg_f[:, bass.ds(t, 1)], -float(FAST), None, ALU.add), carry=True)
                    with dve.Fori(0, n) as i:
                        ln = chain(dve, S["dve_spl"], n0 + i, SPL)
                        v.tensor_copy(o_posi[:, :], o_pos[:, 0:1]).then_inc(S["o_idx"], 1)
                        ln(ts(o_msk[:, 0, :], iota8[:, :], o_pos[:, 1:2], None, ALU.is_ge))
                        ts(o_msk[:, 1, :], o_msk[:, 0, :], -NEG, None, ALU.mult)
                        dve.wait_ge(S["o_winin"], 16 * (n0 + i) + 16)
                        stt(idx[0][:, :], o_msk[:, 0, :], SKIP, o_win[:, :], ALU.mult, ALU.add).then_inc(S["o_kvidx"], 1)
                        ts(o_pos[:, 0:1], o_pos[:, 0:1], float(SLOTS), None, ALU.add)
                        ln(ts(o_pos[:, 1:2], o_pos[:, 1:2], -float(SLOTS), None, ALU.add))
                        dve.wait_ge(S["o_gath"], 16 * SLOTS * (n0 + i) + 16 * SLOTS)
                        ln(times_q(0, t))
                        ln(scores(0))
                        ln(mask(0, o_msk[:, 1, :]))
                        ln(minus_max(0))
                        ln(running(0, t))
                        rescale(0, t).then_inc(S["o_sready"], 1)
                        dve.wait_ge(S["o_pready"], n0 + i + 1)
                        weigh(0, 0)
                        weigh(0, 1).then_inc(S["o_vready"], 1)
                        dve.wait_ge(S["o_sum"], n0 + i + 1)
                        ln(acc_scale(0, t))
                        ln(acc_add(0, t))
                        assert ln.n[0] == SPL, ln.n[0]
            den = acc[:, :, D:SW]
            link(ts(den, den, 0.5, None, ALU.max))
            link(v.reciprocal(den, den))
            link(tt(den, den, bcast(valid[:, :].unsqueeze(2), [P, NT, H]), ALU.mult))
            for c in range(NT // TC):
                tc = slice(c * TC, (c + 1) * TC)
                tt(qtab[:, tc, :].rearrange("p t (h d) -> p t h d", h=H), acc[:, tc, 0:D].rearrange("p t (d h) -> p t h d", h=H),
                   bcast(den[:, tc].unsqueeze(3), [P, TC, H, DK]), ALU.mult).then_inc(S["att_done"], 1)
            dve.wait_ge(S["att_done"], NT // TC)

            dve.wait_ge(S["agg_ready"], 1)
            dve.wait_ge(S["ffn_const"], 3)
            dve.wait_ge(S["w_ffns"], 64)
            link(v.tensor_copy(iotae[:, :], iota_i[:, :]))
            link(ts(region[:, :], iotae[:, :], float(CAP), None, ALU.mult))
            link(v.memset(base[:, :], 0.0))
            tiles_b = range(NB)
            with dve.Fori(0, NT // NB) as i:
                ln = chain(dve, S["dve_rtl"], i, RTL)
                dve.wait_ge(S["fx_in"], 32 * i + 32)
                ln(tt(fx[:, :, :], fx[:, :, :], bcast(aba[:, :].unsqueeze(1), [P, NB, D]), ALU.add))

                def statistics(g):
                    dve.wait_ge(S["x2_ready"], NG * i + g + 1)
                    for b in range(*BANKS[g]):
                        ins = v.bn_stats(fst[:, b, :], x2[:, b, :])
                    return ins

                dve.wait_ge(S["x2_free"], i + 1)
                for g, (lo, hi) in enumerate(BANKS):
                    dve.wait_ge(S["res_ps"], NG * i + g + 1)
                    tt(x2[:, lo:hi, :], ps_r[:, lo:hi, :], fx[:, lo:hi, :], ALU.add).then_inc(S["x2_ready"], 1)
                    if g > 0:
                        statistics(g - 1)
                ins = statistics(NG - 1)
                dve.sem_inc(S["in_free"], 1)
                ln(ins, carry=True)
                for b in tiles_b:
                    ins = v.bn_aggr(fmv[:, b, :], fst[:, b, :])
                ins.then_inc(S["var2"], 1)
                dve.wait_ge(S["std2"], i + 1)
                ln(v.reciprocal(frs[:, :, :], frs[:, :, :]))
                for g, (lo, hi) in enumerate(BANKS):
                    dve.wait_ge(S["scat_free"], NG * i + g + 1)
                    for b in range(lo, hi):
                        ins = ts(x3[:, b, :], x2[:, b, :], fmv[:, b, 0:1], frs[:, b, :], ALU.subtract, ALU.mult)
                    ins.then_inc(S["x3_ready"], 1)
                dve.wait_ge(S["gate_ps"], i + 1)
                ln(tt(lg[:, :, :], ps_b[:, 0:NB * NE].rearrange("p (b e) -> p b e", b=NB),
                      bcast(bgb[:, :].unsqueeze(1), [P, NB, NE]), ALU.add), carry=True)
                for b in tiles_b:
                    ins = v.max(top[:, b, :], lg[:, b, :])
                ln(ins, carry=True)
                for b in tiles_b:
                    ins = v.max_index(topi[:, b, :], top[:, b, :], lg[:, b, :])
                tt(gw[:, :, 0:1], top[:, :, 1:2], top[:, :, 0:1], ALU.subtract).then_inc(S["gate_d"], 1)
                dve.wait_ge(S["gate_d"], i + 1)
                ln(v.tensor_copy(topf[:, :, :], topi[:, :, :]))
                for j in range(2):
                    ins = tt(pick[:, j], bcast(iotae[:, :].unsqueeze(1), [P, NB, NE]),
                             bcast(topf[:, :, j:j + 1], [P, NB, NE]), ALU.is_equal)
                ln(ins)
                tt(both[:, :, :], pick[:, 0], pick[:, 1], ALU.add).then_inc(S["both_ready"], 1)
                dve.wait_ge(S["gate_e"], i + 1)
                ln(ts(gw[:, :, 2:3], gw[:, :, 1:2], 1.0, None, ALU.add))
                ln(v.reciprocal(gw[:, :, 3:4], gw[:, :, 2:3]))
                v.tensor_copy(route_w[:, bass.ds(NB * i, NB), 0:1], gw[:, :, 3:4])
                tt(route_w[:, bass.ds(NB * i, NB), 1:2], gw[:, :, 1:2], gw[:, :, 3:4], ALU.mult)
                dve.wait_ge(S["rank_ps"], i + 1)
                for b in tiles_b:
                    tt(posn[:, b, :], ps_b[:, 64 + b * NE:64 + (b + 1) * NE], base[:, :], ALU.add)
                    ln(tt(base[:, :], ps_b[:, 128 + b * NE:128 + (b + 1) * NE], base[:, :], ALU.add))
                ln(tt(posn[:, :, :], posn[:, :, :], bcast(region[:, :].unsqueeze(1), [P, NB, NE]), ALU.add))
                for j in range(2):
                    ins = tt(prow[:, j], pick[:, j], posn[:, :, :], ALU.mult)
                ln(ins)
                ln(red(rowf[:, :, :], prow[:, :, :, :], X, ALU.add))
                v.tensor_copy(route_f[:, 0, bass.ds(2 * NB * i, 2 * NB)].rearrange("p (t j) -> p j t", j=2), rowf[:, :, :])
                v.tensor_copy(rowi[:, :, :], rowf[:, :, :]).then_inc(S["rows_ready"], 1)
                assert ln.n[0] == RTL, ln.n[0]
            cnt, tn, tend, gain, zr = (tf[:, j, :] for j in range(5))
            dve.wait_ge(S["rows_ready"], NT // NB)
            link(ts(cnt, base[:, :], float(TOK - 1), None, ALU.add))
            link(v.tensor_copy(ti[:, 0, :], cnt))
            link(ts(ti[:, 1, :], ti[:, 0, :], TOK.bit_length() - 1, None, ALU.logical_shift_right))
            link(v.tensor_copy(tn, ti[:, 1, :]))
            link(ts(tn, tn, 1.0, None, ALU.max))
            link(v.tensor_tensor_scan(tend, ones[:, 0:NE], tn, 0.0, ALU.mult, ALU.add))
            link(ts(gain, tn, -float(TOK), float(CAP), ALU.mult, ALU.add))
            link(tt(zr, region[:, :], base[:, :], ALU.add))
            v.tensor_copy(ti[:, 0, :], tn)
            v.tensor_copy(ti[:, 2, :], zr)
            v.tensor_copy(ti[:, 3, 0:1], tend[:, NE - 1:NE])
            link(tt(ti[:, 1, :], tend, tn, ALU.subtract))
            pos_f, row_f, add_f = (frow[0:1, j, :] for j in range(3))
            link(v.tensor_copy(pos_f, fpos_ei[:, :]))
            link(ts(row_f, pos_f, float(TOK), None, ALU.mult))
            for e in range(NE - 1):
                link(ts(add_f, pos_f, tend[0:1, e:e + 1], gain[0:1, e:e + 1], ALU.is_ge, ALU.mult))
                link(tt(row_f, row_f, add_f, ALU.add))
            link(ts(add_f, pos_f, tend[0:1, NE - 1:NE], None, ALU.is_lt))
            link(tt(row_f, row_f, add_f, ALU.mult))
            link(v.tensor_copy(trow[:, :], row_f))
            dve.sem_inc(S["route_done"], 1)
            dve.sem_inc(S["tab_ready"], 1)
            for e in range(NE - 1):
                link(ts(route_f[:, 1, :], route_f[:, 0, :], float(CAP * (e + 1)), gain[:, e:e + 1], ALU.is_ge, ALU.mult))
                if e == 0:
                    link(tt(rows_y[:, :], route_f[:, 0, :], route_f[:, 1, :], ALU.subtract))
                else:
                    link(tt(rows_y[:, :], rows_y[:, :], route_f[:, 1, :], ALU.subtract))
            link(v.tensor_copy(route_r[:, :, :].rearrange("p t j -> p (t j)"), rows_y[:, :]))

            dve.sem_inc(S["y_used"], 2)
            dve.wait_ge(S["route_done"], 3)
            for e in range(NE):
                n = dve.value_load(ti[0:1, 0, e:e + 1], min_val=1, max_val=CAP // TOK)
                n0 = dve.value_load(ti[0:1, 1, e:e + 1], min_val=0, max_val=TABLE - 1)
                with dve.Fori(0, n) as i:
                    f = n0 + i
                    dve.wait_ge(S["y_free"], f + 1)
                    for b in pairs:
                        dve.wait_ge(S["y_ps"], 2 * f + b + 1)
                        tt(yst[:, b, :], ps_y[:, b, 0:D], b2b[:, e, :], ALU.add).then_inc(S["y_used"], 1)
                    dve.wait_ge(S["y_used"], 2 * f + 4)
                    dve.sem_inc(S["y_ready"], 1)

            dve.wait_ge(S["experts_done"], 1)
            def combine(b, i):
                dve.wait_ge(cy_in[b], 32 * i + 32)
                dve.wait_ge(cx_in[b], 16 * i + 16)
                for j in range(2):
                    w = route_w[:, bass.ds(CB * i + b, 1), j:j + 1].rearrange("p a j -> p (a j)")
                    stt(cx[b][:, :], cy[b][:, j, :], w, cx[b][:, :], ALU.mult, ALU.add)\
                        .then_inc(S["dve_cbl" if j == 0 else "c_done"], 1)
                    if j == 0:
                        dve.wait_ge(S["dve_cbl"], CB * i + b + 1)
                dve.wait_ge(S["c_done"], CB * i + b + 1)

            def next_rows(b, t):
                v.tensor_copy(cidx[b][:, :], route_r[:, bass.ds(t, 1), :].rearrange("p a j -> p (a j)"))\
                    .then_inc(S["cidx_ready"], 1)

            for b in range(CB):
                next_rows(b, b)
            with dve.Fori(0, NT // CB - 1) as i:
                for b in range(CB):
                    combine(b, i)
                    next_rows(b, CB * i + CB + b)
            for b in range(CB):
                combine(b, NT // CB - 1)


def kernel(**inputs):
    import numpy as np
    import concourse.bacc as bacc
    from concourse.bass_utils import run_bass_kernel_spmd as run

    nc = bacc.Bacc("TRN2", target_bir_lowering=False, num_devices=1)
    arrays = {k: np.ascontiguousarray(v) for k, v in inputs.items()}
    arrays["x"] = np.concatenate([arrays["x"], np.zeros((NP - N, D), arrays["x"].dtype)])
    arrays["src"] = np.concatenate([arrays["src"], np.zeros(FAST, arrays["src"].dtype)]).reshape(-1, 1)
    arrays["dst"] = np.concatenate([arrays["dst"], np.full(EROWS * P - E, 1 << 20, arrays["dst"].dtype)]).reshape(EROWS, P)
    for k in arrays:
        if "ln_" in k:
            arrays[k] = arrays[k].reshape(-1)
    arrays["L0_gnn_skip"] = arrays["L0_gnn_skip"].reshape(1)
    dram = {k: nc.dram_tensor(k, v.shape, mybir.dt.from_np(v.dtype), kind="ExternalInput").ap() for k, v in arrays.items()}
    out = nc.dram_tensor("out", (NP, D), F32, kind="ExternalOutput").ap()
    build(nc, dram, out)
    r = run(nc, [arrays], core_ids=[0])
    return r.results[0]["out"][:N]
```
